# Optimizing a Trainium2 kernel written in Bass

```python
import numpy as np
import jax
import jax.numpy as jnp

def _softmax(x, axis=-1):
    return jax.nn.softmax(x, axis=axis)

def _gelu(x):
    return jax.nn.gelu(x, approximate=True)

def _silu(x):
    return jax.nn.silu(x)

def _sigmoid(x):
    return jax.nn.sigmoid(x)

def _layernorm(x, axis=-1, eps=1e-05):
    m = jnp.mean(x, axis=axis, keepdims=True)
    v = jnp.var(x, axis=axis, keepdims=True)
    return (x - m) / jnp.sqrt(v + eps)

def _scatter_add(tgt, idx, src, axis=0):
    return tgt.at[idx].add(src)

def _segment_sum(src, seg, n):
    return jax.ops.segment_sum(src, seg, n)
kernel_name = 'mk_gnn_resnorm_d2_gnn_r64_2502b6'

def setup_inputs(seed: int=0):
    np.random.seed(seed)
    _w = jnp.asarray

    def _rec_inputs():
        import jax
        import jax.numpy as jnp
        _gk = jax.random.key(seed)
        x = -0.000202 + 1 * jax.random.normal(jax.random.fold_in(_gk, 1), (100000, 64), jnp.float32)
        src = jax.random.randint(jax.random.fold_in(_gk, 2), (25000,), 0, 100000, jnp.int32)
        dst = jnp.minimum((100000 * jax.random.uniform(jax.random.fold_in(_gk, 3), (25000,)) ** 2.0).astype(jnp.int32), 99999)
        _o = jnp.argsort(dst, stable=True)
        src = src[_o]
        dst = dst[_o]
        edge_attr_32 = -5.3897e-05 + 0.999841 * jax.random.normal(jax.random.fold_in(_gk, 11), (25000, 32), jnp.float32)
        return (x, src, dst, edge_attr_32)
    x, src, dst, edge_attr_32 = _rec_inputs()

    def _L0_gnn_setup():
        import jax, jax.numpy as jnp
        import numpy as np
        N_NODES = 100000
        N_EDGES = 18750
        D_FEAT = 64
        key = jax.random.key(seed)
        k1, k2 = jax.random.split(key)
        x = jax.random.normal(k1, (N_NODES, D_FEAT), dtype=jnp.float32)
        edge_index = jax.random.randint(k2, (2, N_EDGES), 0, N_NODES, dtype=jnp.int32)
        return {'x': x, 'edge_index': edge_index}
    _L0_gnn_all = _L0_gnn_setup()
    _L0_gnn_in = {k: v for k, v in _L0_gnn_all.items() if k in ()}
    del _L0_gnn_all

    def _L1_gnn_setup():
        import jax, jax.numpy as jnp
        import numpy as np
        N_NODES = 50000
        N_EDGES = 12500
        D_NODE = 64
        D_EDGE = 32
        H_MSG = (2 * D_NODE + D_EDGE) // 2
        H_CMB = 3 * D_NODE // 2

        def _gelu(x):
            return jax.nn.gelu(x, approximate=False)
        key = jax.random.key(seed)
        ks = jax.random.split(key, 11)

        def lin(k, fan_in, fan_out):
            bound = 1.0 / np.sqrt(fan_in)
            k1, k2 = jax.random.split(k)
            W = jax.random.uniform(k1, (fan_in, fan_out), jnp.float32, -bound, bound)
            b = jax.random.uniform(k2, (fan_out,), jnp.float32, -bound, bound)
            return (W, b)
        node_vectors = jax.random.normal(ks[0], (N_NODES, D_NODE), jnp.float32)
        edge_vectors = jax.random.normal(ks[1], (N_EDGES, D_EDGE), jnp.float32)
        edge_indices = jax.random.randint(ks[2], (N_EDGES, 2), 0, N_NODES, jnp.int64 if jax.config.jax_enable_x64 else jnp.int32)
        W_m1, b_m1 = lin(ks[3], 2 * D_NODE + D_EDGE, H_MSG)
        W_m2, b_m2 = lin(ks[4], H_MSG, D_NODE)
        W_c1, b_c1 = lin(ks[5], 2 * D_NODE, H_CMB)
        W_c2, b_c2 = lin(ks[6], H_CMB, D_NODE)
        return {'node_vectors': node_vectors, 'edge_vectors': edge_vectors, 'edge_indices': edge_indices, 'W_m1': W_m1, 'b_m1': b_m1, 'W_m2': W_m2, 'b_m2': b_m2, 'W_c1': W_c1, 'b_c1': b_c1, 'W_c2': W_c2, 'b_c2': b_c2}
    _L1_gnn_all = _L1_gnn_setup()
    _L1_gnn_in = {k: v for k, v in _L1_gnn_all.items() if k in ('W_m1', 'b_m1', 'W_m2', 'b_m2', 'W_c1', 'b_c1', 'W_c2', 'b_c2')}
    del _L1_gnn_all
    return {'x': x, 'src': src, 'dst': dst, 'edge_attr_32': edge_attr_32, 'L1_gnn_W_m1': _L1_gnn_in['W_m1'], 'L1_gnn_b_m1': _L1_gnn_in['b_m1'], 'L1_gnn_W_m2': _L1_gnn_in['W_m2'], 'L1_gnn_b_m2': _L1_gnn_in['b_m2'], 'L1_gnn_W_c1': _L1_gnn_in['W_c1'], 'L1_gnn_b_c1': _L1_gnn_in['b_c1'], 'L1_gnn_W_c2': _L1_gnn_in['W_c2'], 'L1_gnn_b_c2': _L1_gnn_in['b_c2']}

def reference(x, src, dst, edge_attr_32, L1_gnn_W_m1, L1_gnn_b_m1, L1_gnn_W_m2, L1_gnn_b_m2, L1_gnn_W_c1, L1_gnn_b_c1, L1_gnn_W_c2, L1_gnn_b_c2):
    import jax
    import jax.numpy as jnp

    def _L0_gnn_ref(x, edge_index):
        import jax, jax.numpy as jnp
        import numpy as np
        N_NODES = 100000
        N_EDGES = 18750
        D_FEAT = 64
        N = x.shape[0]
        src = edge_index[0]
        dst = edge_index[1]
        deg = jnp.ones((N,), dtype=x.dtype).at[src].add(jnp.asarray(1.0, x.dtype))
        dinv = jax.lax.rsqrt(deg)
        w = dinv[src] * dinv[dst]
        y = jax.ops.segment_sum(w[:, None] * x[src], dst, num_segments=N)
        y = y + (dinv * dinv)[:, None] * x
        return y

    def _L1_gnn_ref(node_vectors, edge_vectors, edge_indices, W_m1, b_m1, W_m2, b_m2, W_c1, b_c1, W_c2, b_c2):
        import jax, jax.numpy as jnp
        import numpy as np
        N_NODES = 50000
        N_EDGES = 12500
        D_NODE = 64
        D_EDGE = 32
        H_MSG = (2 * D_NODE + D_EDGE) // 2
        H_CMB = 3 * D_NODE // 2

        def _gelu(x):
            return jax.nn.gelu(x, approximate=False)
        node_i = node_vectors[edge_indices[:, 0]]
        node_j = node_vectors[edge_indices[:, 1]]
        msg_input = jnp.concatenate([node_i, node_j, edge_vectors], axis=1)
        h = _gelu(msg_input @ W_m1 + b_m1)
        messages = _gelu(h @ W_m2 + b_m2)
        boxes = jax.ops.segment_sum(messages, edge_indices[:, 1], num_segments=node_vectors.shape[0])
        pairs = jnp.concatenate([node_vectors, boxes], axis=1)
        c = _gelu(pairs @ W_c1 + b_c1)
        combined = _gelu(c @ W_c2 + b_c2)
        return node_vectors + combined
    edge_index = jnp.stack([src, dst])
    edge_index_t = jnp.stack([src, dst], axis=1)
    x = _layernorm(x + _L0_gnn_ref(x, edge_index), axis=-1)
    x = _layernorm(x + _L1_gnn_ref(x, edge_attr_32, edge_index_t, L1_gnn_W_m1, L1_gnn_b_m1, L1_gnn_W_m2, L1_gnn_b_m2, L1_gnn_W_c1, L1_gnn_b_c1, L1_gnn_W_c2, L1_gnn_b_c2), axis=-1)
    return x

_drawn_inputs = setup_inputs


def setup_inputs(seed=0):
    import zlib

    import numpy as np

    out = dict(_drawn_inputs(seed))
    spreads = {}
    factors = {'edge_attr_32': 8.0,
     'L1_gnn_W_m1': 8.0,
     'L1_gnn_b_m1': 36.126,
     'L1_gnn_W_m2': 8.0,
     'L1_gnn_b_m2': 64.0,
     'L1_gnn_b_c1': 8.0,
     'L1_gnn_b_c2': 3.937}
    for name, (base, spread) in spreads.items():
        noise = np.random.default_rng([zlib.crc32(name.encode()), seed]).standard_normal(out[name].shape)
        drawn = base * np.exp(spread * noise) if base else spread * noise
        out[name] = jnp.asarray(drawn.astype(out[name].dtype))
    for name, factor in factors.items():
        out[name] = (out[name] * factor).astype(out[name].dtype)
    return out
```

```python
from contextlib import ExitStack

import concourse.bass as bass
from concourse import mybir
from concourse.alu_op_type import AluOpType as ALU

F32 = mybir.dt.float32
F16 = mybir.dt.float16
BF16 = mybir.dt.bfloat16
I32 = mybir.dt.int32
ACT = mybir.ActivationFunctionType
AX = mybir.AxisListType

P = 128
N, D = 100000, 64
E, DE = 25000, 32
HM, HC = 80, 96
EPS = 1e-5
J = 16
NCH = P * J
CH = -(-N // NCH)
LASTP = (N - (CH - 1) * NCH) // J
TILES = 196
TPC = 4
ECH = TILES // TPC
EP = TILES * P
ROWS = TILES // 2
RE = 2 * P
OFF = 1 << 17
TW = D + 1
SEG = 8
FREE = J * D
EF = TPC * D
EC = TPC * P
assert CH == ECH and LASTP * J == N - (CH - 1) * NCH


class Chunk:

    def __init__(self, unroll, turn, slot):
        self.unroll, self.turn, self.slot = unroll, turn, slot
        self.n = turn * unroll + slot

    def back(self, k):
        turns, slot = divmod(self.slot - k, self.unroll)
        return Chunk(self.unroll, self.turn + turns, slot)

    def real(self):
        return not isinstance(self.n, int) or 0 <= self.n < CH

    def after(self, k):
        return not isinstance(self.n, int) or self.n >= k


def run_chunks(eng, body, unroll, peel, skew):
    for n in range(peel):
        body(Chunk(unroll, n // unroll, n % unroll))
    last = (CH - 1) // unroll
    with eng.Fori(peel // unroll, last) as turn:
        for slot in range(unroll):
            body(Chunk(unroll, turn, slot))
    for n in range(last * unroll, CH + skew):
        body(Chunk(unroll, n // unroll, n % unroll))


def build(nc, x, src, dst, edge_attr, w_m1, b_m1, w_m2, b_m2, w_c1, b_c1, w_c2, b_c2, out):
    with ExitStack() as ctx:
        def sb(name, shape, dt=F32):
            return ctx.enter_context(nc.sbuf_tensor(name, shape, dt))

        def sem(name):
            return ctx.enter_context(nc.semaphore(name))

        table = nc.dram_tensor("table", (N, TW), F32).ap()
        agg = nc.dram_tensor("agg", (N, D), F32).ap()
        srcs = nc.dram_tensor("srcs", (EP, 1), I32).ap()
        dsts = nc.dram_tensor("dsts", (EP + 2, 1), I32).ap()
        attrs = nc.dram_tensor("attrs", (EP, DE), F32).ap()
        src_perm = nc.dram_tensor("src_perm", (EP, 1), I32).ap()
        dst_perm = nc.dram_tensor("dst_perm", (EP, 1), I32).ap()
        attr_perm = nc.dram_tensor("attr_perm", (EP, DE), F32).ap()

        big = sb("big", [P, ECH * (TPC * TW + EF)])
        xs_all = big[:, 0:ECH * TPC * TW]
        xd_all = big[:, ECH * TPC * TW:]
        keys = big[:, 0:EP]
        x_in = sb("x_in", [P, 4, FREE])
        x1 = sb("x1", [P, 2, FREE])
        xT = sb("xT", [P, FREE])
        cT = sb("cT", [P, 2 * FREE])
        comb = sb("comb", [P, FREE])
        zc = sb("zc", [P, 2, FREE])
        sq = sb("sq", [P, 2, FREE])
        trow = sb("trow", [P, 2, J * TW])
        outb = trow[:, :, :].rearrange("p a b -> p (a b)")[:, 0:2 * FREE].rearrange("p (a b) -> p a b", a=2)
        dinv = sb("dinv", [P, CH * J])
        mean1 = sb("mean1", [P, CH * J])
        scale1 = sb("scale1", [P, CH * J])

        gs = sb("gs", [P, 2, TPC, TW])
        gd = sb("gd", [P, 2, TPC, TW])
        w_x = sb("w_x", [P, TPC, D])
        mask_rhs = sb("mask_rhs", [P, TPC, P], BF16)
        mask = sb("mask", [P, EC])
        fsum = sb("fsum", [D, 2, EC])
        ag = sb("ag", [P, 2, EF])
        v_e = sb("v_e", [P, TPC, D])
        t_e = sb("t_e", [P, TPC, D])
        vc_e = sb("vc_e", [P, 2, TPC, D])
        sm = sb("sm", [P, 64])
        sums = sb("sums", [P, J + TPC])
        var = sb("var", [P, 2, J + TPC])
        rstd = sb("rstd", [P, 2, J + TPC])
        nw = sb("nw", [P, J + TPC])

        idx = sb("idx", [P, ECH, 16], I32)
        istage = sb("istage", [P, 16], I32)
        same_prev = sb("same_prev", [P, TILES])
        same_next = sb("same_next", [P, TILES])
        is_last = sb("is_last", [P, TILES])
        hp = sb("hp", [P, TILES])
        hcol = sb("hcol", [P, TILES])
        flag = sb("flag", [1, 1], I32)

        ident = sb("ident", [P, P])
        flip = sb("flip", [P, P])
        ident_b = sb("ident_b", [P, P], BF16)
        flip_b = sb("flip_b", [P, P], BF16)
        ones_b = sb("ones_b", [P, P], BF16)
        ones_f = sb("ones_f", [P, 1])
        iota_p = sb("iota_p", [P, P], F16)
        wx_d = sb("wx_d", [P, HC])
        wm1 = sb("wm1", [P, HM])
        wme = sb("wme", [DE, HM])
        wm2 = sb("wm2", [HM, D])
        wc1 = sb("wc1", [P, HC])
        wc2 = sb("wc2", [HC + 1, D])
        bm1 = sb("bm1", [HM, 1])
        bm2 = sb("bm2", [D, 1])
        bc1 = sb("bc1", [HC, 1])

        rows = x1[:, :, :].rearrange("p a b -> p (a b)").rearrange("p (n e) -> p n e", e=RE)[0:ROWS]
        rwin = xT[0:ROWS, 0:RE + 2].bitcast(I32)
        rsrc = xT[0:ROWS, 260:260 + RE].bitcast(I32)
        rtmp = xT[0:ROWS, 520:520 + RE].bitcast(I32)
        rtm2 = cT[0:ROWS, 0:RE].bitcast(I32)
        usum = sm[0:ROWS, 0:1]
        hist_b = outb[:, :, :].rearrange("p a b -> p (a b)").bitcast(BF16)
        hb = [hist_b[:, i * CH * J:(i + 1) * CH * J] for i in range(4)]
        ha = [hist_b[:, 3136 + i * P:3136 + (i + 1) * P] for i in range(4)]
        iota_c = cT[:, 1024:1024 + CH * J // 2].bitcast(F16)
        zeros = comb[:, 0:1000]
        seg_out = zc[:, :, :].rearrange("p a b -> p (a b)").bitcast(BF16)[:, 0:EP // SEG]
        dst_e = cT[:, 256:256 + TILES].bitcast(I32)
        dst_ef = cT[:, 456:456 + TILES]
        pos_f = cT[:, 656:656 + TILES]
        pos_i = cT[:, 1420:1420 + TILES].bitcast(I32)
        lower = sq[:, 0, 0:P]
        eq_t = sq[:, 0, P:2 * P]
        seg_n = sm[:, 8:8 + SEG + 1]
        sort_i = sm[:, 32:34].bitcast(I32)
        sort_s = sm[:, 34:35].bitcast(I32)
        sort_e = sq[:, 1, 0:DE]
        m_in = x_in[:, 0:1, :].rearrange("p a (s t f) -> p (a s) t f", s=2, t=TPC)
        xin = [x_in[:, 1, s * EC:(s + 1) * EC] for s in range(2)]
        eattr = x_in[:, 2, 0:2 * TPC * DE].rearrange("p (s t f) -> p s t f", s=2, t=TPC)
        eT = x_in[0:DE, 2, 512:1024]
        hT = x_in[0:HM, 3, 0:EC]
        mT = [x_in[0:D, 3, EC:2 * EC], xT[0:D, 0:EC]]
        c2T = cT[0:HC + 1, 0:EC]
        comb_e = [comb[:, s * EF:(s + 1) * EF].rearrange("p (t f) -> p t f", f=D) for s in range(2)]
        sq_e = outb[:, 0, 0:EF].rearrange("p (t f) -> p t f", f=D)
        zc_e = [outb[:, 1, s * EF:(s + 1) * EF].rearrange("p (t f) -> p t f", f=D) for s in range(2)]
        out_e = [outb[:, 1, (2 + s) * EF:(3 + s) * EF] for s in range(2)]
        ga = gd[:, :, :, :].rearrange("p s t f -> p s (t f)")[:, :, 0:EF]

        ps = ctx.enter_context(nc.psum_tensor("ps", [P, 8, 512], F32))
        ps_xT = ps[:, 0:2, :].rearrange("p a b -> p (a b)")
        ps_c = ps[0:HC, 2:4, :].rearrange("p a b -> p (a b)")
        ps_o = ps[:, 4:6, :].rearrange("p a b -> p (a b)")
        ps_w = ps[0:D, 6, :]
        ps_mask = ps[0:D, 7, :]
        ps_ag = ps[:, 7, 0:EF]
        hist = ps[:, 0:2, 0:CH * J // 2]
        ps_i = ps[:, 2:7, 0:4 * ROWS].rearrange("p a (n h q) -> p a n h q", n=2, h=2)
        ps_flip = ps[:, 7, 0:TILES]
        ps_u = ps[0:1, 7, 508:509]

        s_zeros = sem("s_zeros")
        s_guard = sem("s_guard")
        s_hfill = sem("s_hfill")
        s_ones = sem("s_ones")
        s_consts = sem("s_consts")
        s_lower = sem("s_lower")
        s_iota = sem("s_iota")
        s_pads = sem("s_pads")
        s_copy = sem("s_copy")
        s_weights = sem("s_weights")
        s_win = sem("s_win")
        s_hsrc = sem("s_hsrc")
        s_ucount = sem("s_ucount")
        s_flag = sem("s_flag")
        s_keys = sem("s_keys")
        s_rank = sem("s_rank")
        s_ranked = sem("s_ranked")
        s_stage = sem("s_stage")
        s_tile = sem("s_tile")
        s_perm = sem("s_perm")
        s_back = sem("s_back")
        s_settled = sem("s_settled")
        s_sorted = sem("s_sorted")
        s_rows = sem("s_rows")
        s_hidx = sem("s_hidx")
        s_ri = sem("s_ri")
        s_iT = sem("s_iT")
        s_idx = sem("s_idx")
        s_onehot = sem("s_onehot")
        s_hist = sem("s_hist")
        s_deg = sem("s_deg")
        s_dinv = sem("s_dinv")
        s_zero = sem("s_zero")
        s_x = [sem(f"s_load{i}") for i in range(4)]
        s_xst = sem("s_xst")
        s_xc = sem("s_xc")
        s_trow = sem("s_trow")
        s_tst = [sem(f"s_tst{i}") for i in range(2)]
        s_sq0 = sem("s_sq0")
        s_v0 = sem("s_v0")
        s_scale = sem("s_scale")
        s_root = sem("s_root")

        p_x = [sem(f"p_load{i}") for i in range(2)]
        p_x1 = sem("p_x1")
        p_xT = sem("p_xT")
        p_xTs = sem("p_xTs")
        p_c = sem("p_c")
        p_cg = sem("p_cg")
        p_o = sem("p_o")
        p_og = sem("p_og")
        p_z = sem("p_z")
        p_sq = sem("p_sq")
        p_sqs = sem("p_sqs")
        p_out = sem("p_out")
        p_st = [sem(f"p_st{i}") for i in range(2)]
        q_is = sem("q_is")
        q_il = sem("q_il")
        q_gs = [sem(f"q_gs{i}") for i in range(2)]
        q_gd = [sem(f"q_gd{i}") for i in range(2)]
        q_xs = sem("q_xs")
        q_w = sem("q_w")
        q_wT = sem("q_wT")
        q_mask = sem("q_mask")
        q_f = sem("q_f")
        q_fT = sem("q_fT")
        q_ag = sem("q_ag")
        q_v = sem("q_v")
        q_var = sem("q_var")
        q_pow = sem("q_pow")
        q_xd = sem("q_xd")
        q_sc = [sem(f"q_sc{i}") for i in range(2)]

        r_start = sem("r_start")
        r_is = sem("r_is")
        r_io = sem("r_io")
        r_ga = [sem(f"r_ga{i}") for i in range(2)]
        r_e = [sem(f"r_e{i}") for i in range(2)]
        r_a = sem("r_a")
        r_m = sem("r_m")
        r_md = sem("r_md")
        r_tm = sem("r_tm")
        r_xs = sem("r_xs")
        r_xd = sem("r_xd")
        r_h = sem("r_h")
        r_hg = sem("r_hg")
        r_mm = sem("r_mm")
        r_mg = sem("r_mg")
        r_box = sem("r_box")
        r_c = sem("r_c")
        r_cg = sem("r_cg")
        r_o = sem("r_o")
        r_og = sem("r_og")
        r_z = sem("r_z")
        r_var = sem("r_var")
        r_pow = sem("r_pow")
        r_out = sem("r_out")
        r_sc = [sem(f"r_sc{i}") for i in range(2)]
        block = ctx.enter_context(nc.Block())

        GUARD = slice(1, EP + 1)
        col3 = lambda a: a.rearrange("p (a b) -> p a b", b=D)
        wide = lambda a, n, f: a.unsqueeze(2).to_broadcast([a.shape[0], n, f])

        def x_chunk(c, t):
            if isinstance(c, int) and c == CH - 1:
                return t[c * NCH:N, :].rearrange("(p j) d -> p (j d)", j=J), LASTP
            return t[bass.ds(c * NCH, NCH), :].rearrange("(p j) d -> p (j d)", j=J), P

        def settled(eng):
            eng.sem_inc(s_settled, 1)

        @block.sync
        def _(sp):
            sp.wait_ge(s_zeros, 1)
            sp.dma_start(attrs[E:EP, :], zeros[0:EP - E, 0:DE]).then_inc(s_pads, 16)
            sp.dma_start(srcs[E:EP, :], zeros[0:EP - E, 0:1].bitcast(I32)).then_inc(s_pads, 16)
            sp.dma_start(srcs[0:E, :], src.rearrange("(n a) -> n a", a=1)).then_inc(s_copy, 16)
            sp.dma_start(dsts[1:E + 1, :], dst.rearrange("(n a) -> n a", a=1)).then_inc(s_copy, 16)
            sp.wait_ge(s_guard, 3)
            sp.dma_start(dsts[E + 1:EP + 1, :], sort_s[0:EP - E, :]).then_inc(s_pads, 16)
            sp.dma_start(dsts[0:1, :], sort_i[0:1, 0:1]).then_inc(s_pads, 16)
            sp.dma_start(dsts[EP + 1:EP + 2, :], sort_i[0:1, 1:2]).then_inc(s_pads, 16)
            sp.dma_start(attrs[0:E, :].rearrange("(a b) d -> a (b d)", a=200),
                         edge_attr.rearrange("(a b) d -> a (b d)", a=200)).then_inc(s_copy, 16)
            full = E // RE
            sp.wait_ge(s_hfill, 1)
            sp.dma_start(rsrc[0:full, :], src[0:full * RE].rearrange("(q e) -> q e", e=RE)).then_inc(s_hsrc, 16)
            sp.dma_start(rsrc[full:full + 1, 0:E - full * RE],
                         src[full * RE:E].rearrange("(q e) -> q e", q=1)).then_inc(s_hsrc, 16)
            sp.wait_ge(s_pads, 80)
            sp.wait_ge(s_copy, 48)
            window = bass.AP(dsts.tensor, 0, [[RE, ROWS], [1, RE + 2]])
            sp.dma_start(rwin, window).then_inc(s_win, 16)
            for dst_ap, src_ap in (
                    (wx_d[0:D, :], w_c1[0:D, :]), (wx_d[D:P, :], w_c1[0:D, :]), (wm1[:, :], w_m1[0:P, :]),
                    (wme[:, :], w_m1[P:P + DE, :]), (wm2[:, :], w_m2), (wc1[0:D, :], w_c1[D:P, :]),
                    (wc1[D:P, :], w_c1[0:D, :]), (wc2[0:HC, :], w_c2),
                    (wc2[HC:HC + 1, :], b_c2.rearrange("(a n) -> a n", a=1)),
                    (bm1[:, :], b_m1.rearrange("(n a) -> n a", a=1)),
                    (bm2[:, :], b_m2.rearrange("(n a) -> n a", a=1)),
                    (bc1[:, :], b_c1.rearrange("(n a) -> n a", a=1))):
                sp.dma_start(dst_ap, src_ap).then_inc(s_weights, 16)
            sp.dma_start(agg.rearrange("(p a) d -> p (a d)", p=32).rearrange("p (k f) -> p k f", f=1000),
                         zeros[0:32, :].unsqueeze(1).to_broadcast([32, N * D // 32 // 1000, 1000])).then_inc(s_zero, 16)
            sp.wait_ge(s_sorted, 1)
            sp.wait_ge(s_hidx, 1)
            sp.wait_ge(s_ucount, 1)
            sp.dma_start(rwin, window).then_inc(s_rows, 16)
            sp.dma_start(rsrc, srcs.rearrange("(q e) a -> q (e a)", e=RE)).then_inc(s_rows, 16)

            def load_x0(c):
                if not c.real():
                    return
                if c.after(4):
                    sp.wait_ge(s_xc, c.n - 3)
                    settled(sp)
                    sp.wait_ge(s_trow, 2 * (c.n - 3))
                    settled(sp)
                src_ap, parts = x_chunk(c.n, x)
                sp.dma_start(x_in[0:parts, c.slot, :], src_ap).then_inc(s_x[c.slot], 16)

            run_chunks(sp, load_x0, 4, 4, 0)

            sp.wait_ge(s_xc, CH)
            sp.wait_ge(s_trow, 2 * CH)

            def load_store(c):
                if c.real():
                    if c.after(2):
                        sp.wait_ge(p_x1, 2 * (c.n - 2) + 1)
                        settled(sp)
                    src_ap, parts = x_chunk(c.n, x)
                    sp.dma_start(x_in[0:parts, c.slot, :], src_ap).then_inc(p_x[c.slot], 16)
                o = c.back(3)
                if o.real():
                    sp.wait_ge(p_out, o.n + 1)
                    settled(sp)
                    dst_ap, parts = x_chunk(o.n, out)
                    sp.dma_start(dst_ap, outb[0:parts, o.slot, :]).then_inc(p_st[o.slot], 16)

            run_chunks(sp, load_store, 2, 4, 3)

            sp.wait_ge(p_st[0], 16 * (CH // 2 + 1))
            sp.wait_ge(p_st[1], 16 * (CH // 2))
            sp.wait_ge(r_start, 4)

            def load_e(c):
                if c.real():
                    if c.after(2):
                        sp.wait_ge(r_tm, c.n - 1)
                        settled(sp)
                    k = (CH - 1) - c.n
                    sp.dma_start(eattr[:, c.slot, :, :],
                                 attrs[bass.ds(k * EC, EC), :].rearrange("(t p) d -> p t d", p=P)
                                 ).then_inc(r_e[c.slot], 16)

            run_chunks(sp, load_e, 2, 2, 0)

        @block.scalar
        def _(act):
            act.wait_ge(s_deg, 1)
            act.activation(zc[:, 1, 0:CH * J], zc[:, 0, 0:CH * J], ACT.Sqrt).then_inc(s_root, 1)
            act.wait_ge(s_dinv, 1)

            def rows_chunk(c):
                if c.real():
                    act.wait_ge(s_x[c.slot], 16 * (c.turn + 1))
                    two = c.slot % 2
                    if c.after(2):
                        act.wait_ge(s_tst[two], 16 * (c.turn * 2 + c.slot // 2))
                    t3 = trow[:, two, :].rearrange("p (j f) -> p j f", f=TW)
                    act.activation(t3[:, :, 0:D], col3(x_in[:, c.slot, :]), ACT.Copy).then_inc(s_trow, 1)
                    act.activation(t3[:, :, D:TW], dinv[:, bass.ds(c.n * J, J)].unsqueeze(2), ACT.Copy
                                   ).then_inc(s_trow, 1)
                    act.wait_ge(s_trow, 2 * (c.n + 1))
                    dst_ap, parts = x_chunk(c.n, table)
                    act.dma_start(dst_ap, trow[0:parts, two, :]).then_inc(s_tst[two], 16)
                b = c.back(1)
                if b.real():
                    act.wait_ge(s_xc, b.n + 1)
                    if b.after(2):
                        act.wait_ge(s_v0, b.n - 1)
                    act.activation(sq[:, b.slot % 2, :], zc[:, b.slot % 2, :], ACT.Square).then_inc(s_sq0, 1)

            run_chunks(act, rows_chunk, 4, 4, 1)

            act.wait_ge(s_scale, 5)
            act.activation(sq[:, 0, 0:CH * J], zc[:, 1, 0:CH * J], ACT.Sqrt).then_inc(s_root, 1)

            act.wait_ge(s_weights, 16 * 12)
            act.wait_ge(s_zero, 16)

            def pass1(c):
                e = c.back(1)
                if e.real():
                    act.wait_ge(q_gs[e.slot], 64 * (e.turn + 1))
                    act.activation(xs_all[:, bass.ds(e.n * (TPC * TW), TPC * TW)],
                                   gs[:, e.slot, :, :].rearrange("p t f -> p (t f)"), ACT.Copy).then_inc(q_xs, 1)
                if c.real():
                    act.wait_ge(p_xT, c.n + 1)
                    act.activation(xT[:, :], ps_xT, ACT.Copy).then_inc(p_xTs, 1)
                if e.real():
                    act.wait_ge(q_wT, e.n + 1)
                    act.activation(mask[0:D, :], ps_mask, ACT.Copy).then_inc(q_mask, 1)
                    act.wait_ge(p_z, 4 * (e.n + 1))
                    act.activation(sq[:, 0, :], zc[:, e.slot, :], ACT.Square).then_inc(p_sq, 1)
                if c.real():
                    for half in range(2):
                        act.wait_ge(p_c, 2 * c.n + half + 1)
                        if half == 0 and c.after(1):
                            act.wait_ge(p_o, c.n)
                        act.activation(cT[0:HC, half * FREE:(half + 1) * FREE], ps_c, ACT.Gelu,
                                       bias=bc1[:, 0:1]).then_inc(p_cg, 1)
                    act.wait_ge(p_o, c.n + 1)
                    if c.after(1):
                        act.wait_ge(p_z, 4 * (c.n - 1) + 1)
                    act.activation(comb[:, :], ps_o, ACT.Gelu).then_inc(p_og, 1)

            run_chunks(act, pass1, 2, 2, 1)
            act.wait_ge(p_og, CH)
            act.sem_inc(r_start, 1)
            act.wait_ge(r_start, 4)

            def pass2(c):
                b, g = c.back(2), c.back(3)
                k = (CH - 1) - b.n
                if b.real():
                    if b.after(2):
                        act.wait_ge(r_tm, b.n - 1)
                    act.activation(m_in[:, b.slot, :, D:P],
                                   xd_all[:, bass.ds(k * EF, EF)].rearrange("p (t f) -> p t f", f=D),
                                   ACT.Copy).then_inc(r_md, 1)
                if g.real():
                    act.wait_ge(r_c, g.n + 1)
                    if g.after(1):
                        act.wait_ge(r_o, g.n)
                    act.activation(c2T[0:HC, :], ps[0:HC, 5, :], ACT.Gelu, bias=bc1[:, 0:1]).then_inc(r_cg, 1)
                if b.real():
                    act.wait_ge(r_tm, b.n + 1)
                    if b.after(2):
                        act.wait_ge(r_o, b.n - 1)
                    if b.after(1):
                        act.wait_ge(r_box, b.n)
                    act.activation(xin[b.slot][0:D, :], ps[0:D, 0, :], ACT.Copy).then_inc(r_xs, 1)
                    if b.after(1):
                        act.wait_ge(r_h, b.n)
                    act.activation(mask[:, :], ps[:, 1, :], ACT.Copy).then_inc(r_xs, 1)
                    act.activation(eT, ps[0:DE, 2, :], ACT.Copy).then_inc(r_xs, 1)
                if g.real():
                    act.wait_ge(r_o, g.n + 1)
                    if g.after(2):
                        act.wait_ge(r_z, 6 * (g.n - 1))
                    act.activation(comb_e[g.slot], ps[:, 6 + g.slot, 0:EF].rearrange("p (t f) -> p t f", f=D), ACT.Gelu
                                   ).then_inc(r_og, 1)
                if b.real():
                    act.wait_ge(r_h, b.n + 1)
                    act.activation(hT, ps[0:HM, 3, :], ACT.Gelu, bias=bm1[:, 0:1]).then_inc(r_hg, 1)
                    act.wait_ge(r_mm, b.n + 1)
                    if b.after(2):
                        act.wait_ge(r_box, b.n - 1)
                    act.activation(mT[b.slot], ps[0:D, 4, :], ACT.Gelu, bias=bm2[:, 0:1]).then_inc(r_mg, 1)

            run_chunks(act, pass2, 2, 6, 3)

        @block.tensor
        def _(pe):
            pe.wait_ge(s_ones, 3)
            pe.wait_ge(s_consts, 4)
            pe.wait_ge(s_ucount, 1)
            pe.matmul(ps_u, usum, ones_f[0:ROWS, :], start=True, stop=True).then_inc(s_iT, 1)
            pe.wait_ge(s_hidx, 2)
            for a in range(2):
                for h in range(2):
                    mm = pe.transpose(ps_i[:, 4, a, h, :], rows[:, 6 + a, h * P:(h + 1) * P],
                                      ident[0:ROWS, 0:ROWS])
            mm.then_inc(s_iT, 1)

            def hist_tile(turn, slot, first, last):
                pe.wait_ge(s_onehot, 2 * (4 * turn + slot + 1))
                for b in range(2):
                    half = CH * J // 2
                    mm = pe.matmul(hist[:, b, :], ha[slot], hb[slot][:, b * half:(b + 1) * half],
                                   start=first, stop=last)
                mm.then_inc(s_hist, 1)

            for slot in range(4):
                hist_tile(0, slot, slot == 0, False)
            with pe.Fori(1, TILES // 4 - 1) as turn:
                for slot in range(4):
                    hist_tile(turn, slot, False, False)
            for slot in range(4):
                hist_tile(TILES // 4 - 1, slot, False, slot == 3)

            pe.wait_ge(s_ri, 4)
            pe.wait_ge(s_idx, 2)
            for a in range(6):
                for h in range(2):
                    mm = pe.transpose(ps_i[:, a // 2, a % 2, h, :], rows[:, a, h * P:(h + 1) * P],
                                      ident[0:ROWS, 0:ROWS])
            mm.then_inc(s_iT, 1)
            pe.wait_ge(s_idx, 3)
            pe.matmul(ps_flip, flip[:, :], sq[:, 0, 0:TILES], start=True, stop=True).then_inc(s_iT, 1)

            pe.wait_ge(s_weights, 16 * 12)
            pe.wait_ge(s_idx, 13)

            def pass1(c):
                e = c.back(1)
                if c.real():
                    pe.wait_ge(p_x1, 2 * (c.n + 1))
                    if c.after(1):
                        pe.wait_ge(p_xTs, c.n)
                    for i in range(J // 2):
                        mm = pe.transpose(ps_xT[:, i * P:(i + 1) * P], x1[:, c.slot, i * P:(i + 1) * P], ident[:, :])
                    mm.then_inc(p_xT, 1)
                if e.real():
                    pe.wait_ge(q_w, 2 * (e.n + 1))
                    if e.after(1):
                        pe.wait_ge(q_ag, e.n)
                    settled(pe)
                    for t in range(TPC):
                        pe.transpose(ps_w[:, t * P:(t + 1) * P], w_x[:, t, :], ident[:, :])
                    pe.matmul(ps_mask, ones_b[:, 0:D], mask_rhs[:, :, :].rearrange("p t e -> p (t e)"),
                              start=True, stop=True).then_inc(q_wT, 1)
                if c.real():
                    pe.wait_ge(p_xTs, c.n + 1)
                    for half in range(2):
                        if half == 1 or c.after(1):
                            pe.wait_ge(p_cg, 2 * c.n + half)
                        for i in range(2):
                            mm = pe.matmul(ps_c[:, i * 512:(i + 1) * 512], wx_d[half * D:(half + 1) * D, :],
                                           xT[half * D:(half + 1) * D, i * 512:(i + 1) * 512],
                                           start=True, stop=True)
                        mm.then_inc(p_c, 1)
                if e.real():
                    pe.wait_ge(q_f, e.n + 1)
                    settled(pe)
                    for t in range(TPC):
                        mm = pe.transpose(ps_ag[:, t * D:(t + 1) * D], fsum[:, e.slot, t * P:(t + 1) * P],
                                          ident[0:D, 0:D])
                    mm.then_inc(q_fT, 1)
                if c.real():
                    pe.wait_ge(p_cg, 2 * (c.n + 1))
                    if c.after(1):
                        pe.wait_ge(p_og, c.n)
                    for i in range(J // 2):
                        for half in range(2):
                            j = 2 * i + half
                            mm = pe.matmul(ps_o[:, j * D:(j + 1) * D],
                                           cT[0:HC + 1, half * FREE + i * P:half * FREE + (i + 1) * P],
                                           wc2[:, :], start=True, stop=True)
                    mm.then_inc(p_o, 1)

            run_chunks(pe, pass1, 2, 2, 1)
            pe.wait_ge(p_og, CH)
            pe.sem_inc(r_start, 1)
            pe.wait_ge(r_start, 4)

            def pass2(c):
                b, g = c.back(2), c.back(3)
                if g.real():
                    pe.wait_ge(r_box, g.n + 1)
                    if g.after(1):
                        pe.wait_ge(r_cg, g.n)
                    pe.matmul(ps[0:HC, 5, :], wc1[:, :], xin[g.slot], start=True, stop=True).then_inc(r_c, 1)
                if b.real():
                    pe.wait_ge(r_m, 2 * (b.n + 1))
                    pe.wait_ge(r_md, b.n + 1)
                    pe.wait_ge(r_e[b.slot], 16 * (b.turn + 1))
                    if b.after(1):
                        pe.wait_ge(r_xs, 3 * b.n)
                        pe.wait_ge(r_xd, b.n)
                    for t in range(TPC):
                        u = TPC - 1 - t
                        pe.matmul(ps[:, 0, t * P:(t + 1) * P], m_in[:, b.slot, u, :], flip[:, :],
                                  start=True, stop=True)
                        pe.matmul(ps[0:DE, 2, t * P:(t + 1) * P], eattr[:, b.slot, u, :], flip[:, :],
                                  start=True, stop=True)
                    pe.matmul(ps[:, 1, :], ones_b[:, :], mask_rhs[:, :, :].rearrange("p t e -> p (t e)"),
                              start=True, stop=True).then_inc(r_tm, 1)
                if g.real():
                    pe.wait_ge(r_cg, g.n + 1)
                    if g.after(2):
                        pe.wait_ge(r_z, 6 * (g.n - 2) + 1)
                    for t in range(TPC):
                        pe.matmul(ps[:, 6 + g.slot, t * D:(t + 1) * D], c2T[:, t * P:(t + 1) * P], wc2[:, :],
                                  start=True, stop=True)
                        mm = pe.matmul(ps[:, 6 + g.slot, EF + t * D:EF + (t + 1) * D], xin[g.slot][D:P, t * P:(t + 1) * P],
                                       ident[D:P, D:P], start=True, stop=True)
                    mm.then_inc(r_o, 1)
                if b.real():
                    pe.wait_ge(r_xs, 3 * (b.n + 1))
                    pe.wait_ge(r_xd, b.n + 1)
                    if b.after(1):
                        pe.wait_ge(r_hg, b.n)
                    pe.matmul(ps[0:HM, 3, :], wm1[:, :], xin[b.slot], start=True, stop=False)
                    pe.matmul(ps[0:HM, 3, :], wme[:, :], eT, start=False, stop=True).then_inc(r_h, 1)
                    pe.wait_ge(r_hg, b.n + 1)
                    if b.after(1):
                        pe.wait_ge(r_mg, b.n)
                    pe.matmul(ps[0:D, 4, :], wm2[:, :], hT, start=True, stop=True).then_inc(r_mm, 1)

            run_chunks(pe, pass2, 2, 6, 3)

        @block.vector
        def _(dve):
            def then(ins, sem_, value):
                ins.then_inc(sem_, 1)
                dve.wait_ge(sem_, value)

            def newton(y, v, tmp, sem_, base):
                then(dve.scalar_tensor_tensor(tmp, y, -0.5, y, ALU.mult, ALU.mult), sem_, base + 1)
                then(dve.tensor_tensor(tmp, tmp, v, ALU.mult), sem_, base + 2)
                then(dve.scalar_tensor_tensor(y, tmp, 1.5, y, ALU.add, ALU.mult), sem_, base + 3)

            def rsqrt(y, v, tmp, sem_, base):
                yi = y.bitcast(I32)
                then(dve.tensor_scalar(yi, v.bitcast(I32), 1, None, ALU.arith_shift_right), sem_, base + 1)
                then(dve.tensor_scalar(yi, yi, -1.0, float(0x5F3759DF), ALU.mult, ALU.add), sem_, base + 2)
                for step in range(3):
                    newton(y, v, tmp, sem_, base + 2 + 3 * step)

            dve.memset(comb[:, :], 0.0).then_inc(s_zeros, 1)
            dve.memset(sort_i[0:1, 0:1], -1).then_inc(s_guard, 1)
            dve.memset(sort_i[0:1, 1:2], 2 * OFF).then_inc(s_guard, 1)
            dve.memset(sort_s, OFF).then_inc(s_guard, 1)
            dve.memset(rsrc, OFF).then_inc(s_hfill, 1)
            dve.memset(ones_b[:, :], 1.0).then_inc(s_ones, 1)
            dve.memset(ones_f[:, :], 1.0).then_inc(s_ones, 1)
            dve.memset(sums[:, :], 1.0).then_inc(s_ones, 1)

            dve.wait_ge(s_win, 16)
            dve.tensor_tensor(rows[:, 0, :], rwin[:, 1:RE + 1], rwin[:, 2:RE + 2], ALU.is_gt).then_inc(s_rank, 1)
            dve.wait_ge(s_rank, 1)
            dve.tensor_reduce(usum, rows[:, 0, :], AX.X, ALU.add).then_inc(s_ucount, 1)
            dve.wait_ge(s_hsrc, 32)
            dve.tensor_scalar(rtmp, rsrc, 4, P - 1, ALU.arith_shift_right, ALU.bitwise_and).then_inc(s_rank, 1)
            dve.tensor_scalar(rtm2, rsrc, J - 1, None, ALU.bitwise_and).then_inc(s_rank, 1)
            dve.wait_ge(s_rank, 3)
            dve.tensor_scalar(rsrc, rsrc, 11, 4, ALU.arith_shift_right, ALU.logical_shift_left).then_inc(s_rank, 1)
            dve.wait_ge(s_rank, 4)
            dve.tensor_tensor(rows[:, 7, :], rsrc, rtm2, ALU.add).then_inc(s_hidx, 1)
            dve.tensor_copy(rows[:, 6, :], rtmp).then_inc(s_hidx, 1)
            dve.wait_ge(s_iT, 1)
            dve.tensor_scalar(flag[:, :], ps_u, 1.0, None, ALU.min).then_inc(s_flag, 1)
            dve.wait_ge(s_flag, 1)
            unsorted = dve.value_load(flag[0:1, 0:1], min_val=0, max_val=1)
            with dve.If(unsorted == 1):
                dve.wait_ge(s_lower, 1)
                dve.wait_ge(s_keys, 48)
                then(dve.tensor_copy(dst_ef, dst_e), s_ranked, 1)
                with dve.Fori(0, TILES) as t:
                    mine = dst_ef[:, bass.ds(t, 1)]
                    for g in range(SEG):
                        n = EP // SEG
                        dve.tensor_scalar(seg_out, keys[:, g * n:(g + 1) * n], mine, 0.0, ALU.is_lt, ALU.add,
                                          accum_out=seg_n[:, g:g + 1]).then_inc(s_rank, 1)
                        dve.wait_ge(s_rank, 4 + t * (SEG + 5) + g + 1)
                    tile_keys = keys[:, bass.ds(t * P, P)]
                    base = 4 + t * (SEG + 5) + SEG
                    then(dve.tensor_scalar(eq_t, tile_keys, mine, None, ALU.is_equal), s_rank, base + 1)
                    then(dve.tensor_tensor(eq_t, eq_t, lower, ALU.mult), s_rank, base + 2)
                    then(dve.tensor_reduce(seg_n[:, SEG:SEG + 1], eq_t, AX.X, ALU.add), s_rank, base + 3)
                    then(dve.tensor_reduce(pos_f[:, bass.ds(t, 1)], seg_n, AX.X, ALU.add), s_rank, base + 4)
                    then(dve.tensor_scalar(tile_keys, tile_keys, -0.5, None, ALU.add), s_rank, base + 5)
                then(dve.tensor_copy(pos_i, pos_f), s_ranked, 2)

            dve.wait_ge(s_iota, 2)
            dve.wait_ge(s_iT, 2)
            dve.tensor_copy(hp[:, :].rearrange("p (q h) -> p h q", h=2), ps_i[:, 4, 0, :, :]).then_inc(s_idx, 1)
            dve.tensor_copy(hcol[:, :].rearrange("p (q h) -> p h q", h=2), ps_i[:, 4, 1, :, :]).then_inc(s_idx, 1)
            dve.wait_ge(s_idx, 2)

            def onehots(turn, slot, wait):
                t = 4 * turn + slot
                if wait:
                    dve.wait_ge(s_hist, t - 3)
                dve.tensor_scalar(ha[slot], iota_p[:, :], hp[:, bass.ds(t, 1)], None, ALU.is_equal
                                  ).then_inc(s_onehot, 1)
                dve.tensor_scalar(hb[slot], iota_c, hcol[:, bass.ds(t, 1)], None, ALU.is_equal
                                  ).then_inc(s_onehot, 1)

            for slot in range(4):
                onehots(0, slot, False)
            with dve.Fori(1, TILES // 4) as turn:
                for slot in range(4):
                    onehots(turn, slot, True)
            deg, root = zc[:, 0, 0:CH * J], zc[:, 1, 0:CH * J]
            dve.wait_ge(s_hist, TILES)
            dve.tensor_scalar(deg.rearrange("p (a b) -> p a b", a=2), hist, 1.0, None, ALU.add).then_inc(s_deg, 1)
            dve.wait_ge(s_root, 1)
            then(dve.reciprocal(dinv[:, :], root), s_deg, 2)
            newton(dinv[:, :], deg, root, s_deg, 2)
            dve.sem_inc(s_dinv, 1)

            dve.wait_ge(s_rows, 32)
            here, prev, nxt = rwin[:, 1:RE + 1], rwin[:, 0:RE], rwin[:, 2:RE + 2]
            dve.tensor_copy(rows[:, 0, :], rsrc)
            dve.tensor_scalar(rows[:, 1, :], here, float(N - 1), None, ALU.min)
            then(dve.tensor_tensor(rows[:, 4, :], here, prev, ALU.is_equal), s_ri, 1)
            then(dve.tensor_tensor(rows[:, 5, :], here, nxt, ALU.is_equal), s_ri, 2)
            dve.scalar_tensor_tensor(rows[:, 2, :], rows[:, 5, :], float(OFF), here, ALU.mult, ALU.add
                                     ).then_inc(s_ri, 1)
            dve.scalar_tensor_tensor(rows[:, 3, :], rows[:, 4, :], float(OFF), here, ALU.mult, ALU.add
                                     ).then_inc(s_ri, 1)
            dve.wait_ge(s_iT, 3)
            by_tile = lambda a: ps_i[:, a // 2, a % 2, :, :]
            qh = lambda a: a.rearrange("p (q h) -> p h q", h=2)
            dve.tensor_copy(qh(sq[:, 0, 0:TILES]), by_tile(3)).then_inc(s_idx, 1)
            four = idx[:, :, :].rearrange("p (k2 x) (a i) -> p k2 x a i", x=1, i=TPC)
            for a in range(3):
                for h in range(2):
                    dve.tensor_copy(
                        four[:, :, 0, a, h::2],
                        ps_i[:, a // 2, a % 2, h, :].rearrange("p (k i) -> p k i", i=2)).then_inc(s_idx, 1)
            dve.tensor_copy(qh(same_prev[:, :]), by_tile(4)).then_inc(s_idx, 1)
            dve.tensor_copy(qh(same_next[:, :]), by_tile(5)).then_inc(s_idx, 1)
            dve.wait_ge(s_idx, 11)
            dve.tensor_scalar(is_last[:, :], same_next[:, :], -1.0, 1.0, ALU.mult, ALU.add).then_inc(s_idx, 1)
            dve.wait_ge(s_iT, 4)
            dve.tensor_copy(four[:, :, 0, 3, :], ps_flip.rearrange("p (k i) -> p k i", i=TPC)).then_inc(s_idx, 1)

            def stats0(c):
                if c.real():
                    two = c.slot % 2
                    dve.wait_ge(s_x[c.slot], 16 * (c.turn + 1))
                    cols = mean1[:, bass.ds(c.n * J, J)]
                    x3 = col3(x_in[:, c.slot, :])
                    then(dve.tensor_reduce(cols, x3, AX.X, ALU.add), s_xst, 2 * c.n + 1)
                    then(dve.tensor_scalar(cols, cols, 1.0 / D, None, ALU.mult), s_xst, 2 * c.n + 2)
                    if c.after(2):
                        dve.wait_ge(s_sq0, c.n - 1)
                    dve.tensor_tensor(col3(zc[:, two, :]), x3, wide(cols, J, D), ALU.subtract).then_inc(s_xc, 1)
                b = c.back(1)
                if b.real():
                    dve.wait_ge(s_sq0, b.n + 1)
                    dve.tensor_reduce(scale1[:, bass.ds(b.n * J, J)], col3(sq[:, b.slot % 2, :]), AX.X, ALU.add
                                      ).then_inc(s_v0, 1)

            run_chunks(dve, stats0, 4, 4, 1)

            a1 = zc[:, 0, 0:CH * J]
            tmp = zc[:, 1, 0:CH * J]
            dve.wait_ge(s_v0, CH)
            dve.wait_ge(s_sq0, CH)
            then(dve.tensor_tensor(a1, dinv[:, :], dinv[:, :], ALU.mult), s_scale, 1)
            then(dve.tensor_scalar(a1, a1, 1.0, None, ALU.add), s_scale, 2)
            then(dve.tensor_tensor(tmp, a1, a1, ALU.mult), s_scale, 3)
            then(dve.tensor_tensor(tmp, tmp, scale1[:, :], ALU.mult), s_scale, 4)
            then(dve.tensor_scalar(tmp, tmp, 1.0 / D, EPS, ALU.mult, ALU.add), s_scale, 5)
            dve.wait_ge(s_root, 2)
            then(dve.reciprocal(scale1[:, :], sq[:, 0, 0:CH * J]), s_scale, 6)
            newton(scale1[:, :], tmp, sq[:, 1, 0:CH * J], s_scale, 6)
            then(dve.tensor_tensor(scale1[:, :], scale1[:, :], a1, ALU.mult), s_scale, 10)
            dve.memset(cT[HC:HC + 1, :], 1.0).then_inc(s_scale, 1)

            dve.wait_ge(s_tst[0], 16 * (CH // 2 + 1))
            dve.wait_ge(s_tst[1], 16 * (CH // 2))

            def pass1(c):
                e, l = c.back(1), c.back(2)
                if l.real():
                    dve.wait_ge(q_pow, 11 * (l.n + 1))
                    if l.after(2):
                        dve.wait_ge(p_st[l.slot], 16 * l.turn)
                    dve.tensor_tensor(col3(outb[:, l.slot, :]), col3(zc[:, l.slot, :]),
                                      wide(rstd[:, l.slot, 0:J], J, D), ALU.mult).then_inc(p_out, 1)
                    then(dve.tensor_tensor(sm[:, 0:TPC], rstd[:, l.slot, J:J + TPC],
                                           is_last[:, bass.ds(l.n * TPC, TPC)], ALU.mult), q_xd, 2 * l.n + 1)
                    dve.tensor_tensor(xd_all[:, bass.ds(l.n * EF, EF)].rearrange("p (t f) -> p t f", f=D),
                                      vc_e[:, l.slot, :, :], wide(sm[:, 0:TPC], TPC, D), ALU.mult).then_inc(q_xd, 1)
                if c.real():
                    dve.wait_ge(p_x[c.slot], 16 * (c.turn + 1))
                    then(dve.tensor_tensor(col3(x1[:, c.slot, :]), col3(x_in[:, c.slot, :]),
                                           wide(mean1[:, bass.ds(c.n * J, J)], J, D), ALU.subtract),
                         p_x1, 2 * c.n + 1)
                    dve.tensor_tensor(col3(x1[:, c.slot, :]), col3(x1[:, c.slot, :]),
                                      wide(scale1[:, bass.ds(c.n * J, J)], J, D), ALU.mult).then_inc(p_x1, 1)
                if e.real():
                    s = e.slot
                    dve.wait_ge(q_gs[s], 64 * (e.turn + 1))
                    if e.after(1):
                        dve.wait_ge(q_wT, e.n)
                    dve.tensor_tensor(w_x[:, :, :], gs[:, s, :, 0:D], gs[:, s, :, D:TW].to_broadcast([P, TPC, D]),
                                      ALU.mult).then_inc(q_w, 1)
                    dve.tensor_tensor(mask_rhs[:, :, :], ident_b[:, :].unsqueeze(1).to_broadcast([P, TPC, P]),
                                      wide(same_prev[:, bass.ds(e.n * TPC, TPC)], TPC, P), ALU.mult).then_inc(q_w, 1)
                    dve.wait_ge(p_og, e.n + 1)
                    z3 = col3(zc[:, s, :])
                    then(dve.scalar_tensor_tensor(zc[:, s, :], x1[:, s, :], 2.0, comb[:, :], ALU.mult, ALU.add), p_z, 4 * e.n + 1)
                    then(dve.tensor_reduce(sums[:, 0:J], z3, AX.X, ALU.add), p_z, 4 * e.n + 2)
                    then(dve.tensor_scalar(sums[:, 0:J], sums[:, 0:J], 1.0 / D, None, ALU.mult), p_z, 4 * e.n + 3)
                    dve.tensor_tensor(z3, z3, wide(sums[:, 0:J], J, D), ALU.subtract).then_inc(p_z, 1)
                    dve.wait_ge(q_wT, e.n + 1)
                    dve.wait_ge(q_mask, e.n + 1)
                    if e.after(1):
                        dve.wait_ge(q_f, e.n)
                        carry = fsum[:, 1 - s, EC - 1:EC]
                    else:
                        carry = 0.0
                    dve.tensor_tensor_scan(fsum[:, s, :], mask[0:D, :], ps_w, carry, ALU.mult, ALU.add).then_inc(q_f, 1)
                    dve.wait_ge(p_sq, e.n + 1)
                    dve.wait_ge(p_z, 4 * (e.n + 1))
                    dve.tensor_reduce(sums[:, 0:J], col3(sq[:, 0, :]), AX.X, ALU.add).then_inc(p_sqs, 1)
                    dve.wait_ge(q_fT, e.n + 1)
                    if e.after(2):
                        dve.wait_ge(q_sc[s], 64 * e.turn)
                    agv = ag[:, s, :].rearrange("p (t f) -> p t f", f=D)
                    dve.tensor_copy(ag[:, s, :], ps_ag).then_inc(q_ag, 1)
                    dve.wait_ge(q_gd[s], 64 * (e.turn + 1))
                    dcol = gd[:, s, :, D:TW]
                    q = 9 * e.n
                    then(dve.tensor_tensor(sm[:, 4:8].unsqueeze(2), dcol, dcol, ALU.mult), q_v, q + 1)
                    then(dve.scalar_tensor_tensor(v_e[:, :, :], wide(sm[:, 4:8], TPC, D), 1.0, gd[:, s, :, 0:D],
                                                  ALU.add, ALU.mult), q_v, q + 2)
                    dve.wait_ge(q_ag, e.n + 1)
                    then(dve.tensor_tensor(t_e[:, :, :], agv, dcol.to_broadcast([P, TPC, D]), ALU.mult), q_v, q + 3)
                    then(dve.tensor_tensor(v_e[:, :, :], v_e[:, :, :], t_e[:, :, :], ALU.add), q_v, q + 4)
                    then(dve.tensor_reduce(sm[:, 8:12], v_e[:, :, :], AX.X, ALU.add), q_v, q + 5)
                    then(dve.tensor_scalar(sm[:, 8:12], sm[:, 8:12], 1.0 / D, None, ALU.mult), q_v, q + 6)
                    then(dve.tensor_tensor(vc_e[:, s, :, :], v_e[:, :, :], wide(sm[:, 8:12], TPC, D), ALU.subtract),
                         q_v, q + 7)
                    then(dve.tensor_tensor(t_e[:, :, :], vc_e[:, s, :, :], vc_e[:, s, :, :], ALU.mult), q_v, q + 8)
                    then(dve.tensor_reduce(sums[:, J:J + TPC], t_e[:, :, :], AX.X, ALU.add), q_v, q + 9)
                    dve.wait_ge(p_sqs, e.n + 1)
                    dve.tensor_scalar(var[:, s, :], sums[:, :], 1.0 / D, EPS, ALU.mult, ALU.add).then_inc(q_var, 1)
                    dve.wait_ge(q_var, e.n + 1)
                    rsqrt(rstd[:, s, :], var[:, s, :], nw[:, :], q_pow, 11 * e.n)

            run_chunks(dve, pass1, 2, 4, 2)
            dve.wait_ge(q_xd, 2 * CH)
            dve.wait_ge(p_st[0], 16 * (CH // 2 + 1))
            dve.wait_ge(p_st[1], 16 * (CH // 2))
            dve.sem_inc(r_start, 1)
            dve.wait_ge(r_start, 4)

            def pass2(c):
                a, b, g, h, l = c.back(1), c.back(2), c.back(3), c.back(4), c.back(5)
                if l.real():
                    dve.wait_ge(r_pow, 11 * (l.n + 4))
                    if l.after(2):
                        dve.wait_ge(r_sc[l.slot], 64 * l.turn)
                    dve.tensor_tensor(out_e[l.slot].rearrange("p (t f) -> p t f", f=D), zc_e[l.slot],
                                      wide(rstd[:, b.slot, TPC:2 * TPC], TPC, D), ALU.mult).then_inc(r_out, 1)
                if g.real():
                    dve.wait_ge(r_mg, g.n + 1)
                    dve.wait_ge(r_xs, 3 * (g.n + 1))
                    dve.wait_ge(r_h, g.n + 1)
                    if g.after(1):
                        dve.wait_ge(r_box, g.n)
                        carry = xin[1 - g.slot][0:D, EC - 1:EC]
                    else:
                        carry = 0.0
                    dve.tensor_tensor_scan(xin[g.slot][0:D, :], mask[0:D, :], mT[g.slot], carry,
                                           ALU.mult, ALU.add).then_inc(r_box, 1)
                if b.real():
                    k = (CH - 1) - b.n
                    dve.wait_ge(r_pow, 11 * (b.n + 1))
                    if b.after(1):
                        dve.wait_ge(r_tm, b.n)
                    dve.tensor_tensor(m_in[:, b.slot, :, 0:D], vc_e[:, b.slot, :, :],
                                      wide(rstd[:, b.slot, 0:TPC], TPC, D), ALU.mult).then_inc(r_m, 1)
                    for t in range(TPC):
                        u = TPC - 1 - t
                        ins = dve.tensor_scalar(mask_rhs[:, t, :], flip_b[:, :],
                                                same_next[:, bass.ds(k * TPC + u, 1)], None, ALU.mult)
                    ins.then_inc(r_m, 1)
                if a.real():
                    k = (CH - 1) - a.n
                    s = a.slot
                    q = 9 * a.n
                    rows_ = xs_all[:, bass.ds(k * (TPC * TW), TPC * TW)].rearrange("p (t f) -> p t f", f=TW)
                    dcol = rows_[:, :, D:TW]
                    then(dve.tensor_tensor(sm[:, 4:8].unsqueeze(2), dcol, dcol, ALU.mult), r_a, q + 1)
                    then(dve.scalar_tensor_tensor(v_e[:, :, :], wide(sm[:, 4:8], TPC, D), 1.0, rows_[:, :, 0:D],
                                                  ALU.add, ALU.mult), r_a, q + 2)
                    dve.wait_ge(r_ga[s], 64 * (a.turn + 1))
                    then(dve.tensor_tensor(t_e[:, :, :], ga[:, s, :].rearrange("p (t f) -> p t f", f=D),
                                           dcol.to_broadcast([P, TPC, D]), ALU.mult), r_a, q + 3)
                    then(dve.tensor_tensor(v_e[:, :, :], v_e[:, :, :], t_e[:, :, :], ALU.add), r_a, q + 4)
                    then(dve.tensor_reduce(sm[:, 8:12], v_e[:, :, :], AX.X, ALU.add), r_a, q + 5)
                    then(dve.tensor_scalar(sm[:, 8:12], sm[:, 8:12], 1.0 / D, None, ALU.mult), r_a, q + 6)
                    then(dve.tensor_tensor(vc_e[:, s, :, :], v_e[:, :, :], wide(sm[:, 8:12], TPC, D), ALU.subtract),
                         r_a, q + 7)
                    then(dve.tensor_tensor(t_e[:, :, :], vc_e[:, s, :, :], vc_e[:, s, :, :], ALU.mult), r_a, q + 8)
                    then(dve.tensor_reduce(sums[:, 0:TPC], t_e[:, :, :], AX.X, ALU.add), r_a, q + 9)
                if b.real():
                    dve.wait_ge(r_tm, b.n + 1)
                    dve.wait_ge(r_xs, 3 * b.n + 2)
                    if b.after(2):
                        dve.wait_ge(r_o, b.n - 1)
                    if b.after(1):
                        dve.wait_ge(r_xd, b.n)
                        carry = xin[1 - b.slot][D:P, EC - 1:EC]
                    else:
                        carry = 0.0
                    dve.tensor_tensor_scan(xin[b.slot][D:P, :], mask[D:P, :], ps[D:P, 0, :], carry,
                                           ALU.mult, ALU.add).then_inc(r_xd, 1)
                if h.real():
                    q = 6 * h.n
                    s = h.slot
                    dve.wait_ge(r_og, h.n + 1)
                    then(dve.scalar_tensor_tensor(zc_e[s], ps[:, 6 + s, EF:2 * EF].rearrange("p (t f) -> p t f", f=D), 2.0,
                                                  comb_e[s], ALU.mult, ALU.add), r_z, q + 1)
                    then(dve.tensor_reduce(sm[:, 12:16], zc_e[s], AX.X, ALU.add), r_z, q + 2)
                    then(dve.tensor_scalar(sm[:, 12:16], sm[:, 12:16], 1.0 / D, None, ALU.mult), r_z, q + 3)
                    then(dve.tensor_tensor(zc_e[s], zc_e[s], wide(sm[:, 12:16], TPC, D), ALU.subtract), r_z, q + 4)
                    then(dve.tensor_tensor(sq_e, zc_e[s], zc_e[s], ALU.mult), r_z, q + 5)
                    then(dve.tensor_reduce(sums[:, TPC:2 * TPC], sq_e, AX.X, ALU.add), r_z, q + 6)
                if a.real() or h.real():
                    dve.tensor_scalar(var[:, a.slot, 0:2 * TPC], sums[:, 0:2 * TPC], 1.0 / D, EPS,
                                      ALU.mult, ALU.add).then_inc(r_var, 1)
                    dve.wait_ge(r_var, a.n + 1)
                    rsqrt(rstd[:, a.slot, 0:2 * TPC], var[:, a.slot, 0:2 * TPC], nw[:, 0:2 * TPC], r_pow, 11 * a.n)

            run_chunks(dve, pass2, 2, 6, 5)

        @block.gpsimd
        def _(pool):
            pool.memset(ident[:, :], 1.0).then_inc(s_stage, 1)
            pool.memset(flip[:, :], 1.0).then_inc(s_stage, 1)
            pool.memset(lower, 1.0).then_inc(s_stage, 1)
            pool.iota(iota_p[:, :], [[1, P]], base=0, channel_multiplier=0,
                      allow_small_or_imprecise_dtypes=True).then_inc(s_iota, 1)
            pool.iota(iota_c, [[1, CH * J]], base=0, channel_multiplier=0,
                      allow_small_or_imprecise_dtypes=True).then_inc(s_iota, 1)
            pool.wait_ge(s_stage, 3)
            pool.affine_select(ident[:, :], ident[:, :], [[-1, P]], ALU.is_equal, 0.0, base=0,
                               channel_multiplier=1).then_inc(s_consts, 1)
            pool.affine_select(flip[:, :], flip[:, :], [[1, P]], ALU.is_equal, 0.0, base=-(P - 1),
                               channel_multiplier=1).then_inc(s_consts, 1)
            pool.affine_select(lower, lower, [[-1, P]], ALU.is_gt, 0.0, base=0,
                               channel_multiplier=1).then_inc(s_lower, 1)
            pool.wait_ge(s_consts, 2)
            pool.tensor_copy(ident_b[:, :], ident[:, :]).then_inc(s_consts, 1)
            pool.tensor_copy(flip_b[:, :], flip[:, :]).then_inc(s_consts, 1)

            pool.wait_ge(s_flag, 1)
            unsorted = pool.value_load(flag[0:1, 0:1], min_val=0, max_val=1)
            with pool.If(unsorted == 1):
                key_row = dsts[GUARD, :].rearrange("n a -> (n a)")
                pool.dma_start(keys.bitcast(I32), key_row.partition_broadcast(P)).then_inc(s_perm, 16)
                for half in range(2):
                    t0 = half * ROWS
                    pool.dma_start(dst_e[:, t0:t0 + ROWS],
                                   dsts[1 + t0 * P:1 + (t0 + ROWS) * P, :].rearrange("(t p) a -> p (t a)", p=P),
                                   allow_slow_non_contiguous=True).then_inc(s_keys, 16)
                pool.wait_ge(s_perm, 16)
                pool.tensor_copy(keys, keys.bitcast(I32)).then_inc(s_keys, 16)
                pool.wait_ge(s_ranked, 2)
                with pool.Fori(0, TILES) as t:
                    pool.dma_start(sort_s, srcs[bass.ds(t * P, P), :]).then_inc(s_tile, 16)
                    pool.dma_start(sort_e, attrs[bass.ds(t * P, P), :]).then_inc(s_tile, 16)
                    pool.tensor_copy(sort_i[:, 0:1], pos_i[:, bass.ds(t, 1)]).then_inc(s_stage, 1)
                    pool.tensor_copy(sort_i[:, 1:2], dst_e[:, bass.ds(t, 1)]).then_inc(s_stage, 1)
                    pool.wait_ge(s_tile, 32 * (t + 1))
                    pool.wait_ge(s_stage, 3 + 2 * (t + 1))
                    at = bass.IndirectOffsetOnAxis(ap=sort_i[:, 0:1], axis=0)
                    settled(pool)
                    pool.indirect_dma_start(src_perm, at, sort_s, None).then_inc(s_perm, 16)
                    pool.indirect_dma_start(dst_perm, at, sort_i[:, 1:2], None).then_inc(s_perm, 16)
                    pool.indirect_dma_start(attr_perm, at, sort_e, None).then_inc(s_perm, 16)
                    pool.wait_ge(s_perm, 16 + 48 * (t + 1))
                pool.dma_start(srcs, src_perm).then_inc(s_back, 16)
                pool.dma_start(dsts[GUARD, :], dst_perm).then_inc(s_back, 16)
                pool.dma_start(attrs, attr_perm).then_inc(s_back, 16)
                pool.wait_ge(s_back, 48)
            pool.sem_inc(s_sorted, 1)

            pool.wait_ge(s_idx, 13)
            pool.wait_ge(s_tst[0], 16 * (CH // 2 + 1))
            pool.wait_ge(s_tst[1], 16 * (CH // 2))
            pool.wait_ge(s_zero, 16)

            def pass1(c):
                e, l = c, c.back(1)
                if e.real():
                    if e.after(1):
                        prev = e.back(1)
                        pool.wait_ge(q_gs[prev.slot], 64 * (prev.turn + 1))
                        pool.wait_ge(q_gd[prev.slot], 64 * (prev.turn + 1))
                    settled(pool)
                    pool.tensor_copy(istage[:, 0:8], idx[:, bass.ds(e.n, 1), 0:8].rearrange("p a b -> p (a b)")
                                     ).then_inc(q_is, 1)
                    pool.wait_ge(q_is, e.n + 1)
                    if e.after(2):
                        pool.wait_ge(q_xs, e.n - 1)
                        pool.wait_ge(q_w, 2 * (e.n - 1))
                    settled(pool)
                    for t in range(TPC):
                        pool.indirect_dma_start(gs[:, e.slot, t, :], None, table,
                                                bass.IndirectOffsetOnAxis(ap=istage[:, t:t + 1], axis=0)
                                                ).then_inc(q_gs[e.slot], 16)
                    if e.after(2):
                        pool.wait_ge(q_v, 9 * (e.n - 1))
                    settled(pool)
                    for t in range(TPC):
                        pool.indirect_dma_start(gd[:, e.slot, t, :], None, table,
                                                bass.IndirectOffsetOnAxis(ap=istage[:, TPC + t:TPC + t + 1], axis=0)
                                                ).then_inc(q_gd[e.slot], 16)
                if l.real():
                    if l.after(1):
                        prev = l.back(1)
                        pool.wait_ge(q_sc[prev.slot], 64 * (prev.turn + 1))
                    settled(pool)
                    pool.tensor_copy(istage[:, 8:12], idx[:, bass.ds(l.n, 1), 8:12].rearrange("p a b -> p (a b)")
                                     ).then_inc(q_il, 1)
                    pool.wait_ge(q_il, l.n + 1)
                    pool.wait_ge(q_ag, l.n + 1)
                    settled(pool)
                    for t in range(TPC):
                        pool.indirect_dma_start(agg, bass.IndirectOffsetOnAxis(ap=istage[:, 8 + t:9 + t], axis=0),
                                                ag[:, l.slot, t * D:(t + 1) * D], None,
                                                bounds_check=N - 1, oob_is_err=False).then_inc(q_sc[l.slot], 16)

            run_chunks(pool, pass1, 2, 2, 1)
            pool.wait_ge(q_sc[0], 64 * (CH // 2 + 1))
            pool.wait_ge(q_sc[1], 64 * (CH // 2))
            pool.wait_ge(q_v, 9 * CH)
            pool.sem_inc(r_start, 1)
            pool.wait_ge(r_start, 4)
            pool.wait_ge(p_st[0], 16 * (CH // 2 + 1))
            pool.wait_ge(p_st[1], 16 * (CH // 2))

            def pass2(c):
                l = c.back(5)
                if c.real():
                    k = (CH - 1) - c.n
                    if c.after(1):
                        prev = c.back(1)
                        pool.wait_ge(r_ga[prev.slot], 64 * (prev.turn + 1))
                    settled(pool)
                    pool.tensor_copy(istage[:, 0:4], idx[:, bass.ds(k, 1), 0:4].rearrange("p a b -> p (a b)")
                                     ).then_inc(r_is, 1)
                    pool.wait_ge(r_is, c.n + 1)
                    if c.after(2):
                        pool.wait_ge(r_a, 9 * (c.n - 1))
                    settled(pool)
                    for t in range(TPC):
                        pool.indirect_dma_start(ga[:, c.slot, t * D:(t + 1) * D], None, agg,
                                                bass.IndirectOffsetOnAxis(ap=istage[:, t:t + 1], axis=0)
                                                ).then_inc(r_ga[c.slot], 16)
                if l.real():
                    k = (CH - 1) - l.n
                    if l.after(1):
                        prev = l.back(1)
                        pool.wait_ge(r_sc[prev.slot], 64 * (prev.turn + 1))
                    settled(pool)
                    pool.tensor_copy(istage[:, 12:16], idx[:, bass.ds(k, 1), 12:16].rearrange("p a b -> p (a b)")
                                     ).then_inc(r_io, 1)
                    pool.wait_ge(r_io, l.n + 1)
                    pool.wait_ge(r_out, l.n + 1)
                    settled(pool)
                    for t in range(TPC):
                        u = 12 + TPC - 1 - t
                        pool.indirect_dma_start(out, bass.IndirectOffsetOnAxis(ap=istage[:, u:u + 1], axis=0),
                                                out_e[l.slot][:, t * D:(t + 1) * D], None,
                                                bounds_check=N - 1, oob_is_err=False).then_inc(r_sc[l.slot], 16)

            run_chunks(pool, pass2, 2, 6, 5)
            pool.wait_ge(r_sc[0], 64 * (CH // 2 + 1))
            pool.wait_ge(r_sc[1], 64 * (CH // 2))


_INS = ['x', 'src', 'dst', 'edge_attr_32', 'L1_gnn_W_m1', 'L1_gnn_b_m1', 'L1_gnn_W_m2', 'L1_gnn_b_m2',
        'L1_gnn_W_c1', 'L1_gnn_b_c1', 'L1_gnn_W_c2', 'L1_gnn_b_c2']


def kernel(**inputs):
    import numpy as _np
    import concourse.bacc as _bacc
    from concourse import mybir as _mybir
    from concourse.bass_utils import run_bass_kernel_spmd as _run

    nc = _bacc.Bacc("TRN2", target_bir_lowering=False, num_devices=1)
    arrays, args = {}, []
    for name in _INS:
        a = _np.ascontiguousarray(inputs[name])
        arrays[f"in_{name}_dram"] = a
        args.append(nc.dram_tensor(f"in_{name}_dram", a.shape, _mybir.dt.from_np(a.dtype), kind="ExternalInput").ap())
    result = nc.dram_tensor("out_0_dram", (N, D), F32, kind="ExternalOutput").ap()
    build(nc, *args, result)
    r = _run(nc, [arrays], core_ids=[0])
    return r.results[0]["out_0_dram"]
```

```python
from contextlib import ExitStack

import concourse.bass as bass
from concourse import mybir
from concourse.alu_op_type import AluOpType as ALU

F32 = mybir.dt.float32
F16 = mybir.dt.float16
BF16 = mybir.dt.bfloat16
I32 = mybir.dt.int32
ACT = mybir.ActivationFunctionType
AX = mybir.AxisListType

P = 128
N, D = 100000, 64
E, DE = 25000, 32
HM, HC = 80, 96
EPS = 1e-5
J = 16
NCH = P * J
CH = -(-N // NCH)
LASTP = (N - (CH - 1) * NCH) // J
TILES = 196
TPC = 4
ECH = TILES // TPC
EP = TILES * P
ROWS = TILES // 2
RE = 2 * P
OFF = 1 << 17
SEG = 8
FREE = J * D
EF = TPC * D
EC = TPC * P
EARLY = 3
assert CH == ECH and LASTP * J == N - (CH - 1) * NCH


class Chunk:

    def __init__(self, unroll, turn, slot):
        self.unroll, self.turn, self.slot = unroll, turn, slot
        self.n = turn * unroll + slot

    def back(self, k):
        turns, slot = divmod(self.slot - k, self.unroll)
        return Chunk(self.unroll, self.turn + turns, slot)

    @property
    def two(self):
        return self.slot % 2

    @property
    def uses(self):
        return self.turn * (self.unroll // 2) + self.slot // 2

    def real(self):
        return not isinstance(self.n, int) or 0 <= self.n < CH

    def after(self, k):
        return not isinstance(self.n, int) or self.n >= k


def run_chunks(eng, body, unroll, peel, skew, ahead=0):
    for n in range(peel):
        body(Chunk(unroll, n // unroll, n % unroll))
    last = (CH - 1 - ahead) // unroll
    with eng.Fori(peel // unroll, last) as turn:
        for slot in range(unroll):
            body(Chunk(unroll, turn, slot))
    for n in range(last * unroll, CH + skew):
        body(Chunk(unroll, n // unroll, n % unroll))


def build(nc, x, src, dst, edge_attr, w_m1, b_m1, w_m2, b_m2, w_c1, b_c1, w_c2, b_c2, out):
    with ExitStack() as ctx:
        def sb(name, shape, dt=F32):
            return ctx.enter_context(nc.sbuf_tensor(name, shape, dt))

        def sem(name):
            return ctx.enter_context(nc.semaphore(name))

        x1t = nc.dram_tensor("x1t", (N, D), F32).ap()
        dinv_t = nc.dram_tensor("dinv_t", (CH * NCH, 1), F32).ap()
        srcs = nc.dram_tensor("srcs", (EP, 1), I32).ap()
        dsts = nc.dram_tensor("dsts", (EP + 2, 1), I32).ap()
        attrs = nc.dram_tensor("attrs", (EP, DE), F32).ap()
        src_perm = nc.dram_tensor("src_perm", (EP, 1), I32).ap()
        dst_perm = nc.dram_tensor("dst_perm", (EP, 1), I32).ap()
        attr_perm = nc.dram_tensor("attr_perm", (EP, DE), F32).ap()

        x_all = sb("x_all", [P, ECH * 2 * EF])
        keys = x_all[:, 0:EP]
        d_all = sb("d_all", [P, ECH * 2 * TPC])
        x_in = sb("x_in", [P, 4, FREE])
        xT = sb("xT", [P, 2, FREE])
        cT = sb("cT", [P, 2 * FREE])
        zT = sb("zT", [P, 2, FREE])
        sq = sb("sq", [P, 2, FREE])
        outb = sb("outb", [P, 2, FREE])
        dinv = sb("dinv", [P, CH * J])
        eps_a = sb("eps_a", [P, CH * J])
        dsum = sb("dsum", [P, 3, J])
        dvar = sb("dvar", [P, 2 * J])
        drstd = sb("drstd", [P, 2, 2 * J])
        dnw = sb("dnw", [P, 2 * J])

        gx = sb("gx", [P, 2, 2 * EF])
        gdv = sb("gdv", [P, 2, 2 * TPC])
        w_x = sb("w_x", [P, 2, TPC, D])
        mask_rhs = sb("mask_rhs", [P, 2, TPC, P], BF16)
        mask = sb("mask", [P, EC])
        fsum = sb("fsum", [D, 2, EC])
        v_e = sb("v_e", [P, TPC, D])
        ag_e = sb("ag_e", [P, TPC, D])
        t_e = sb("t_e", [P, TPC, D])
        vc_e = sb("vc_e", [P, 2, TPC, D])
        sm = sb("sm", [P, 64])

        idx = sb("idx", [P, ECH, 16], I32)
        istage = sb("istage", [P, 5, 2, 2 * TPC], I32)
        same_prev = sb("same_prev", [P, TILES])
        same_next = sb("same_next", [P, TILES])
        is_last = sb("is_last", [P, TILES])
        hp = sb("hp", [P, TILES])
        hcol = sb("hcol", [P, TILES])
        flag = sb("flag", [1, 1], I32)

        ident = sb("ident", [P, P])
        flip = sb("flip", [P, P])
        centre = sb("centre", [P, P])
        ident_b = sb("ident_b", [P, P], BF16)
        flip_b = sb("flip_b", [P, P], BF16)
        ones_b = sb("ones_b", [P, P], BF16)
        ones_f = sb("ones_f", [P, 1])
        iota_p = sb("iota_p", [P, P], F16)
        wx_d = sb("wx_d", [P, HC])
        wm1 = sb("wm1", [P, HM])
        wme = sb("wme", [DE, HM])
        wm2 = sb("wm2", [HM, D])
        wc1 = sb("wc1", [P, HC])
        wc2 = sb("wc2", [HC + 1, D])
        bm1 = sb("bm1", [HM, 1])
        bm2 = sb("bm2", [D, 1])
        bc1 = sb("bc1", [HC, 1])
        bc2 = sb("bc2", [P, 1])

        rows = zT[:, :, :].rearrange("p a b -> p (a b)").rearrange("p (n e) -> p n e", e=RE)[0:ROWS]
        rwin = xT[0:ROWS, 0, 0:RE + 2].bitcast(I32)
        rsrc = xT[0:ROWS, 0, 260:260 + RE].bitcast(I32)
        rtmp = xT[0:ROWS, 0, 520:520 + RE].bitcast(I32)
        rsorted = xT[0:ROWS, 1, 0:RE].bitcast(I32)
        rtm2 = cT[0:ROWS, 0:RE].bitcast(I32)
        usum = sm[0:ROWS, 0:1]
        hist_b = outb[:, :, :].rearrange("p a b -> p (a b)").bitcast(BF16)
        hb = [hist_b[:, i * CH * J:(i + 1) * CH * J] for i in range(4)]
        ha = [hist_b[:, 4 * CH * J + i * P:4 * CH * J + (i + 1) * P] for i in range(4)]
        iota_c = cT[:, 1024:1024 + CH * J // 2].bitcast(F16)
        zeros = mask[0:EP - E, 0:DE]
        seg_out = outb[:, :, :].rearrange("p a b -> p (a b)").bitcast(BF16)[:, 0:EP // SEG]
        dst_e = cT[:, 256:256 + TILES].bitcast(I32)
        dst_ef = cT[:, 456:456 + TILES]
        pos_f = cT[:, 656:656 + TILES]
        pos_i = cT[:, 1420:1420 + TILES].bitcast(I32)
        lower = sq[:, 0, 0:P]
        eq_t = sq[:, 0, P:2 * P]
        seg_n = sm[:, 8:8 + SEG + 1]
        sort_i = sm[:, 32:34].bitcast(I32)
        sort_s = sm[:, 34:35].bitcast(I32)
        sort_e = sq[:, 1, 0:DE]
        m_in = x_in[:, 0, :].rearrange("p (s t f) -> p s t f", s=2, t=TPC)
        halves = lambda a: [a[:, i * EC:(i + 1) * EC] for i in range(2)]
        xin = halves(x_in[:, 1, :]) + halves(x_in[:, 2, :])
        mask_m = halves(x_in[:, 3, :]) + halves(outb[:, 1, :])
        eattr = sq[:, 1, 0:2 * TPC * DE].rearrange("p (s t f) -> p s t f", s=2, t=TPC)
        eT = halves(xT[0:DE, 0, :])
        mT = halves(xT[0:D, 1, :])
        hT = cT[0:HM, EC:2 * EC]
        c2T = cT[0:HC + 1, 0:EC]
        comb_e = [zT[:, 0, s * EF:(s + 1) * EF].rearrange("p (t f) -> p t f", f=D) for s in range(2)]
        zc_e = [zT[:, 1, s * EF:(s + 1) * EF].rearrange("p (t f) -> p t f", f=D) for s in range(2)]
        sq_e = sq[:, 0, 0:EF].rearrange("p (t f) -> p t f", f=D)
        out_e = [outb[:, 0, s * EF:(s + 1) * EF] for s in range(2)]

        ps = ctx.enter_context(nc.psum_tensor("ps", [P, 8, 512], F32))
        ps_xT = ps[:, 0:2, :]
        ps_z = [ps[:, 4 + 2 * s:6 + 2 * s, :].rearrange("p a b -> p (a b)") for s in range(2)]
        ps_w = [ps[0:D, s, :] for s in range(2)]
        ps_mask = [ps[0:D, 2 + s, :] for s in range(2)]
        ps_ag = [ps[:, 4 + s, 0:EF] for s in range(2)]
        hist = ps[:, 0:2, 0:CH * J // 2]
        ps_i = ps[:, 2:7, 0:4 * ROWS].rearrange("p a (n h q) -> p a n h q", n=2, h=2)
        ps_flip = ps[:, 7, 0:TILES]
        ps_u = ps[0:1, 7, 508:509]

        s_zeros = sem("s_zeros")
        s_guard = sem("s_guard")
        s_hfill = sem("s_hfill")
        s_ones = sem("s_ones")
        s_consts = sem("s_consts")
        s_lower = sem("s_lower")
        s_iota = sem("s_iota")
        s_pads = sem("s_pads")
        s_copy = sem("s_copy")
        s_weights = sem("s_weights")
        s_win = sem("s_win")
        s_hsrc = sem("s_hsrc")
        s_ucount = sem("s_ucount")
        s_flag = sem("s_flag")
        s_keys = sem("s_keys")
        s_keyf = sem("s_keyf")
        s_rank = sem("s_rank")
        s_ranked = sem("s_ranked")
        s_stage = sem("s_stage")
        s_tile = sem("s_tile")
        s_perm = sem("s_perm")
        s_back = sem("s_back")
        s_settled = sem("s_settled")
        s_sorted = sem("s_sorted")
        s_rows = sem("s_rows")
        s_hidx = sem("s_hidx")
        s_ri = sem("s_ri")
        s_iT = sem("s_iT")
        s_idx = sem("s_idx")
        s_onehot = sem("s_onehot")
        s_hist = sem("s_hist")
        s_deg = sem("s_deg")
        s_dinv = sem("s_dinv")
        s_root = sem("s_root")
        s_scale = sem("s_scale")
        s_dt = sem("s_dt")
        s_centre = sem("s_centre")
        s_biasrow = sem("s_biasrow")

        g_ia = sem("g_ia")
        g_x = [sem(f"g_x{i}") for i in range(2)]
        g_xk = [sem(f"g_xk{i}") for i in range(2)]
        g_ib = sem("g_ib")
        g_d = [sem(f"g_d{i}") for i in range(2)]
        g_dk = [sem(f"g_dk{i}") for i in range(2)]

        d_x = [sem(f"d_load{i}") for i in range(4)]
        d_m = sem("d_m")
        d_xc = sem("d_xc")
        d_sq1 = sem("d_sq1")
        d_s1 = sem("d_s1")
        d_v1 = sem("d_v1")
        d_v2 = sem("d_v2")
        d_pow = sem("d_pow")
        d_x1 = sem("d_x1")
        d_st1 = [sem(f"d_st1_{i}") for i in range(4)]
        d_T = sem("d_T")
        d_Ts = sem("d_Ts")
        d_c = sem("d_c")
        d_cg = sem("d_cg")
        d_o = sem("d_o")
        d_og = sem("d_og")
        d_zT = sem("d_zT")
        d_z = sem("d_z")
        d_sq2 = sem("d_sq2")
        d_s2 = sem("d_s2")
        d_out = sem("d_out")
        d_st = [sem(f"d_st{i}") for i in range(2)]

        q_w = sem("q_w")
        q_wT = sem("q_wT")
        q_mask = sem("q_mask")
        q_f = sem("q_f")
        q_fT = sem("q_fT")
        q_v = sem("q_v")
        q_sq = sem("q_sq")
        q_s = sem("q_s")
        q_var = sem("q_var")
        q_pow = sem("q_pow")
        q_xd = sem("q_xd")
        q_ks = [sem(f"q_ks{i}") for i in range(2)]
        q_ic = sem("q_ic")
        q_sc = [sem(f"q_sc{i}") for i in range(2)]

        r_start = sem("r_start")
        r_is = sem("r_is")
        r_io = sem("r_io")
        r_ga = [sem(f"r_ga{i}") for i in range(2)]
        r_e = [sem(f"r_e{i}") for i in range(2)]
        r_m = sem("r_m")
        r_md = sem("r_md")
        r_tm = sem("r_tm")
        r_xs = sem("r_xs")
        r_sq = sem("r_sq")
        r_s = sem("r_s")
        r_xd = sem("r_xd")
        r_h = sem("r_h")
        r_hg = sem("r_hg")
        r_mm = sem("r_mm")
        r_mg = sem("r_mg")
        r_box = sem("r_box")
        r_c = sem("r_c")
        r_cg = sem("r_cg")
        r_o = sem("r_o")
        r_og = sem("r_og")
        r_z = sem("r_z")
        r_var = sem("r_var")
        r_pow = sem("r_pow")
        r_out = sem("r_out")
        r_sc = [sem(f"r_sc{i}") for i in range(2)]
        block = ctx.enter_context(nc.Block())

        GUARD = slice(1, EP + 1)
        col3 = lambda a: a.rearrange("p (a b) -> p a b", b=D)
        wide = lambda a, n, f: a.unsqueeze(2).to_broadcast([a.shape[0], n, f])

        def x_chunk(c, t):
            if isinstance(c, int) and c == CH - 1:
                return t[c * NCH:N, :].rearrange("(p j) d -> p (j d)", j=J), LASTP
            return t[bass.ds(c * NCH, NCH), :].rearrange("(p j) d -> p (j d)", j=J), P

        def settled(eng):
            eng.sem_inc(s_settled, 1)

        @block.sync
        def _(sp):
            sp.wait_ge(s_zeros, 1)
            sp.dma_start(attrs[E:EP, :], zeros).then_inc(s_pads, 16)
            sp.dma_start(srcs[E:EP, :], zeros[:, 0:1].bitcast(I32)).then_inc(s_pads, 16)
            sp.dma_start(srcs[0:E, :], src.rearrange("(n a) -> n a", a=1)).then_inc(s_copy, 16)
            sp.dma_start(dsts[1:E + 1, :], dst.rearrange("(n a) -> n a", a=1)).then_inc(s_copy, 16)
            sp.wait_ge(s_guard, 3)
            sp.dma_start(dsts[E + 1:EP + 1, :], sort_s[0:EP - E, :]).then_inc(s_pads, 16)
            sp.dma_start(dsts[0:1, :], sort_i[0:1, 0:1]).then_inc(s_pads, 16)
            sp.dma_start(dsts[EP + 1:EP + 2, :], sort_i[0:1, 1:2]).then_inc(s_pads, 16)
            sp.dma_start(attrs[0:E, :].rearrange("(a b) d -> a (b d)", a=200),
                         edge_attr.rearrange("(a b) d -> a (b d)", a=200)).then_inc(s_copy, 16)
            full = E // RE
            sp.wait_ge(s_hfill, 1)
            sp.dma_start(rsrc[0:full, :], src[0:full * RE].rearrange("(q e) -> q e", e=RE)).then_inc(s_hsrc, 16)
            sp.dma_start(rsrc[full:full + 1, 0:E - full * RE],
                         src[full * RE:E].rearrange("(q e) -> q e", q=1)).then_inc(s_hsrc, 16)
            sp.wait_ge(s_pads, 80)
            sp.wait_ge(s_copy, 48)
            window = bass.AP(dsts.tensor, 0, [[RE, ROWS], [1, RE + 2]])
            sp.dma_start(rwin, window).then_inc(s_win, 16)
            sp.wait_ge(s_sorted, 1)
            sp.wait_ge(s_ucount, 1)
            sp.dma_start(rwin, window).then_inc(s_rows, 16)
            sp.dma_start(rsorted, srcs.rearrange("(q e) a -> q (e a)", e=RE)).then_inc(s_rows, 16)
            for dst_ap, src_ap in (
                    (wx_d[0:D, :], w_c1[0:D, :]), (wx_d[D:P, :], w_c1[0:D, :]), (wm1[:, :], w_m1[0:P, :]),
                    (wme[:, :], w_m1[P:P + DE, :]), (wm2[:, :], w_m2), (wc1[0:D, :], w_c1[D:P, :]),
                    (wc1[D:P, :], w_c1[0:D, :]), (wc2[0:HC, :], w_c2),
                    (wc2[HC:HC + 1, :], b_c2.rearrange("(a n) -> a n", a=1)),
                    (bm1[:, :], b_m1.rearrange("(n a) -> n a", a=1)),
                    (bm2[:, :], b_m2.rearrange("(n a) -> n a", a=1)),
                    (bc1[:, :], b_c1.rearrange("(n a) -> n a", a=1)),
                    (bc2[0:D, :], b_c2.rearrange("(n a) -> n a", a=1)),
                    (bc2[D:P, :], b_c2.rearrange("(n a) -> n a", a=1))):
                sp.dma_start(dst_ap, src_ap).then_inc(s_weights, 16)

            def keep_x(c):
                sp.wait_ge(g_x[c.slot], 128 * (c.turn + 1))
                settled(sp)
                sp.dma_start(x_all[:, bass.ds(c.n * (2 * EF), 2 * EF)], gx[:, c.slot, :]).then_inc(g_xk[c.slot], 16)

            def keep_d(c):
                sp.wait_ge(g_d[c.slot], 128 * (c.turn + 1))
                settled(sp)
                sp.dma_start(d_all[:, bass.ds(c.n * (2 * TPC), 2 * TPC)], gdv[:, c.slot, :]).then_inc(g_dk[c.slot], 16)

            def scatter_source(c):
                sp.wait_ge(q_xd, 2 * (c.n + 1))
                settled(sp)
                if c.after(2):
                    sp.wait_ge(q_sc[c.slot], 64 * c.turn)
                    settled(sp)
                sp.dma_start(gx[:, c.slot, 0:EF], x_all[:, bass.ds(c.n * (2 * EF) + EF, EF)]
                             ).then_inc(q_ks[c.slot], 16)

            run_chunks(sp, keep_x, 2, 2, 0)
            run_chunks(sp, keep_d, 2, 2, 0)
            run_chunks(sp, scatter_source, 2, 2, 0)
            sp.wait_ge(r_start, 4)

            def load_e(c):
                if c.after(2):
                    sp.wait_ge(r_tm, c.n - 1)
                    settled(sp)
                k = (CH - 1) - c.n
                sp.dma_start(eattr[:, c.two, :, :],
                             attrs[bass.ds(k * EC, EC), :].rearrange("(t p) d -> p t d", p=P)
                             ).then_inc(r_e[c.two], 16)

            run_chunks(sp, load_e, 2, 2, 0)

        @block.scalar
        def _(act):
            def load(c):
                src_ap, parts = x_chunk(c.n, x)
                act.dma_start(x_in[0:parts, c.slot, :], src_ap).then_inc(d_x[c.slot], 16)

            for n in range(4):
                load(Chunk(4, 0, n))
            act.wait_ge(s_deg, 1)
            act.activation(zT[:, 1, 0:CH * J], zT[:, 0, 0:CH * J], ACT.Sqrt).then_inc(s_root, 1)
            act.wait_ge(s_dinv, 1)
            act.dma_start(dinv_t.rearrange("(c p j) a -> p c (j a)", p=P, j=J),
                          dinv[:, :].rearrange("p (c j) -> p c j", j=J)).then_inc(s_dt, 16)

            act.wait_ge(s_weights, 16 * 14)

            def dense(c):
                n, g, o = c.back(2), c.back(4), c.back(6)
                nxt = c.back(-1)
                if n.real():
                    act.wait_ge(d_x1, n.n + 1)
                    dst_ap, parts = x_chunk(n.n, x1t)
                    act.dma_start(dst_ap, x_in[0:parts, n.slot, :]).then_inc(d_st1[n.slot], 16)
                if o.real():
                    act.wait_ge(d_out, o.n + 1)
                    dst_ap, parts = x_chunk(o.n, out)
                    act.dma_start(dst_ap, outb[0:parts, o.two, :]).then_inc(d_st[o.two], 16)
                if nxt.real() and nxt.after(4):
                    act.wait_ge(d_st1[nxt.slot], 16 * nxt.turn)
                    act.wait_ge(d_T, 2 * (nxt.n - 3))
                    load(nxt)
                if n.real():
                    s = n.two
                    if n.after(2):
                        act.wait_ge(d_zT, n.n - 1)
                        act.wait_ge(d_c, 4 * (n.n - 1))
                    for i in range(2):
                        act.wait_ge(d_T, 2 * n.n + i + 1)
                        act.activation(xT[:, s, i * 512:(i + 1) * 512], ps_xT[:, i, :], ACT.Copy).then_inc(d_Ts, 1)
                if g.real():
                    act.wait_ge(d_z, g.n + 1)
                    if g.after(1):
                        act.wait_ge(d_s2, g.n)
                    act.activation(sq[:, 1, :], ps_z[g.two], ACT.Square).then_inc(d_sq2, 1)
                for q in range(4):
                    if n.real():
                        i, half = divmod(q, 2)
                        act.wait_ge(d_c, 4 * n.n + q + 1)
                        if q == 0 and n.after(1):
                            act.wait_ge(d_o, n.n)
                        act.activation(cT[0:HC, half * FREE + i * 512:half * FREE + (i + 1) * 512], ps[0:HC, 2 + half, :],
                                       ACT.Gelu, bias=bc1[:, 0:1]).then_inc(d_cg, 1)
                    if q == 1 and c.real():
                        act.wait_ge(d_xc, c.n + 1)
                        if c.after(1):
                            act.wait_ge(d_s1, c.n)
                        act.activation(sq[:, 0, :], x_in[:, c.slot, :], ACT.Square).then_inc(d_sq1, 1)
                if n.real():
                    act.wait_ge(d_o, n.n + 1)
                    if n.after(2):
                        act.wait_ge(d_z, n.n - 1)
                    act.activation(zT[:, n.two, :], ps_xT.rearrange("p a b -> p (a b)"), ACT.Gelu,
                                   bias=bc2[:, 0:1]).then_inc(d_og, 1)

            run_chunks(act, dense, 4, 8, 6, ahead=1)

            def sums_pass(c):
                g = c.back(2)
                if c.real():
                    act.wait_ge(q_wT, c.n + 1)
                    if c.after(1):
                        act.wait_ge(q_f, c.n)
                    act.activation(mask[0:D, :], ps_mask[c.slot], ACT.Copy).then_inc(q_mask, 1)
                if g.real():
                    act.wait_ge(q_v, 7 * (g.n + 1))
                    if g.after(1):
                        act.wait_ge(q_s, g.n)
                    act.activation(t_e[:, :, :], vc_e[:, g.slot, :, :], ACT.Square).then_inc(q_sq, 1)

            run_chunks(act, sums_pass, 2, 4, 2)
            act.sem_inc(r_start, 1)
            act.wait_ge(r_start, 4)

            def messages(c):
                b, m, g, h = c.back(1), c.back(2), c.back(3), c.back(4)
                if c.real():
                    k = (CH - 1) - c.n
                    if c.after(2):
                        act.wait_ge(r_tm, c.n - 1)
                    act.activation(m_in[:, c.two, :, D:P],
                                   x_all[:, bass.ds(k * (2 * EF) + EF, EF)].rearrange("p (t f) -> p t f", f=D),
                                   ACT.Copy).then_inc(r_md, 1)
                if m.real():
                    act.wait_ge(r_h, m.n + 1)
                    if m.after(1):
                        act.wait_ge(r_mm, m.n)
                    act.activation(hT, ps[0:HM, 3, :], ACT.Gelu, bias=bm1[:, 0:1]).then_inc(r_hg, 1)
                if g.real():
                    act.wait_ge(r_c, g.n + 1)
                    if g.after(1):
                        act.wait_ge(r_o, g.n)
                    act.activation(c2T[0:HC, :], ps[0:HC, 5, :], ACT.Gelu, bias=bc1[:, 0:1]).then_inc(r_cg, 1)
                if m.real():
                    act.wait_ge(r_mm, m.n + 1)
                    if m.after(2):
                        act.wait_ge(r_box, m.n - 1)
                    act.activation(mT[m.two], ps[0:D, 4, :], ACT.Gelu, bias=bm2[:, 0:1]).then_inc(r_mg, 1)
                if b.real():
                    act.wait_ge(r_tm, b.n + 1)
                    if b.after(4):
                        act.wait_ge(r_o, b.n - 3)
                        act.wait_ge(r_box, b.n - 2)
                    act.activation(xin[b.slot][0:D, :], ps[0:D, 0, :], ACT.Copy).then_inc(r_xs, 1)
                    act.activation(mask_m[b.slot], ps[:, 1, :], ACT.Copy).then_inc(r_xs, 1)
                    if b.after(2):
                        act.wait_ge(r_h, b.n - 1)
                    act.activation(eT[b.two], ps[0:DE, 2, :], ACT.Copy).then_inc(r_xs, 1)
                if h.real():
                    act.wait_ge(r_z, 4 * (h.n + 1))
                    if h.after(1):
                        act.wait_ge(r_s, h.n)
                    act.activation(sq_e, zc_e[h.two], ACT.Square).then_inc(r_sq, 1)
                if g.real():
                    act.wait_ge(r_o, g.n + 1)
                    if g.after(2):
                        act.wait_ge(r_z, 4 * (g.n - 1))
                    act.activation(comb_e[g.two], ps[:, 6 + g.two, 0:EF].rearrange("p (t f) -> p t f", f=D), ACT.Gelu
                                   ).then_inc(r_og, 1)

            run_chunks(act, messages, 4, 8, 4)

        @block.tensor
        def _(pe):
            pe.wait_ge(s_ones, 3)
            pe.wait_ge(s_consts, 4)
            pe.wait_ge(s_ucount, 1)
            pe.matmul(ps_u, usum, ones_f[0:ROWS, :], start=True, stop=True).then_inc(s_iT, 1)
            pe.wait_ge(s_hidx, 2)
            for a in range(2):
                for h in range(2):
                    mm = pe.transpose(ps_i[:, 4, a, h, :], rows[:, 6 + a, h * P:(h + 1) * P],
                                      ident[0:ROWS, 0:ROWS])
            mm.then_inc(s_iT, 1)

            def hist_tile(turn, slot, first, last):
                pe.wait_ge(s_onehot, 2 * (4 * turn + slot + 1))
                for b in range(2):
                    half = CH * J // 2
                    mm = pe.matmul(hist[:, b, :], ha[slot], hb[slot][:, b * half:(b + 1) * half],
                                   start=first, stop=last)
                mm.then_inc(s_hist, 1)

            for slot in range(4):
                hist_tile(0, slot, slot == 0, False)
            with pe.Fori(1, EARLY) as turn:
                for slot in range(4):
                    hist_tile(turn, slot, False, False)

            pe.wait_ge(s_ri, 4)
            pe.wait_ge(s_idx, 2)
            for a in range(6):
                for h in range(2):
                    mm = pe.transpose(ps_i[:, a // 2, a % 2, h, :], rows[:, a, h * P:(h + 1) * P],
                                      ident[0:ROWS, 0:ROWS])
            mm.then_inc(s_iT, 1)
            pe.wait_ge(s_idx, 3)
            pe.matmul(ps_flip, flip[:, :], sq[:, 0, 0:TILES], start=True, stop=True).then_inc(s_iT, 1)

            with pe.Fori(EARLY, TILES // 4 - 1) as turn:
                for slot in range(4):
                    hist_tile(turn, slot, False, False)
            for slot in range(4):
                hist_tile(TILES // 4 - 1, slot, False, slot == 3)

            pe.wait_ge(s_weights, 16 * 14)
            pe.wait_ge(s_centre, 4)

            def dense(c):
                n, b = c.back(2), c.back(3)
                if n.real():
                    s = n.two
                    pe.wait_ge(d_x1, n.n + 1)
                    if n.after(1):
                        pe.wait_ge(d_og, n.n)
                    for i in range(2):
                        for k in range(4 * i, 4 * i + 4):
                            mm = pe.transpose(ps_xT[:, i, (k % 4) * P:(k % 4 + 1) * P],
                                              x_in[:, n.slot, k * P:(k + 1) * P], ident[:, :])
                        mm.then_inc(d_T, 1)
                    for q in range(4):
                        i, half = divmod(q, 2)
                        pe.wait_ge(d_Ts, 2 * n.n + i + 1)
                        if q >= 2 or n.after(1):
                            pe.wait_ge(d_cg, 4 * n.n + q - 1)
                        pe.matmul(ps[0:HC, 2 + half, :], wx_d[half * D:(half + 1) * D, :],
                                  xT[half * D:(half + 1) * D, s, i * 512:(i + 1) * 512],
                                  start=True, stop=True).then_inc(d_c, 1)
                    for q in range(4):
                        i, half = divmod(q, 2)
                        pe.wait_ge(d_cg, 4 * n.n + q + 1)
                        mm = pe.matmul(ps[half * D:(half + 1) * D, i, :], wc2[0:HC, :],
                                       cT[0:HC, half * FREE + i * 512:half * FREE + (i + 1) * 512],
                                       start=True, stop=True)
                    mm.then_inc(d_o, 1)
                if b.real():
                    s = b.two
                    pe.wait_ge(d_zT, b.n + 1)
                    if b.after(2):
                        pe.wait_ge(d_out, b.n - 1)
                    for k in range(J // 2):
                        mm = pe.matmul(ps_z[s][:, k * P:(k + 1) * P], zT[:, s, k * P:(k + 1) * P], centre[:, :],
                                       start=True, stop=True)
                    mm.then_inc(d_z, 1)

            run_chunks(pe, dense, 4, 8, 3)

            pe.wait_ge(d_og, CH)
            pe.wait_ge(d_out, CH)

            def sums_pass(c):
                b = c.back(1)
                if c.real():
                    pe.wait_ge(q_w, 2 * (c.n + 1))
                    if c.after(2):
                        pe.wait_ge(q_f, c.n - 1)
                    settled(pe)
                    for t in range(TPC):
                        pe.transpose(ps_w[c.slot][:, t * P:(t + 1) * P], w_x[:, c.slot, t, :], ident[:, :])
                    pe.matmul(ps_mask[c.slot], ones_b[:, 0:D],
                              mask_rhs[:, c.slot, :, :].rearrange("p t e -> p (t e)"),
                              start=True, stop=True).then_inc(q_wT, 1)
                if b.real():
                    pe.wait_ge(q_f, b.n + 1)
                    if b.after(2):
                        pe.wait_ge(q_v, 7 * (b.n - 1))
                    settled(pe)
                    for t in range(TPC):
                        mm = pe.transpose(ps_ag[b.slot][:, t * D:(t + 1) * D], fsum[:, b.slot, t * P:(t + 1) * P],
                                          ident[0:D, 0:D])
                    mm.then_inc(q_fT, 1)

            run_chunks(pe, sums_pass, 2, 4, 1)
            pe.sem_inc(r_start, 1)
            pe.wait_ge(r_start, 4)

            def messages(c):
                b, m, g = c.back(1), c.back(2), c.back(3)
                if m.real():
                    pe.wait_ge(r_xs, 3 * (m.n + 1))
                    pe.wait_ge(r_xd, m.n + 1)
                    if m.after(1):
                        pe.wait_ge(r_hg, m.n)
                    pe.matmul(ps[0:HM, 3, :], wm1[:, :], xin[m.slot], start=True, stop=False)
                    pe.matmul(ps[0:HM, 3, :], wme[:, :], eT[m.two], start=False, stop=True).then_inc(r_h, 1)
                if g.real():
                    pe.wait_ge(r_box, g.n + 1)
                    if g.after(1):
                        pe.wait_ge(r_cg, g.n)
                    pe.matmul(ps[0:HC, 5, :], wc1[:, :], xin[g.slot], start=True, stop=True).then_inc(r_c, 1)
                if m.real():
                    pe.wait_ge(r_hg, m.n + 1)
                    if m.after(1):
                        pe.wait_ge(r_mg, m.n)
                    pe.matmul(ps[0:D, 4, :], wm2[:, :], hT, start=True, stop=True).then_inc(r_mm, 1)
                if b.real():
                    pe.wait_ge(r_m, b.n + 1)
                    pe.wait_ge(r_md, b.n + 1)
                    pe.wait_ge(r_ga[b.two], 64 * (b.uses + 1))
                    pe.wait_ge(r_e[b.two], 16 * (b.uses + 1))
                    if b.after(1):
                        pe.wait_ge(r_xs, 3 * b.n)
                        pe.wait_ge(r_xd, b.n)
                    for t in range(TPC):
                        u = TPC - 1 - t
                        pe.matmul(ps[:, 0, t * P:(t + 1) * P], m_in[:, b.two, u, :], flip[:, :],
                                  start=True, stop=True)
                    pe.matmul(ps[:, 1, :], ones_b[:, :], mask_rhs[:, b.two, :, :].rearrange("p t e -> p (t e)"),
                              start=True, stop=True)
                    for t in range(TPC):
                        u = TPC - 1 - t
                        mm = pe.matmul(ps[0:DE, 2, t * P:(t + 1) * P], eattr[:, b.two, u, :], flip[:, :],
                                       start=True, stop=True)
                    mm.then_inc(r_tm, 1)
                if g.real():
                    pe.wait_ge(r_cg, g.n + 1)
                    if g.after(2):
                        pe.wait_ge(r_z, 4 * (g.n - 2) + 1)
                    for t in range(TPC):
                        pe.matmul(ps[:, 6 + g.two, t * D:(t + 1) * D], c2T[:, t * P:(t + 1) * P], wc2[:, :],
                                  start=True, stop=True)
                        mm = pe.matmul(ps[:, 6 + g.two, EF + t * D:EF + (t + 1) * D], xin[g.slot][D:P, t * P:(t + 1) * P],
                                       ident[D:P, D:P], start=True, stop=True)
                    mm.then_inc(r_o, 1)

            run_chunks(pe, messages, 4, 8, 3)

        @block.vector
        def _(dve):
            def then(ins, sem_, value):
                ins.then_inc(sem_, 1)
                dve.wait_ge(sem_, value)

            def newton(y, v, tmp, sem_, base):
                then(dve.scalar_tensor_tensor(tmp, y, -0.5, y, ALU.mult, ALU.mult), sem_, base + 1)
                then(dve.tensor_tensor(tmp, tmp, v, ALU.mult), sem_, base + 2)
                then(dve.scalar_tensor_tensor(y, tmp, 1.5, y, ALU.add, ALU.mult), sem_, base + 3)

            def rsqrt_step(k, y, v, tmp, sem_, base):
                if k > 1:
                    dve.wait_ge(sem_, base + k - 1)
                yi = y.bitcast(I32)
                if k == 1:
                    ins = dve.tensor_scalar(yi, v.bitcast(I32), 1, None, ALU.arith_shift_right)
                elif k == 2:
                    ins = dve.tensor_scalar(yi, yi, -1.0, float(0x5F3759DF), ALU.mult, ALU.add)
                elif k % 3 == 0:
                    ins = dve.scalar_tensor_tensor(tmp, y, -0.5, y, ALU.mult, ALU.mult)
                elif k % 3 == 1:
                    ins = dve.tensor_tensor(tmp, tmp, v, ALU.mult)
                else:
                    ins = dve.scalar_tensor_tensor(y, tmp, 1.5, y, ALU.add, ALU.mult)
                ins.then_inc(sem_, 1)

            dve.memset(mask[:, :], 0.0).then_inc(s_zeros, 1)
            dve.memset(sort_i[0:1, 0:1], -1).then_inc(s_guard, 1)
            dve.memset(sort_i[0:1, 1:2], 2 * OFF).then_inc(s_guard, 1)
            dve.memset(sort_s, OFF).then_inc(s_guard, 1)
            dve.memset(rsrc, OFF).then_inc(s_hfill, 1)
            dve.memset(ones_b[:, :], 1.0).then_inc(s_ones, 1)
            dve.memset(ones_f[:, :], 1.0).then_inc(s_ones, 1)
            dve.memset(dvar[:, :], 1.0).then_inc(s_ones, 1)
            then(dve.memset(centre[:, :], 0.0), s_centre, 1)
            dve.memset(centre[0:D, 0:D], -1.0 / D).then_inc(s_centre, 1)
            then(dve.memset(centre[D:P, D:P], -1.0 / D), s_centre, 3)

            dve.wait_ge(s_win, 16)
            dve.tensor_tensor(rows[:, 0, :], rwin[:, 1:RE + 1], rwin[:, 2:RE + 2], ALU.is_gt).then_inc(s_rank, 1)
            dve.wait_ge(s_rank, 1)
            dve.tensor_reduce(usum, rows[:, 0, :], AX.X, ALU.add).then_inc(s_ucount, 1)
            dve.wait_ge(s_hsrc, 32)
            dve.tensor_scalar(rtmp, rsrc, 4, P - 1, ALU.arith_shift_right, ALU.bitwise_and).then_inc(s_rank, 1)
            dve.tensor_scalar(rtm2, rsrc, J - 1, None, ALU.bitwise_and).then_inc(s_rank, 1)
            dve.wait_ge(s_rank, 3)
            dve.tensor_scalar(rsrc, rsrc, 11, 4, ALU.arith_shift_right, ALU.logical_shift_left).then_inc(s_rank, 1)
            dve.wait_ge(s_rank, 4)
            dve.tensor_tensor(rows[:, 7, :], rsrc, rtm2, ALU.add).then_inc(s_hidx, 1)
            dve.tensor_copy(rows[:, 6, :], rtmp).then_inc(s_hidx, 1)
            dve.wait_ge(s_iT, 1)
            dve.tensor_scalar(flag[:, :], ps_u, 1.0, None, ALU.min).then_inc(s_flag, 1)
            dve.wait_ge(s_flag, 1)
            unsorted = dve.value_load(flag[0:1, 0:1], min_val=0, max_val=1)
            with dve.If(unsorted == 1):
                dve.wait_ge(s_lower, 1)
                dve.wait_ge(s_keyf, 1)
                dve.wait_ge(s_keys, 32)
                then(dve.tensor_copy(dst_ef, dst_e), s_ranked, 1)
                with dve.Fori(0, TILES) as t:
                    mine = dst_ef[:, bass.ds(t, 1)]
                    for g in range(SEG):
                        n = EP // SEG
                        dve.tensor_scalar(seg_out, keys[:, g * n:(g + 1) * n], mine, 0.0, ALU.is_lt, ALU.add,
                                          accum_out=seg_n[:, g:g + 1]).then_inc(s_rank, 1)
                        dve.wait_ge(s_rank, 4 + t * (SEG + 5) + g + 1)
                    tile_keys = keys[:, bass.ds(t * P, P)]
                    base = 4 + t * (SEG + 5) + SEG
                    then(dve.tensor_scalar(eq_t, tile_keys, mine, None, ALU.is_equal), s_rank, base + 1)
                    then(dve.tensor_tensor(eq_t, eq_t, lower, ALU.mult), s_rank, base + 2)
                    then(dve.tensor_reduce(seg_n[:, SEG:SEG + 1], eq_t, AX.X, ALU.add), s_rank, base + 3)
                    then(dve.tensor_reduce(pos_f[:, bass.ds(t, 1)], seg_n, AX.X, ALU.add), s_rank, base + 4)
                    then(dve.tensor_scalar(tile_keys, tile_keys, -0.5, None, ALU.add), s_rank, base + 5)
                then(dve.tensor_copy(pos_i, pos_f), s_ranked, 2)

            dve.wait_ge(s_iota, 2)
            dve.wait_ge(s_iT, 2)
            dve.tensor_copy(hp[:, :].rearrange("p (q h) -> p h q", h=2), ps_i[:, 4, 0, :, :]).then_inc(s_idx, 1)
            dve.tensor_copy(hcol[:, :].rearrange("p (q h) -> p h q", h=2), ps_i[:, 4, 1, :, :]).then_inc(s_idx, 1)
            dve.wait_ge(s_idx, 2)

            def onehots(turn, slot, wait):
                t = 4 * turn + slot
                if wait:
                    dve.wait_ge(s_hist, t - 3)
                dve.tensor_scalar(ha[slot], iota_p[:, :], hp[:, bass.ds(t, 1)], None, ALU.is_equal
                                  ).then_inc(s_onehot, 1)
                dve.tensor_scalar(hb[slot], iota_c, hcol[:, bass.ds(t, 1)], None, ALU.is_equal
                                  ).then_inc(s_onehot, 1)

            for slot in range(4):
                onehots(0, slot, False)
            with dve.Fori(1, EARLY) as turn:
                for slot in range(4):
                    onehots(turn, slot, True)

            dve.wait_ge(s_rows, 32)
            here, prev, nxt = rwin[:, 1:RE + 1], rwin[:, 0:RE], rwin[:, 2:RE + 2]
            dve.tensor_copy(rows[:, 0, :], rsorted)
            dve.tensor_scalar(rows[:, 1, :], here, float(N - 1), None, ALU.min)
            then(dve.tensor_tensor(rows[:, 4, :], here, prev, ALU.is_equal), s_ri, 1)
            then(dve.tensor_tensor(rows[:, 5, :], here, nxt, ALU.is_equal), s_ri, 2)
            dve.scalar_tensor_tensor(rows[:, 2, :], rows[:, 5, :], float(OFF), here, ALU.mult, ALU.add
                                     ).then_inc(s_ri, 1)
            dve.scalar_tensor_tensor(rows[:, 3, :], rows[:, 4, :], float(OFF), here, ALU.mult, ALU.add
                                     ).then_inc(s_ri, 1)
            dve.wait_ge(s_iT, 3)
            by_tile = lambda a: ps_i[:, a // 2, a % 2, :, :]
            qh = lambda a: a.rearrange("p (q h) -> p h q", h=2)
            dve.tensor_copy(qh(sq[:, 0, 0:TILES]), by_tile(3)).then_inc(s_idx, 1)
            four = idx[:, :, :].rearrange("p (k2 x) (a i) -> p k2 x a i", x=1, i=TPC)
            for a in range(3):
                for h in range(2):
                    dve.tensor_copy(
                        four[:, :, 0, a, h::2],
                        ps_i[:, a // 2, a % 2, h, :].rearrange("p (k i) -> p k i", i=2)).then_inc(s_idx, 1)
            dve.tensor_copy(qh(same_prev[:, :]), by_tile(4)).then_inc(s_idx, 1)
            dve.tensor_copy(qh(same_next[:, :]), by_tile(5)).then_inc(s_idx, 1)
            dve.wait_ge(s_idx, 11)
            dve.tensor_scalar(is_last[:, :], same_next[:, :], -1.0, 1.0, ALU.mult, ALU.add).then_inc(s_idx, 1)
            dve.wait_ge(s_iT, 4)
            dve.tensor_copy(four[:, :, 0, 3, :], ps_flip.rearrange("p (k i) -> p k i", i=TPC)).then_inc(s_idx, 1)

            with dve.Fori(EARLY, TILES // 4) as turn:
                for slot in range(4):
                    onehots(turn, slot, True)
            deg, root = zT[:, 0, 0:CH * J], zT[:, 1, 0:CH * J]
            dve.wait_ge(s_hist, TILES)
            dve.tensor_scalar(deg.rearrange("p (a b) -> p a b", a=2), hist, 1.0, None, ALU.add).then_inc(s_deg, 1)
            dve.wait_ge(s_root, 1)
            then(dve.reciprocal(dinv[:, :], root), s_deg, 2)
            newton(dinv[:, :], deg, root, s_deg, 2)
            dve.sem_inc(s_dinv, 1)
            a1, r1 = zT[:, 0, 0:CH * J], zT[:, 1, 0:CH * J]
            then(dve.tensor_tensor(a1, dinv[:, :], dinv[:, :], ALU.mult), s_scale, 1)
            then(dve.tensor_scalar(a1, a1, 1.0, None, ALU.add), s_scale, 2)
            then(dve.tensor_tensor(a1, a1, a1, ALU.mult), s_scale, 3)
            then(dve.reciprocal(r1, a1), s_scale, 4)
            then(dve.tensor_scalar(eps_a[:, :], r1, EPS, None, ALU.mult), s_scale, 5)
            dve.memset(cT[HC:HC + 1, 0:EC], 1.0).then_inc(s_biasrow, 1)
            dve.wait_ge(s_consts, 4)
            dve.tensor_tensor(centre[:, :], centre[:, :], ident[:, :], ALU.add).then_inc(s_centre, 1)

            def dense(c):
                a, b, g, h = c.back(1), c.back(3), c.back(4), c.back(5)
                chain = a.real() or h.real()
                rstd = drstd[:, a.two, :]

                def root_step(k):
                    if chain:
                        rsqrt_step(k, rstd, dvar[:, :], dnw[:, :], d_pow, 11 * a.n)

                if a.real():
                    dve.wait_ge(d_s1, a.n + 1)
                    dve.scalar_tensor_tensor(dvar[:, 0:J], dsum[:, 1, :], 1.0 / D, eps_a[:, bass.ds(a.n * J, J)],
                                             ALU.mult, ALU.add).then_inc(d_v1, 1)
                if h.real():
                    dve.wait_ge(d_s2, h.n + 1)
                    dve.tensor_scalar(dvar[:, J:2 * J], dsum[:, 2, :], 1.0 / D, EPS, ALU.mult, ALU.add
                                      ).then_inc(d_v2, 1)
                if c.real():
                    dve.wait_ge(d_x[c.slot], 16 * (c.turn + 1))
                    x3 = col3(x_in[:, c.slot, :])
                    dve.tensor_reduce(dsum[:, 0, :], x3, AX.X, ALU.add).then_inc(d_m, 1)
                if a.real():
                    dve.wait_ge(d_v1, a.n + 1)
                if h.real():
                    dve.wait_ge(d_v2, h.n + 1)
                root_step(1)
                if c.real():
                    dve.wait_ge(d_m, 2 * c.n + 1)
                    dve.tensor_scalar(dsum[:, 0, :], dsum[:, 0, :], 1.0 / D, None, ALU.mult).then_inc(d_m, 1)
                root_step(2)
                if b.real():
                    s = b.two
                    dve.wait_ge(d_og, b.n + 1)
                    dve.scalar_tensor_tensor(zT[:, s, :], xT[:, s, :], 2.0, zT[:, s, :], ALU.mult, ALU.add
                                             ).then_inc(d_zT, 1)
                root_step(3)
                if c.real():
                    dve.wait_ge(d_m, 2 * (c.n + 1))
                    dve.tensor_tensor(x3, x3, wide(dsum[:, 0, :], J, D), ALU.subtract).then_inc(d_xc, 1)
                root_step(4)
                root_step(5)
                if g.real():
                    dve.wait_ge(d_sq2, g.n + 1)
                    dve.tensor_reduce(dsum[:, 2, :], col3(sq[:, 1, :]), AX.X, ALU.add).then_inc(d_s2, 1)
                for k in range(6, 12):
                    root_step(k)
                if a.real():
                    dve.wait_ge(d_pow, 11 * (a.n + 1))
                    dve.wait_ge(d_sq1, a.n + 1)
                    xa = col3(x_in[:, a.slot, :])
                    dve.tensor_tensor(xa, xa, wide(rstd[:, 0:J], J, D), ALU.mult).then_inc(d_x1, 1)
                if h.real():
                    s = h.two
                    dve.wait_ge(d_pow, 11 * (a.n + 1))
                    dve.wait_ge(d_sq2, h.n + 1)
                    if h.after(2):
                        dve.wait_ge(d_st[s], 16 * h.uses)
                    dve.tensor_tensor(col3(outb[:, s, :]), col3(ps_z[s]), wide(rstd[:, J:2 * J], J, D), ALU.mult
                                      ).then_inc(d_out, 1)
                if c.real():
                    dve.wait_ge(d_sq1, c.n + 1)
                    dve.tensor_reduce(dsum[:, 1, :], col3(sq[:, 0, :]), AX.X, ALU.add).then_inc(d_s1, 1)

            run_chunks(dve, dense, 4, 8, 5)

            tile4 = lambda a: a.rearrange("p (t f) -> p t f", t=TPC)
            evar, erstd, enw = sm[:, 16:16 + TPC], sm[:, 20:28], sm[:, 28:28 + TPC]
            esum = sm[:, 12:12 + TPC]

            def spread_factors(c, k, eye, same, reverse):
                for t in range(TPC):
                    u = TPC - 1 - t if reverse else t
                    ins = dve.tensor_scalar(mask_rhs[:, c.two, t, :], eye[:, :], same[:, bass.ds(k * TPC + u, 1)],
                                            None, ALU.mult)
                return ins

            def sums_pass(c):
                b, g, h = c.back(1), c.back(2), c.back(3)
                s = h.slot
                rstd = erstd[:, s * TPC:(s + 1) * TPC]
                if g.real():
                    dcol = d_all[:, bass.ds(g.n * (2 * TPC) + TPC, TPC)]
                    xd = tile4(x_all[:, bass.ds(g.n * (2 * EF) + EF, EF)])

                def root_step(k):
                    if h.real():
                        rsqrt_step(k, rstd, evar, enw, q_pow, 11 * h.n)

                if h.real():
                    dve.wait_ge(q_s, h.n + 1)
                    dve.tensor_scalar(evar, esum, 1.0 / D, EPS, ALU.mult, ALU.add).then_inc(q_var, 1)
                if c.real():
                    dve.wait_ge(g_xk[c.slot], 16 * (c.turn + 1))
                    dve.wait_ge(g_dk[c.slot], 16 * (c.turn + 1))
                    if c.after(2):
                        dve.wait_ge(q_wT, c.n - 1)
                    dve.tensor_tensor(w_x[:, c.slot, :, :], tile4(x_all[:, bass.ds(c.n * (2 * EF), EF)]),
                                      wide(d_all[:, bass.ds(c.n * (2 * TPC), TPC)], TPC, D), ALU.mult).then_inc(q_w, 1)
                if h.real():
                    dve.wait_ge(q_var, h.n + 1)
                root_step(1)
                if c.real():
                    spread_factors(c, c.n, ident_b, same_prev, False).then_inc(q_w, 1)
                root_step(2)
                q = 7 * g.n
                if g.real():
                    dve.tensor_tensor(sm[:, 4:8], dcol, dcol, ALU.mult).then_inc(q_v, 1)
                root_step(3)
                if g.real():
                    dve.wait_ge(q_fT, g.n + 1)
                    dve.wait_ge(q_v, q + 1)
                    dve.scalar_tensor_tensor(v_e[:, :, :], wide(sm[:, 4:8], TPC, D), 1.0, xd, ALU.add, ALU.mult
                                             ).then_inc(q_v, 1)
                root_step(4)
                if g.real():
                    dve.wait_ge(q_v, q + 2)
                    dve.tensor_tensor(ag_e[:, :, :], tile4(ps_ag[g.slot]), wide(dcol, TPC, D), ALU.mult
                                      ).then_inc(q_v, 1)
                root_step(5)
                if b.real():
                    dve.wait_ge(q_wT, b.n + 1)
                    dve.wait_ge(q_mask, b.n + 1)
                    if b.after(2):
                        dve.wait_ge(q_fT, b.n - 1)
                    if b.after(1):
                        dve.wait_ge(q_f, b.n)
                        carry = fsum[:, 1 - b.slot, EC - 1:EC]
                    else:
                        carry = 0.0
                    dve.tensor_tensor_scan(fsum[:, b.slot, :], mask[0:D, :], ps_w[b.slot], carry, ALU.mult, ALU.add
                                           ).then_inc(q_f, 1)
                root_step(6)
                if g.real():
                    dve.wait_ge(q_v, q + 3)
                    dve.tensor_tensor(v_e[:, :, :], v_e[:, :, :], ag_e[:, :, :], ALU.add).then_inc(q_v, 1)
                root_step(7)
                if g.real():
                    dve.wait_ge(q_v, q + 4)
                    dve.tensor_reduce(sm[:, 8:12], v_e[:, :, :], AX.X, ALU.add).then_inc(q_v, 1)
                root_step(8)
                if g.real():
                    dve.wait_ge(q_v, q + 5)
                    dve.tensor_scalar(sm[:, 8:12], sm[:, 8:12], 1.0 / D, None, ALU.mult).then_inc(q_v, 1)
                root_step(9)
                if g.real():
                    dve.wait_ge(q_v, q + 6)
                    dve.tensor_tensor(vc_e[:, g.slot, :, :], v_e[:, :, :], wide(sm[:, 8:12], TPC, D), ALU.subtract
                                      ).then_inc(q_v, 1)
                root_step(10)
                root_step(11)
                if h.real():
                    dve.wait_ge(q_pow, 11 * (h.n + 1))
                    then(dve.tensor_tensor(sm[:, 0:TPC], rstd, is_last[:, bass.ds(h.n * TPC, TPC)], ALU.mult),
                         q_xd, 2 * h.n + 1)
                    dve.wait_ge(q_v, 7 * (h.n + 1))
                    dve.tensor_tensor(tile4(x_all[:, bass.ds(h.n * (2 * EF) + EF, EF)]), vc_e[:, s, :, :],
                                      wide(sm[:, 0:TPC], TPC, D), ALU.mult).then_inc(q_xd, 1)
                if g.real():
                    dve.wait_ge(q_sq, g.n + 1)
                    dve.tensor_reduce(esum, t_e[:, :, :], AX.X, ALU.add).then_inc(q_s, 1)

            run_chunks(dve, sums_pass, 2, 4, 3)
            dve.sem_inc(r_start, 1)
            dve.wait_ge(r_start, 4)

            def messages(c):
                b, g, h, l = c.back(1), c.back(3), c.back(4), c.back(5)
                k = (CH - 1) - c.n
                rstd = erstd[:, l.two * TPC:(l.two + 1) * TPC]
                q = 4 * h.n
                z = zc_e[h.two]

                def root_step(i):
                    if l.real():
                        rsqrt_step(i, rstd, evar, enw, r_pow, 11 * l.n)

                if g.real():
                    dve.wait_ge(r_mg, g.n + 1)
                    dve.wait_ge(r_xs, 3 * (g.n + 1))
                    dve.wait_ge(r_h, g.n + 1)
                    if g.after(1):
                        dve.wait_ge(r_box, g.n)
                        carry = xin[g.back(1).slot][0:D, EC - 1:EC]
                    else:
                        carry = 0.0
                    dve.tensor_tensor_scan(xin[g.slot][0:D, :], mask_m[g.slot][0:D, :], mT[g.two], carry,
                                           ALU.mult, ALU.add).then_inc(r_box, 1)
                if l.real():
                    dve.wait_ge(r_s, l.n + 1)
                    dve.tensor_scalar(evar, esum, 1.0 / D, EPS, ALU.mult, ALU.add).then_inc(r_var, 1)
                if h.real():
                    dve.wait_ge(r_og, h.n + 1)
                    if h.after(2):
                        dve.wait_ge(r_out, h.n - 1)
                    dve.scalar_tensor_tensor(z, tile4(ps[:, 6 + h.two, EF:2 * EF]), 2.0, comb_e[h.two],
                                             ALU.mult, ALU.add).then_inc(r_z, 1)
                if l.real():
                    dve.wait_ge(r_var, l.n + 1)
                root_step(1)
                if c.real():
                    if c.after(2):
                        dve.wait_ge(r_tm, c.n - 1)
                    settled(dve)
                    spread_factors(c, k, flip_b, same_next, True).then_inc(r_m, 1)
                root_step(2)
                if h.real():
                    dve.wait_ge(r_z, q + 1)
                    dve.tensor_reduce(sm[:, 8:12], z, AX.X, ALU.add).then_inc(r_z, 1)
                root_step(3)
                root_step(4)
                if h.real():
                    dve.wait_ge(r_z, q + 2)
                    dve.tensor_scalar(sm[:, 8:12], sm[:, 8:12], 1.0 / D, None, ALU.mult).then_inc(r_z, 1)
                root_step(5)
                root_step(6)
                if h.real():
                    dve.wait_ge(r_z, q + 3)
                    dve.tensor_tensor(z, z, wide(sm[:, 8:12], TPC, D), ALU.subtract).then_inc(r_z, 1)
                root_step(7)
                root_step(8)
                if b.real():
                    dve.wait_ge(r_tm, b.n + 1)
                    dve.wait_ge(r_xs, 3 * b.n + 2)
                    if b.after(4):
                        dve.wait_ge(r_o, b.n - 3)
                    if b.after(1):
                        dve.wait_ge(r_xd, b.n)
                        carry = xin[b.back(1).slot][D:P, EC - 1:EC]
                    else:
                        carry = 0.0
                    dve.tensor_tensor_scan(xin[b.slot][D:P, :], mask_m[b.slot][D:P, :], ps[D:P, 0, :], carry,
                                           ALU.mult, ALU.add).then_inc(r_xd, 1)
                root_step(9)
                root_step(10)
                root_step(11)
                if l.real():
                    dve.wait_ge(r_pow, 11 * (l.n + 1))
                    if l.after(2):
                        dve.wait_ge(r_sc[l.two], 64 * l.uses)
                    dve.tensor_tensor(tile4(out_e[l.two]), zc_e[l.two], wide(rstd, TPC, D), ALU.mult
                                      ).then_inc(r_out, 1)
                if h.real():
                    dve.wait_ge(r_sq, h.n + 1)
                    dve.tensor_reduce(esum, sq_e, AX.X, ALU.add).then_inc(r_s, 1)

            run_chunks(dve, messages, 4, 8, 5)

        @block.gpsimd
        def _(pool):
            pool.memset(ident[:, :], 1.0).then_inc(s_stage, 1)
            pool.memset(flip[:, :], 1.0).then_inc(s_stage, 1)
            pool.memset(lower, 1.0).then_inc(s_stage, 1)
            pool.iota(iota_p[:, :], [[1, P]], base=0, channel_multiplier=0,
                      allow_small_or_imprecise_dtypes=True).then_inc(s_iota, 1)
            pool.iota(iota_c, [[1, CH * J]], base=0, channel_multiplier=0,
                      allow_small_or_imprecise_dtypes=True).then_inc(s_iota, 1)
            pool.wait_ge(s_stage, 3)
            pool.affine_select(ident[:, :], ident[:, :], [[-1, P]], ALU.is_equal, 0.0, base=0,
                               channel_multiplier=1).then_inc(s_consts, 1)
            pool.affine_select(flip[:, :], flip[:, :], [[1, P]], ALU.is_equal, 0.0, base=-(P - 1),
                               channel_multiplier=1).then_inc(s_consts, 1)
            pool.affine_select(lower, lower, [[-1, P]], ALU.is_gt, 0.0, base=0,
                               channel_multiplier=1).then_inc(s_lower, 1)
            pool.wait_ge(s_consts, 2)
            pool.tensor_copy(ident_b[:, :], ident[:, :]).then_inc(s_consts, 1)
            pool.tensor_copy(flip_b[:, :], flip[:, :]).then_inc(s_consts, 1)

            pool.wait_ge(s_flag, 1)
            unsorted = pool.value_load(flag[0:1, 0:1], min_val=0, max_val=1)
            with pool.If(unsorted == 1):
                key_row = dsts[GUARD, :].rearrange("n a -> (n a)")
                pool.dma_start(keys.bitcast(I32), key_row.partition_broadcast(P)).then_inc(s_perm, 16)
                for half in range(2):
                    t0 = half * ROWS
                    pool.dma_start(dst_e[:, t0:t0 + ROWS],
                                   dsts[1 + t0 * P:1 + (t0 + ROWS) * P, :].rearrange("(t p) a -> p (t a)", p=P),
                                   allow_slow_non_contiguous=True).then_inc(s_keys, 16)
                pool.wait_ge(s_perm, 16)
                pool.tensor_copy(keys, keys.bitcast(I32)).then_inc(s_keyf, 1)
                pool.wait_ge(s_ranked, 2)
                with pool.Fori(0, TILES) as t:
                    pool.dma_start(sort_s, srcs[bass.ds(t * P, P), :]).then_inc(s_tile, 16)
                    pool.dma_start(sort_e, attrs[bass.ds(t * P, P), :]).then_inc(s_tile, 16)
                    pool.tensor_copy(sort_i[:, 0:1], pos_i[:, bass.ds(t, 1)]).then_inc(s_stage, 1)
                    pool.tensor_copy(sort_i[:, 1:2], dst_e[:, bass.ds(t, 1)]).then_inc(s_stage, 1)
                    pool.wait_ge(s_tile, 32 * (t + 1))
                    pool.wait_ge(s_stage, 3 + 2 * (t + 1))
                    at = bass.IndirectOffsetOnAxis(ap=sort_i[:, 0:1], axis=0)
                    settled(pool)
                    pool.indirect_dma_start(src_perm, at, sort_s, None).then_inc(s_perm, 16)
                    pool.indirect_dma_start(dst_perm, at, sort_i[:, 1:2], None).then_inc(s_perm, 16)
                    pool.indirect_dma_start(attr_perm, at, sort_e, None).then_inc(s_perm, 16)
                    pool.wait_ge(s_perm, 16 + 48 * (t + 1))
                pool.dma_start(srcs, src_perm).then_inc(s_back, 16)
                pool.dma_start(dsts[GUARD, :], dst_perm).then_inc(s_back, 16)
                pool.dma_start(attrs, attr_perm).then_inc(s_back, 16)
                pool.wait_ge(s_back, 48)
            pool.sem_inc(s_sorted, 1)

            pool.wait_ge(s_idx, 13)

            def stage(use, c, first, width, staged):
                settled(pool)
                pool.tensor_copy(istage[:, use, c.slot, 0:width],
                                 idx[:, bass.ds(c.n, 1), first:first + width].rearrange("p a b -> p (a b)")
                                 ).then_inc(staged, 1)

            def gather_both(use, c, staged, landed, kept, source, place):
                nxt, prev = c.back(-1), c.back(1)
                pool.wait_ge(staged, c.n + 1)
                if c.after(2):
                    pool.wait_ge(kept[c.slot], 16 * c.turn)
                settled(pool)
                for i in range(2 * TPC):
                    if i == TPC and nxt.real():
                        if c.after(1):
                            pool.wait_ge(landed[prev.slot], 128 * (prev.turn + 1))
                        stage(use, nxt, 0, 2 * TPC, staged)
                    at = bass.IndirectOffsetOnAxis(ap=istage[:, use, c.slot, i:i + 1], axis=0)
                    pool.indirect_dma_start(place(i), None, source, at).then_inc(landed[c.slot], 16)

            def gather_x(c):
                gather_both(0, c, g_ia, g_x, g_xk, x, lambda i: gx[:, c.slot, i * D:(i + 1) * D])

            def gather_d(c):
                gather_both(1, c, g_ib, g_d, g_dk, dinv_t, lambda i: gdv[:, c.slot, i:i + 1])

            zero = Chunk(2, 0, 0)
            stage(0, zero, 0, 2 * TPC, g_ia)
            stage(1, zero, 0, 2 * TPC, g_ib)
            stage(2, zero, 2 * TPC, TPC, q_ic)
            run_chunks(pool, gather_x, 2, 2, 0, ahead=1)
            pool.wait_ge(s_dt, 16)
            run_chunks(pool, gather_d, 2, 2, 0, ahead=1)

            for i in range(4):
                pool.wait_ge(d_st1[i], 16 * ((CH - 1 - i) // 4 + 1))

            def scatter_x1(c):
                nxt, prev = c.back(-1), c.back(1)
                pool.wait_ge(q_ic, c.n + 1)
                pool.wait_ge(q_ks[c.slot], 16 * (c.turn + 1))
                settled(pool)
                for t in range(TPC):
                    if t == TPC - 1 and nxt.real():
                        if c.after(1):
                            pool.wait_ge(q_sc[prev.slot], 64 * (prev.turn + 1))
                        stage(2, nxt, 2 * TPC, TPC, q_ic)
                    pool.indirect_dma_start(
                        x1t, bass.IndirectOffsetOnAxis(ap=istage[:, 2, c.slot, t:t + 1], axis=0),
                        gx[:, c.slot, t * D:(t + 1) * D], None, bounds_check=N - 1, oob_is_err=False
                    ).then_inc(q_sc[c.slot], 16)

            run_chunks(pool, scatter_x1, 2, 2, 0, ahead=1)
            for i in range(2):
                pool.wait_ge(d_st[i], 16 * ((CH - 1 - i) // 2 + 1))
            pool.sem_inc(r_start, 1)
            pool.wait_ge(r_start, 4)
            pool.wait_ge(q_sc[0], 64 * (CH // 2 + 1))
            pool.wait_ge(q_sc[1], 64 * (CH // 2))

            def stage_back(use, c, first, staged):
                settled(pool)
                k = (CH - 1) - c.n
                pool.tensor_copy(istage[:, use, c.two, 0:TPC],
                                 idx[:, bass.ds(k, 1), first:first + TPC].rearrange("p a b -> p (a b)")
                                 ).then_inc(staged, 1)

            def messages(c):
                l = c.back(5)
                if c.real():
                    nxt, prev = c.back(-1), c.back(1)
                    pool.wait_ge(r_is, c.n + 1)
                    if c.after(2):
                        pool.wait_ge(r_tm, c.n - 1)
                    settled(pool)
                    for t in range(TPC):
                        if t == TPC - 1 and nxt.real():
                            if c.after(1):
                                pool.wait_ge(r_ga[prev.two], 64 * (prev.uses + 1))
                            stage_back(3, nxt, 0, r_is)
                        pool.indirect_dma_start(m_in[:, c.two, t, 0:D], None, x1t,
                                                bass.IndirectOffsetOnAxis(ap=istage[:, 3, c.two, t:t + 1], axis=0)
                                                ).then_inc(r_ga[c.two], 16)
                if l.real():
                    nxt, prev = l.back(-1), l.back(1)
                    pool.wait_ge(r_io, l.n + 1)
                    pool.wait_ge(r_out, l.n + 1)
                    settled(pool)
                    for t in range(TPC):
                        if t == TPC - 1 and nxt.real():
                            if l.after(1):
                                pool.wait_ge(r_sc[prev.two], 64 * (prev.uses + 1))
                            stage_back(4, nxt, 3 * TPC, r_io)
                        u = TPC - 1 - t
                        pool.indirect_dma_start(out, bass.IndirectOffsetOnAxis(ap=istage[:, 4, l.two, u:u + 1], axis=0),
                                                out_e[l.two][:, t * D:(t + 1) * D], None,
                                                bounds_check=N - 1, oob_is_err=False).then_inc(r_sc[l.two], 16)

            stage_back(3, zero, 0, r_is)
            stage_back(4, zero, 3 * TPC, r_io)
            run_chunks(pool, messages, 4, 8, 5, ahead=1)
            pool.wait_ge(r_sc[0], 64 * (CH // 2 + 1))
            pool.wait_ge(r_sc[1], 64 * (CH // 2))


_INS = ['x', 'src', 'dst', 'edge_attr_32', 'L1_gnn_W_m1', 'L1_gnn_b_m1', 'L1_gnn_W_m2', 'L1_gnn_b_m2',
        'L1_gnn_W_c1', 'L1_gnn_b_c1', 'L1_gnn_W_c2', 'L1_gnn_b_c2']


def kernel(**inputs):
    import numpy as _np
    import concourse.bacc as _bacc
    from concourse import mybir as _mybir
    from concourse.bass_utils import run_bass_kernel_spmd as _run

    nc = _bacc.Bacc("TRN2", target_bir_lowering=False, num_devices=1)
    arrays, args = {}, []
    for name in _INS:
        a = _np.ascontiguousarray(inputs[name])
        arrays[f"in_{name}_dram"] = a
        args.append(nc.dram_tensor(f"in_{name}_dram", a.shape, _mybir.dt.from_np(a.dtype), kind="ExternalInput").ap())
    result = nc.dram_tensor("out_0_dram", (N, D), F32, kind="ExternalOutput").ap()
    build(nc, *args, result)
    r = _run(nc, [arrays], core_ids=[0])
    return r.results[0]["out_0_dram"]
```

```python
from contextlib import ExitStack

import concourse.bass as bass
from concourse import mybir
from concourse.alu_op_type import AluOpType as ALU

F32 = mybir.dt.float32
F16 = mybir.dt.float16
BF16 = mybir.dt.bfloat16
I32 = mybir.dt.int32
ACT = mybir.ActivationFunctionType
AX = mybir.AxisListType

P = 128
N, D = 100000, 64
E, DE = 25000, 32
HM, HC = 80, 96
EPS = 1e-5
J = 16
NCH = P * J
CH = -(-N // NCH)
LASTP = (N - (CH - 1) * NCH) // J
TILES = 196
TPC = 4
ECH = TILES // TPC
EP = TILES * P
ROWS = TILES // 2
RE = 2 * P
OFF = 1 << 17
SEG = 8
FREE = J * D
EF = TPC * D
EC = TPC * P
RS = 9
LOOK = 2
KB = 112
NB = CH * J // KB
GD = 2 * TPC - LOOK
EARLY = 2
assert CH == ECH and LASTP * J == N - (CH - 1) * NCH


class Chunk:

    def __init__(self, unroll, turn, slot):
        self.unroll, self.turn, self.slot = unroll, turn, slot
        self.n = turn * unroll + slot

    def back(self, k):
        turns, slot = divmod(self.slot - k, self.unroll)
        return Chunk(self.unroll, self.turn + turns, slot)

    @property
    def two(self):
        return self.slot % 2

    @property
    def uses(self):
        return self.turn * (self.unroll // 2) + self.slot // 2

    def real(self):
        return not isinstance(self.n, int) or 0 <= self.n < CH

    def after(self, k):
        return not isinstance(self.n, int) or self.n >= k


def run_chunks(eng, body, unroll, peel, skew, ahead=0):
    for n in range(peel):
        body(Chunk(unroll, n // unroll, n % unroll))
    last = (CH - 1 - ahead) // unroll
    with eng.Fori(peel // unroll, last) as turn:
        for slot in range(unroll):
            body(Chunk(unroll, turn, slot))
    for n in range(last * unroll, CH + skew):
        body(Chunk(unroll, n // unroll, n % unroll))


def build(nc, x, src, dst, edge_attr, w_m1, b_m1, w_m2, b_m2, w_c1, b_c1, w_c2, b_c2, out):
    with ExitStack() as ctx:
        def sb(name, shape, dt=F32):
            return ctx.enter_context(nc.sbuf_tensor(name, shape, dt))

        def sem(name):
            return ctx.enter_context(nc.semaphore(name))

        x1t = nc.dram_tensor("x1t", (N, D), F32).ap()
        dinv_t = nc.dram_tensor("dinv_t", (CH * NCH, 1), F32).ap()
        srcs = nc.dram_tensor("srcs", (EP, 1), I32).ap()
        dsts = nc.dram_tensor("dsts", (EP + 2, 1), I32).ap()
        attrs = nc.dram_tensor("attrs", (EP, DE), F32).ap()
        src_perm = nc.dram_tensor("src_perm", (EP, 1), I32).ap()
        dst_perm = nc.dram_tensor("dst_perm", (EP, 1), I32).ap()
        attr_perm = nc.dram_tensor("attr_perm", (EP, DE), F32).ap()

        x_all = sb("x_all", [P, ECH * 2 * EF])
        keys = x_all[:, 0:EP]
        d_all = sb("d_all", [P, ECH * 2 * TPC])
        x_in = sb("x_in", [P, 4, FREE])
        xT = sb("xT", [P, 2, FREE])
        cT = sb("cT", [P, 2 * FREE])
        zT = sb("zT", [P, 2, FREE])
        sq = sb("sq", [P, 2, FREE])
        outb = sb("outb", [P, 2, FREE])
        deg = sb("deg", [P, CH * J])
        dinv = sb("dinv", [P, CH * J])
        eps_a = sb("eps_a", [P, CH * J])
        dsum = sb("dsum", [P, 3, J])
        dvar = sb("dvar", [P, 2 * J])
        drstd = sb("drstd", [P, 2, 2 * J])
        dnw = sb("dnw", [P, 2 * J])

        gx = sb("gx", [P, 2, 2 * EF])
        gdv = sb("gdv", [P, 2, GD])
        w_x = sb("w_x", [P, 2, TPC, D])
        mask_rhs = sb("mask_rhs", [P, 2, TPC, P], BF16)
        mask = sb("mask", [P, EC])
        fsum = sb("fsum", [D, 2, EC])
        v_e = sb("v_e", [P, TPC, D])
        ag_e = sb("ag_e", [P, TPC, D])
        t_e = sb("t_e", [P, TPC, D])
        vc_e = sb("vc_e", [P, 2, TPC, D])
        sm = sb("sm", [P, 64])

        idx = sb("idx", [P, ECH, 16], I32)
        istage = sb("istage", [P, 5, 2, 2, 2 * TPC], I32)
        same_prev = sb("same_prev", [P, TILES])
        same_next = sb("same_next", [P, TILES])
        is_last = sb("is_last", [P, TILES])
        hp = sb("hp", [P, TILES])
        hcol = sb("hcol", [P, TILES])
        lp = sb("lp", [P, TILES])
        lcol = sb("lcol", [P, TILES])
        iota_cf = sb("iota_cf", [P, CH * J], F16)
        elast = sb("elast", [P, 2, TPC])
        flag = sb("flag", [1, 1], I32)

        ident = sb("ident", [P, P])
        flip = sb("flip", [P, P])
        centre = sb("centre", [P, P])
        ident_b = sb("ident_b", [P, P], BF16)
        flip_b = sb("flip_b", [P, P], BF16)
        ones_b = sb("ones_b", [P, P], BF16)
        ones_f = sb("ones_f", [P, 1])
        iota_p = sb("iota_p", [P, P], F16)
        wx_d = sb("wx_d", [P, HC])
        wm1 = sb("wm1", [P, HM])
        wme = sb("wme", [DE, HM])
        wm2 = sb("wm2", [HM, D])
        wc1 = sb("wc1", [P, HC])
        wc2 = sb("wc2", [HC + 1, D])
        bm1 = sb("bm1", [HM, 1])
        bm2 = sb("bm2", [D, 1])
        bc1 = sb("bc1", [HC, 1])
        bc2 = sb("bc2", [P, 1])

        esum = sm[:, 12:12 + TPC]

        rows = zT[:, :, :].rearrange("p a b -> p (a b)").rearrange("p (n e) -> p n e", e=RE)[0:ROWS]
        rwin = xT[0:ROWS, 0, 0:RE + 2].bitcast(I32)
        rsrc = xT[0:ROWS, 0, 260:260 + RE].bitcast(I32)
        rtmp = xT[0:ROWS, 0, 520:520 + RE].bitcast(I32)
        rsorted = xT[0:ROWS, 1, 0:RE].bitcast(I32)
        rtm2 = cT[0:ROWS, 0:RE].bitcast(I32)
        usum = sm[0:ROWS, 0:1]
        hist_b = outb[:, :, :].rearrange("p a b -> p (a b)").bitcast(BF16)
        hb = [hist_b[:, i * CH * J:(i + 1) * CH * J] for i in range(4)]
        ha = [hist_b[:, 4 * CH * J + i * P:4 * CH * J + (i + 1) * P] for i in range(4)]
        h_dist = [xT[:, 0, 800 + i * P // 2:800 + (i + 1) * P // 2].bitcast(F16) for i in range(2)]
        iota_c = iota_cf[:, :]
        zeros = mask[0:EP - E, 0:DE]
        seg_out = outb[:, :, :].rearrange("p a b -> p (a b)").bitcast(BF16)[:, 0:EP // SEG]
        dst_e = cT[:, 256:256 + TILES].bitcast(I32)
        dst_ef = cT[:, 456:456 + TILES]
        pos_f = cT[:, 656:656 + TILES]
        pos_i = cT[:, 1420:1420 + TILES].bitcast(I32)
        lower = sq[:, 0, 0:P]
        eq_t = sq[:, 0, P:2 * P]
        seg_n = sm[:, 8:8 + SEG + 1]
        sort_i = sm[:, 32:34].bitcast(I32)
        sort_s = sm[:, 34:35].bitcast(I32)
        sort_e = sq[:, 1, 0:DE]
        parts = xT[0:KB, 0, :].bitcast(BF16)[:, 0:2 * NB * P].rearrange("p (k a b) -> p k a b", a=2, b=P)
        l_hot = sq[:, :, :].rearrange("p a b -> p (a b)").bitcast(BF16)[:, 0:2 * LOOK * CH * J]
        l_hot = l_hot.rearrange("p (s i b) -> p s i b", s=2, i=LOOK)
        l_hT = cT[0:KB, :].bitcast(BF16)[:, 0:2 * LOOK * NB * P].rearrange("p (s i b) -> p s i b", s=2, i=LOOK)
        l_sel = xT[:, 1, 0:2 * LOOK * P].rearrange("p (i a b) -> p i a b", i=LOOK, a=2)
        halves = lambda a: [a[:, i * EC:(i + 1) * EC] for i in range(2)]
        m_in = [a.rearrange("p (t f) -> p t f", t=TPC)
                for a in halves(x_in[:, 0, :]) + [zT[:, i, EC:2 * EC] for i in range(2)]]
        xin = halves(x_in[:, 1, :]) + halves(x_in[:, 2, :])
        mask_m = halves(x_in[:, 3, :]) + halves(outb[:, 1, :])
        eattr = sq[:, 1, 0:2 * TPC * DE].rearrange("p (s t f) -> p s t f", s=2, t=TPC)
        eT = halves(xT[0:DE, 0, :])
        mT = halves(xT[0:D, 1, :])
        hT = cT[0:HM, EC:2 * EC]
        c2T = cT[0:HC + 1, 0:EC]
        comb_e = [zT[:, 0, s * EF:(s + 1) * EF].rearrange("p (t f) -> p t f", f=D) for s in range(2)]
        zc_e = [zT[:, 1, s * EF:(s + 1) * EF].rearrange("p (t f) -> p t f", f=D) for s in range(2)]
        sq_e = sq[:, 0, 0:EF].rearrange("p (t f) -> p t f", f=D)
        out_e = [outb[:, 0, s * EF:(s + 1) * EF] for s in range(4)]

        ps = ctx.enter_context(nc.psum_tensor("ps", [P, 8, 512], F32))
        ps_xT = ps[:, 0:2, :]
        ps_z = [ps[:, 4 + 2 * s:6 + 2 * s, :].rearrange("p a b -> p (a b)") for s in range(2)]
        ps_w = [ps[0:D, s, :] for s in range(2)]
        ps_mask = ps[0:D, 2, :]
        ps_ag = [ps[:, 3 + s, 0:EF] for s in range(2)]
        ps_hT = [ps[0:KB, 5 + i, :].bitcast(BF16)[:, 0:NB * P] for i in range(LOOK)]
        ps_look = ps[:, 7, 0:LOOK * 2 * P].rearrange("p (i b) -> p i b", i=LOOK)
        hist = ps[:, 0:2, 0:CH * J // 2]
        ps_i = ps[:, 2:7, 0:4 * ROWS].rearrange("p a (n h q) -> p a n h q", n=2, h=2)
        ps_flip = ps[:, 7, 0:TILES]
        ps_u = ps[0:1, 7, 508:509]

        s_zeros = sem("s_zeros")
        s_guard = sem("s_guard")
        s_hfill = sem("s_hfill")
        s_ones = sem("s_ones")
        s_consts = sem("s_consts")
        s_lower = sem("s_lower")
        s_iota = sem("s_iota")
        s_dst = sem("s_dst")
        s_copy = sem("s_copy")
        s_attr = sem("s_attr")
        s_weights = sem("s_weights")
        s_win = sem("s_win")
        s_hsrc = sem("s_hsrc")
        s_ucount = sem("s_ucount")
        s_flag = sem("s_flag")
        s_keys = sem("s_keys")
        s_keyf = sem("s_keyf")
        s_rank = sem("s_rank")
        s_ranked = sem("s_ranked")
        s_stage = sem("s_stage")
        s_tile = sem("s_tile")
        s_perm = sem("s_perm")
        s_back = sem("s_back")
        s_settled = sem("s_settled")
        s_sorted = sem("s_sorted")
        s_rows = sem("s_rows")
        s_hidx = sem("s_hidx")
        s_ri = sem("s_ri")
        s_iT = sem("s_iT")
        s_idx = sem("s_idx")
        s_onehot = sem("s_onehot")
        s_dist = sem("s_dist")
        s_onehot2 = sem("s_onehot2")
        s_hist = sem("s_hist")
        s_deg = sem("s_deg")
        s_dinv = sem("s_dinv")
        s_root = sem("s_root")
        s_scale = sem("s_scale")
        s_dt = sem("s_dt")
        s_centre = sem("s_centre")
        s_biasrow = sem("s_biasrow")

        g_ia = sem("g_ia")
        g_x = [sem(f"g_x{i}") for i in range(2)]
        g_xk = [sem(f"g_xk{i}") for i in range(2)]
        g_ib = sem("g_ib")
        g_d = [sem(f"g_d{i}") for i in range(2)]
        g_dk = [sem(f"g_dk{i}") for i in range(2)]

        d_x = [sem(f"d_load{i}") for i in range(4)]
        d_m = sem("d_m")
        d_xc = sem("d_xc")
        d_sq1 = sem("d_sq1")
        d_s1 = sem("d_s1")
        d_v1 = sem("d_v1")
        d_v2 = sem("d_v2")
        d_pow = sem("d_pow")
        d_x1 = sem("d_x1")
        d_st1 = [sem(f"d_st1_{i}") for i in range(4)]
        d_T = sem("d_T")
        d_Ts = sem("d_Ts")
        d_c = sem("d_c")
        d_cg = sem("d_cg")
        d_o = sem("d_o")
        d_og = sem("d_og")
        d_zT = sem("d_zT")
        d_z = sem("d_z")
        d_sq2 = sem("d_sq2")
        d_s2 = sem("d_s2")
        d_out = sem("d_out")
        d_st = [sem(f"d_st{i}") for i in range(2)]

        q_w = sem("q_w")
        q_mr = sem("q_mr")
        q_wT = sem("q_wT")
        q_mask = sem("q_mask")
        q_f = sem("q_f")
        q_fT = sem("q_fT")
        q_v = sem("q_v")
        q_sq = sem("q_sq")
        q_var = sem("q_var")
        q_pow = sem("q_pow")
        q_last = sem("q_last")
        q_xd = sem("q_xd")
        q_dT = sem("q_dT")
        q_part = sem("q_part")
        q_hot = sem("q_hot")
        q_hT = sem("q_hT")
        q_hTs = sem("q_hTs")
        q_look = sem("q_look")
        q_sel = sem("q_sel")
        q_put = sem("q_put")
        q_ks = [sem(f"q_ks{i}") for i in range(2)]
        q_ic = sem("q_ic")
        q_sc = [sem(f"q_sc{i}") for i in range(2)]

        r_start = sem("r_start")
        r_is = sem("r_is")
        r_io = sem("r_io")
        r_ga = [sem(f"r_ga{i}") for i in range(4)]
        r_e = [sem(f"r_e{i}") for i in range(2)]
        r_m = sem("r_m")
        r_md = sem("r_md")
        r_tm = sem("r_tm")
        r_xs = sem("r_xs")
        r_sq = sem("r_sq")
        r_s = sem("r_s")
        r_xd = sem("r_xd")
        r_h = sem("r_h")
        r_hg = sem("r_hg")
        r_mm = sem("r_mm")
        r_mg = sem("r_mg")
        r_box = sem("r_box")
        r_c = sem("r_c")
        r_cg = sem("r_cg")
        r_o = sem("r_o")
        r_og = sem("r_og")
        r_z = sem("r_z")
        r_var = sem("r_var")
        r_pow = sem("r_pow")
        r_out = sem("r_out")
        r_sc = [sem(f"r_sc{i}") for i in range(4)]
        block = ctx.enter_context(nc.Block())

        GUARD = slice(1, EP + 1)
        col3 = lambda a: a.rearrange("p (a b) -> p a b", b=D)
        wide = lambda a, n, f: a.unsqueeze(2).to_broadcast([a.shape[0], n, f])

        def x_chunk(c, t):
            if isinstance(c, int) and c == CH - 1:
                return t[c * NCH:N, :].rearrange("(p j) d -> p (j d)", j=J), LASTP
            return t[bass.ds(c * NCH, NCH), :].rearrange("(p j) d -> p (j d)", j=J), P

        def settled(eng):
            eng.sem_inc(s_settled, 1)

        @block.sync
        def _(sp):
            sp.dma_start(dsts[1:E + 1, :], dst.rearrange("(n a) -> n a", a=1)).then_inc(s_dst, 16)
            sp.wait_ge(s_guard, 3)
            sp.dma_start(dsts[E + 1:EP + 1, :], sort_s[0:EP - E, :]).then_inc(s_dst, 16)
            sp.dma_start(dsts[0:1, :], sort_i[0:1, 0:1]).then_inc(s_dst, 16)
            sp.dma_start(dsts[EP + 1:EP + 2, :], sort_i[0:1, 1:2]).then_inc(s_dst, 16)
            full = E // RE
            sp.wait_ge(s_hfill, 1)
            sp.dma_start(rsrc[0:full, :], src[0:full * RE].rearrange("(q e) -> q e", e=RE)).then_inc(s_hsrc, 16)
            sp.dma_start(rsrc[full:full + 1, 0:E - full * RE],
                         src[full * RE:E].rearrange("(q e) -> q e", q=1)).then_inc(s_hsrc, 16)
            sp.wait_ge(s_dst, 64)
            window = bass.AP(dsts.tensor, 0, [[RE, ROWS], [1, RE + 2]])
            sp.dma_start(rwin, window).then_inc(s_win, 16)
            sp.wait_ge(s_zeros, 1)
            sp.dma_start(srcs[0:E, :], src.rearrange("(n a) -> n a", a=1)).then_inc(s_copy, 16)
            sp.dma_start(srcs[E:EP, :], zeros[:, 0:1].bitcast(I32)).then_inc(s_copy, 16)
            sp.wait_ge(s_sorted, 1)
            sp.wait_ge(s_ucount, 1)
            sp.wait_ge(s_copy, 32)
            sp.dma_start(rwin, window).then_inc(s_rows, 16)
            sp.dma_start(rsorted, srcs.rearrange("(q e) a -> q (e a)", e=RE)).then_inc(s_rows, 16)
            for dst_ap, src_ap in (
                    (wx_d[0:D, :], w_c1[0:D, :]), (wx_d[D:P, :], w_c1[0:D, :]), (wm1[:, :], w_m1[0:P, :]),
                    (wme[:, :], w_m1[P:P + DE, :]), (wm2[:, :], w_m2), (wc1[0:D, :], w_c1[D:P, :]),
                    (wc1[D:P, :], w_c1[0:D, :]), (wc2[0:HC, :], w_c2),
                    (wc2[HC:HC + 1, :], b_c2.rearrange("(a n) -> a n", a=1)),
                    (bm1[:, :], b_m1.rearrange("(n a) -> n a", a=1)),
                    (bm2[:, :], b_m2.rearrange("(n a) -> n a", a=1)),
                    (bc1[:, :], b_c1.rearrange("(n a) -> n a", a=1)),
                    (bc2[0:D, :], b_c2.rearrange("(n a) -> n a", a=1)),
                    (bc2[D:P, :], b_c2.rearrange("(n a) -> n a", a=1))):
                sp.dma_start(dst_ap, src_ap).then_inc(s_weights, 16)

            def keep_x(c):
                sp.wait_ge(g_x[c.slot], 128 * (c.turn + 1))
                settled(sp)
                sp.dma_start(x_all[:, bass.ds(c.n * (2 * EF), 2 * EF)], gx[:, c.slot, :]).then_inc(g_xk[c.slot], 16)

            def keep_d(c):
                sp.wait_ge(g_d[c.slot], 16 * GD * (c.turn + 1))
                settled(sp)
                sp.dma_start(d_all[:, bass.ds(c.n * (2 * TPC) + LOOK, GD)], gdv[:, c.slot, :]).then_inc(g_dk[c.slot], 16)

            def scatter_source(c):
                sp.wait_ge(q_xd, c.n + 1)
                settled(sp)
                if c.after(2):
                    sp.wait_ge(q_sc[c.slot], 64 * c.turn)
                    settled(sp)
                sp.dma_start(gx[:, c.slot, 0:EF], x_all[:, bass.ds(c.n * (2 * EF) + EF, EF)]
                             ).then_inc(q_ks[c.slot], 16)

            run_chunks(sp, keep_x, 2, 2, 0)
            run_chunks(sp, keep_d, 2, 2, 0)
            run_chunks(sp, scatter_source, 2, 2, 0)
            sp.wait_ge(r_start, 4)

            def load_e(c):
                if c.after(2):
                    sp.wait_ge(r_tm, c.n - 1)
                    settled(sp)
                k = (CH - 1) - c.n
                sp.dma_start(eattr[:, c.two, :, :],
                             attrs[bass.ds(k * EC, EC), :].rearrange("(t p) d -> p t d", p=P)
                             ).then_inc(r_e[c.two], 16)

            sp.wait_ge(s_attr, 32)
            run_chunks(sp, load_e, 2, 2, 0)

        @block.scalar
        def _(act):
            def load(c):
                src_ap, parts = x_chunk(c.n, x)
                act.dma_start(x_in[0:parts, c.slot, :], src_ap).then_inc(d_x[c.slot], 16)

            act.dma_start(attrs[0:E, :].rearrange("(a b) d -> a (b d)", a=200),
                          edge_attr.rearrange("(a b) d -> a (b d)", a=200)).then_inc(s_attr, 16)
            act.wait_ge(s_zeros, 1)
            act.dma_start(attrs[E:EP, :], zeros).then_inc(s_attr, 16)
            for n in range(4):
                load(Chunk(4, 0, n))
            act.wait_ge(s_ones, 3)
            act.wait_ge(s_iota, 2)
            act.wait_ge(s_idx, 2)

            def onehots(turn, slot, wait):
                t = 4 * turn + slot
                if wait:
                    act.wait_ge(s_hist, t - 3)
                act.activation(h_dist[slot // 2], iota_p[:, :], ACT.Abs, scale=-1.0,
                               bias=hp[:, bass.ds(t, 1)]).then_inc(s_dist, 1)
                act.wait_ge(s_dist, 2 * turn + slot // 2 + 1)
                act.activation(ha[slot], h_dist[slot // 2], ACT.Relu, scale=-1.0, bias=ones_f[:, 0:1]
                               ).then_inc(s_onehot2, 1)

            for slot in (1, 3):
                onehots(0, slot, False)
            with act.Fori(1, TILES // 4) as turn:
                for slot in (1, 3):
                    onehots(turn, slot, True)
            act.wait_ge(s_deg, 1)
            act.activation(zT[:, 1, 0:CH * J], deg[:, :], ACT.Sqrt).then_inc(s_root, 1)
            act.wait_ge(s_dinv, 1)
            act.dma_start(dinv_t.rearrange("(c p j) a -> p c (j a)", p=P, j=J),
                          dinv[:, :].rearrange("p (c j) -> p c j", j=J)).then_inc(s_dt, 16)

            act.wait_ge(s_weights, 16 * 14)

            def dense(c):
                n, g, o = c.back(2), c.back(4), c.back(6)
                nxt = c.back(-2)
                if n.real():
                    act.wait_ge(d_x1, n.n + 1)
                    dst_ap, parts = x_chunk(n.n, x1t)
                    act.dma_start(dst_ap, x_in[0:parts, n.slot, :]).then_inc(d_st1[n.slot], 16)
                if o.real():
                    act.wait_ge(d_out, o.n + 1)
                    dst_ap, parts = x_chunk(o.n, out)
                    act.dma_start(dst_ap, outb[0:parts, o.two, :]).then_inc(d_st[o.two], 16)
                if n.real():
                    s = n.two
                    if n.after(2):
                        act.wait_ge(d_zT, n.n - 1)
                        act.wait_ge(d_c, 4 * (n.n - 1))
                    for i in range(2):
                        act.wait_ge(d_T, 2 * n.n + i + 1)
                        act.activation(xT[:, s, i * 512:(i + 1) * 512], ps_xT[:, i, :], ACT.Copy).then_inc(d_Ts, 1)
                if g.real():
                    act.wait_ge(d_z, g.n + 1)
                    if g.after(1):
                        act.wait_ge(d_s2, g.n)
                    act.activation(sq[:, 1, :], ps_z[g.two], ACT.Square).then_inc(d_sq2, 1)
                for q in range(4):
                    if n.real():
                        i, half = divmod(q, 2)
                        act.wait_ge(d_c, 4 * n.n + q + 1)
                        if q == 0 and n.after(1):
                            act.wait_ge(d_o, n.n)
                        act.activation(cT[0:HC, half * FREE + i * 512:half * FREE + (i + 1) * 512], ps[0:HC, 2 + half, :],
                                       ACT.Gelu, bias=bc1[:, 0:1]).then_inc(d_cg, 1)
                    if q == 1 and c.real():
                        act.wait_ge(d_xc, c.n + 1)
                        if c.after(1):
                            act.wait_ge(d_s1, c.n)
                        act.activation(sq[:, 0, :], x_in[:, c.slot, :], ACT.Square).then_inc(d_sq1, 1)
                if n.real():
                    act.wait_ge(d_o, n.n + 1)
                    if n.after(2):
                        act.wait_ge(d_z, n.n - 1)
                    act.activation(zT[:, n.two, :], ps_xT.rearrange("p a b -> p (a b)"), ACT.Gelu,
                                   bias=bc2[:, 0:1]).then_inc(d_og, 1)
                if nxt.real() and nxt.after(4):
                    act.wait_ge(d_st1[nxt.slot], 16 * nxt.turn)
                    act.wait_ge(d_T, 2 * (nxt.n - 3))
                    load(nxt)

            run_chunks(act, dense, 4, 8, 6, ahead=2)

            def sums_pass(c):
                b, g, h = c.back(1), c.back(4), c.back(5)
                if c.real():
                    if c.after(2):
                        act.wait_ge(q_wT, c.n - 1)
                    for t in range(TPC):
                        ins = act.activation(mask_rhs[:, c.slot, t, :], ident_b[:, :], ACT.Copy,
                                             scale=same_prev[:, bass.ds(c.n * TPC + t, 1)])
                    ins.then_inc(q_mr, 1)
                if b.real():
                    act.wait_ge(q_wT, b.n + 1)
                    if b.after(1):
                        act.wait_ge(q_f, b.n)
                    act.activation(mask[0:D, :], ps_mask, ACT.Copy).then_inc(q_mask, 1)
                    act.wait_ge(q_hT, b.n + 1)
                    if b.after(2):
                        act.wait_ge(q_look, b.n - 1)
                    for i in range(LOOK):
                        ins = act.activation(l_hT[:, b.slot, i, :], ps_hT[i], ACT.Copy)
                    ins.then_inc(q_hTs, 1)
                if g.real():
                    act.wait_ge(q_v, 8 * (g.n + 1))
                    if g.after(1):
                        act.wait_ge(q_var, g.n)
                    for t in range(TPC):
                        ins = act.activation(t_e[:, t, :], vc_e[:, g.slot, t, :], ACT.Square, accum_out=esum[:, t:t + 1])
                    ins.then_inc(q_sq, 1)
                if h.real():
                    act.wait_ge(q_last, h.n + 1)
                    for t in range(TPC):
                        ins = act.activation(x_all[:, bass.ds(h.n * (2 * EF) + EF + t * D, D)], vc_e[:, h.slot, t, :],
                                             ACT.Copy, scale=elast[:, h.slot, t:t + 1])
                    ins.then_inc(q_xd, 1)

            run_chunks(act, sums_pass, 2, 6, 5)
            act.sem_inc(r_start, 1)
            act.wait_ge(r_start, 4)

            def messages(c):
                b, m, g, h = c.back(1), c.back(2), c.back(3), c.back(4)
                if c.real():
                    k = (CH - 1) - c.n
                    if c.after(4):
                        act.wait_ge(r_tm, c.n - 3)
                    act.activation(m_in[c.slot][:, :, D:P],
                                   x_all[:, bass.ds(k * (2 * EF) + EF, EF)].rearrange("p (t f) -> p t f", f=D),
                                   ACT.Copy).then_inc(r_md, 1)
                if m.real():
                    act.wait_ge(r_h, m.n + 1)
                    if m.after(1):
                        act.wait_ge(r_mm, m.n)
                    act.activation(hT, ps[0:HM, 3, :], ACT.Gelu, bias=bm1[:, 0:1]).then_inc(r_hg, 1)
                if g.real():
                    act.wait_ge(r_c, g.n + 1)
                    if g.after(1):
                        act.wait_ge(r_o, g.n)
                    act.activation(c2T[0:HC, :], ps[0:HC, 5, :], ACT.Gelu, bias=bc1[:, 0:1]).then_inc(r_cg, 1)
                if m.real():
                    act.wait_ge(r_mm, m.n + 1)
                    if m.after(2):
                        act.wait_ge(r_box, m.n - 1)
                    act.activation(mT[m.two], ps[0:D, 4, :], ACT.Gelu, bias=bm2[:, 0:1]).then_inc(r_mg, 1)
                if b.real():
                    act.wait_ge(r_tm, b.n + 1)
                    if b.after(4):
                        act.wait_ge(r_o, b.n - 3)
                        act.wait_ge(r_box, b.n - 2)
                    act.activation(xin[b.slot][0:D, :], ps[0:D, 0, :], ACT.Copy).then_inc(r_xs, 1)
                    act.activation(mask_m[b.slot], ps[:, 1, :], ACT.Copy).then_inc(r_xs, 1)
                    if b.after(2):
                        act.wait_ge(r_h, b.n - 1)
                    act.activation(eT[b.two], ps[0:DE, 2, :], ACT.Copy).then_inc(r_xs, 1)
                if h.real():
                    act.wait_ge(r_z, 3 * (h.n + 1))
                    if h.after(1):
                        act.wait_ge(r_s, h.n)
                    act.activation(sq_e, zc_e[h.two], ACT.Square).then_inc(r_sq, 1)
                if g.real():
                    act.wait_ge(r_o, g.n + 1)
                    if g.after(2):
                        act.wait_ge(r_z, 3 * (g.n - 1))
                    act.activation(comb_e[g.two], ps[:, 6 + g.two, 0:EF].rearrange("p (t f) -> p t f", f=D), ACT.Gelu
                                   ).then_inc(r_og, 1)

            run_chunks(act, messages, 4, 8, 4)

        @block.tensor
        def _(pe):
            pe.wait_ge(s_ones, 3)
            pe.wait_ge(s_consts, 4)
            pe.wait_ge(s_ucount, 1)
            pe.matmul(ps_u, usum, ones_f[0:ROWS, :], start=True, stop=True).then_inc(s_iT, 1)
            pe.wait_ge(s_hidx, 2)
            for a in range(2):
                for h in range(2):
                    mm = pe.transpose(ps_i[:, 4, a, h, :], rows[:, 6 + a, h * P:(h + 1) * P],
                                      ident[0:ROWS, 0:ROWS])
            mm.then_inc(s_iT, 1)

            def hist_tile(turn, slot, first, last):
                pe.wait_ge(s_onehot, 4 * turn + slot + 1)
                if slot % 2 == 1:
                    pe.wait_ge(s_onehot2, 2 * turn + slot // 2 + 1)
                for b in range(2):
                    half = CH * J // 2
                    mm = pe.matmul(hist[:, b, :], ha[slot], hb[slot][:, b * half:(b + 1) * half],
                                   start=first, stop=last)
                mm.then_inc(s_hist, 1)

            for slot in range(4):
                hist_tile(0, slot, slot == 0, False)
            with pe.Fori(1, EARLY) as turn:
                for slot in range(4):
                    hist_tile(turn, slot, False, False)

            pe.wait_ge(s_ri, 4)
            pe.wait_ge(s_idx, 2)
            for a in range(8):
                if a == 6:
                    pe.wait_ge(s_ri, 10)
                for h in range(2):
                    mm = pe.transpose(ps_i[:, a // 2, a % 2, h, :], rows[:, a, h * P:(h + 1) * P],
                                      ident[0:ROWS, 0:ROWS])
                if a in (5, 7):
                    mm.then_inc(s_iT, 1)
            pe.wait_ge(s_idx, 3)
            pe.matmul(ps_flip, flip[:, :], sq[:, 0, 0:TILES], start=True, stop=True).then_inc(s_iT, 1)

            with pe.Fori(EARLY, TILES // 4 - 1) as turn:
                for slot in range(4):
                    hist_tile(turn, slot, False, False)
            for slot in range(4):
                hist_tile(TILES // 4 - 1, slot, False, slot == 3)

            pe.wait_ge(s_weights, 16 * 14)
            pe.wait_ge(s_centre, 4)

            def dense(c):
                n, b = c.back(2), c.back(4)
                if n.real():
                    pe.wait_ge(d_x1, n.n + 1)
                    if n.after(1):
                        pe.wait_ge(d_og, n.n)
                    for i in range(2):
                        for k in range(4 * i, 4 * i + 4):
                            mm = pe.transpose(ps_xT[:, i, (k % 4) * P:(k % 4 + 1) * P],
                                              x_in[:, n.slot, k * P:(k + 1) * P], ident[:, :])
                        mm.then_inc(d_T, 1)
                if b.real():
                    s = b.two
                    pe.wait_ge(d_zT, b.n + 1)
                    if b.after(2):
                        pe.wait_ge(d_out, b.n - 1)
                    for k in range(J // 2):
                        mm = pe.matmul(ps_z[s][:, k * P:(k + 1) * P], zT[:, s, k * P:(k + 1) * P], centre[:, :],
                                       start=True, stop=True)
                    mm.then_inc(d_z, 1)
                if n.real():
                    s = n.two
                    for q in range(4):
                        i, half = divmod(q, 2)
                        pe.wait_ge(d_Ts, 2 * n.n + i + 1)
                        if q >= 2 or n.after(1):
                            pe.wait_ge(d_cg, 4 * n.n + q - 1)
                        pe.matmul(ps[0:HC, 2 + half, :], wx_d[half * D:(half + 1) * D, :],
                                  xT[half * D:(half + 1) * D, s, i * 512:(i + 1) * 512],
                                  start=True, stop=True).then_inc(d_c, 1)
                    for q in range(4):
                        i, half = divmod(q, 2)
                        pe.wait_ge(d_cg, 4 * n.n + q + 1)
                        mm = pe.matmul(ps[half * D:(half + 1) * D, i, :], wc2[0:HC, :],
                                       cT[0:HC, half * FREE + i * 512:half * FREE + (i + 1) * 512],
                                       start=True, stop=True)
                    mm.then_inc(d_o, 1)
            run_chunks(pe, dense, 4, 8, 4)

            pe.wait_ge(d_og, CH)
            pe.wait_ge(d_out, CH)

            for k in range(NB):
                mm = pe.transpose(ps[0:KB, k // 4, (k % 4) * P:(k % 4 + 1) * P], deg[:, k * KB:(k + 1) * KB], ident[:, :])
            mm.then_inc(q_dT, 1)
            pe.wait_ge(q_part, 6)

            def sums_pass(c):
                b, m, d = c.back(1), c.back(2), c.back(3)
                if b.real():
                    pe.wait_ge(q_w, b.n + 1)
                    pe.wait_ge(q_mr, b.n + 1)
                    if b.after(2):
                        pe.wait_ge(q_f, b.n - 1)
                    if b.after(1):
                        pe.wait_ge(q_mask, b.n)
                    settled(pe)
                    for t in range(TPC):
                        pe.transpose(ps_w[b.slot][:, t * P:(t + 1) * P], w_x[:, b.slot, t, :], ident[:, :])
                    pe.matmul(ps_mask, ones_b[:, 0:D],
                              mask_rhs[:, b.slot, :, :].rearrange("p t e -> p (t e)"),
                              start=True, stop=True).then_inc(q_wT, 1)
                if d.real():
                    pe.wait_ge(q_f, d.n + 1)
                    if d.after(2):
                        pe.wait_ge(q_v, 8 * (d.n - 1))
                    settled(pe)
                    for t in range(TPC):
                        mm = pe.transpose(ps_ag[d.slot][:, t * D:(t + 1) * D], fsum[:, d.slot, t * P:(t + 1) * P],
                                          ident[0:D, 0:D])
                    mm.then_inc(q_fT, 1)
                if b.real():
                    pe.wait_ge(q_hot, b.n + 1)
                    if b.after(1):
                        pe.wait_ge(q_hTs, b.n)
                    settled(pe)
                    for i in range(LOOK):
                        for k in range(NB):
                            mm = pe.transpose(ps_hT[i][:, k * P:(k + 1) * P], l_hot[:, b.slot, i, k * KB:(k + 1) * KB],
                                              ident_b[:, :])
                    mm.then_inc(q_hT, 1)
                if m.real():
                    pe.wait_ge(q_hTs, m.n + 1)
                    if m.after(1):
                        pe.wait_ge(q_sel, LOOK * m.n)
                    for i in range(LOOK):
                        for k in range(NB):
                            mm = pe.matmul(ps_look[:, i, :], l_hT[:, m.slot, i, k * P:(k + 1) * P],
                                           parts[:, k, :, :].rearrange("p a b -> p (a b)"),
                                           start=k == 0, stop=k == NB - 1)
                    mm.then_inc(q_look, 1)

            run_chunks(pe, sums_pass, 2, 6, 3)
            pe.sem_inc(r_start, 1)
            pe.wait_ge(r_start, 4)

            def messages(c):
                b, m, g = c.back(1), c.back(2), c.back(3)
                if m.real():
                    pe.wait_ge(r_xs, 3 * (m.n + 1))
                    pe.wait_ge(r_xd, m.n + 1)
                    if m.after(1):
                        pe.wait_ge(r_hg, m.n)
                    pe.matmul(ps[0:HM, 3, :], wm1[:, :], xin[m.slot], start=True, stop=False)
                    pe.matmul(ps[0:HM, 3, :], wme[:, :], eT[m.two], start=False, stop=True).then_inc(r_h, 1)
                if g.real():
                    pe.wait_ge(r_box, g.n + 1)
                    if g.after(1):
                        pe.wait_ge(r_cg, g.n)
                    pe.matmul(ps[0:HC, 5, :], wc1[:, :], xin[g.slot], start=True, stop=True).then_inc(r_c, 1)
                if m.real():
                    pe.wait_ge(r_hg, m.n + 1)
                    if m.after(1):
                        pe.wait_ge(r_mg, m.n)
                    pe.matmul(ps[0:D, 4, :], wm2[:, :], hT, start=True, stop=True).then_inc(r_mm, 1)
                if b.real():
                    pe.wait_ge(r_m, b.n + 1)
                    pe.wait_ge(r_md, b.n + 1)
                    pe.wait_ge(r_ga[b.slot], 64 * (b.turn + 1))
                    pe.wait_ge(r_e[b.two], 16 * (b.uses + 1))
                    if b.after(1):
                        pe.wait_ge(r_xs, 3 * b.n)
                        pe.wait_ge(r_xd, b.n)
                    for t in range(TPC):
                        u = TPC - 1 - t
                        pe.matmul(ps[:, 0, t * P:(t + 1) * P], m_in[b.slot][:, u, :], flip[:, :],
                                  start=True, stop=True)
                    pe.matmul(ps[:, 1, :], ones_b[:, :], mask_rhs[:, b.two, :, :].rearrange("p t e -> p (t e)"),
                              start=True, stop=True)
                    for t in range(TPC):
                        u = TPC - 1 - t
                        mm = pe.matmul(ps[0:DE, 2, t * P:(t + 1) * P], eattr[:, b.two, u, :], flip[:, :],
                                       start=True, stop=True)
                    mm.then_inc(r_tm, 1)
                if g.real():
                    pe.wait_ge(r_cg, g.n + 1)
                    if g.after(2):
                        pe.wait_ge(r_z, 3 * (g.n - 2) + 1)
                    for t in range(TPC):
                        pe.matmul(ps[:, 6 + g.two, t * D:(t + 1) * D], c2T[:, t * P:(t + 1) * P], wc2[:, :],
                                  start=True, stop=True)
                        mm = pe.matmul(ps[:, 6 + g.two, EF + t * D:EF + (t + 1) * D], xin[g.slot][D:P, t * P:(t + 1) * P],
                                       ident[D:P, D:P], start=True, stop=True)
                    mm.then_inc(r_o, 1)

            run_chunks(pe, messages, 4, 8, 3)

        @block.vector
        def _(dve):
            def then(ins, sem_, value):
                ins.then_inc(sem_, 1)
                dve.wait_ge(sem_, value)

            def newton(y, v, tmp, sem_, base):
                then(dve.scalar_tensor_tensor(tmp, y, -0.5, y, ALU.mult, ALU.mult), sem_, base + 1)
                then(dve.tensor_tensor(tmp, tmp, v, ALU.mult), sem_, base + 2)
                then(dve.scalar_tensor_tensor(y, tmp, 1.5, y, ALU.add, ALU.mult), sem_, base + 3)

            def rsqrt_step(k, y, v, tmp, sem_, base):
                if k > 1:
                    dve.wait_ge(sem_, base + k - 1)
                yi = y.bitcast(I32)
                if k == 1:
                    ins = dve.tensor_scalar(yi, v.bitcast(I32), 1, None, ALU.arith_shift_right)
                elif k == 2:
                    ins = dve.tensor_scalar(yi, yi, -1.0, float(0x5F3759DF), ALU.mult, ALU.add)
                elif k == 3:
                    ins = dve.tensor_tensor(tmp, y, y, ALU.mult)
                elif k == 5:
                    ins = dve.scalar_tensor_tensor(tmp, tmp, -10.0 / 3.0, tmp, ALU.add, ALU.mult)
                elif k == 6:
                    ins = dve.scalar_tensor_tensor(y, tmp, 5.0, y, ALU.add, ALU.mult)
                elif k == 7:
                    ins = dve.scalar_tensor_tensor(tmp, y, -0.5 * 0.375 ** 3, y, ALU.mult, ALU.mult)
                elif k == 9:
                    ins = dve.scalar_tensor_tensor(y, tmp, 1.5 * 0.375, y, ALU.add, ALU.mult)
                else:
                    ins = dve.tensor_tensor(tmp, tmp, v, ALU.mult)
                ins.then_inc(sem_, 1)

            dve.memset(mask[:, :], 0.0).then_inc(s_zeros, 1)
            dve.memset(sort_i[0:1, 0:1], -1).then_inc(s_guard, 1)
            dve.memset(sort_i[0:1, 1:2], 2 * OFF).then_inc(s_guard, 1)
            dve.memset(sort_s, OFF).then_inc(s_guard, 1)
            dve.memset(rsrc, OFF).then_inc(s_hfill, 1)
            dve.memset(ones_b[:, :], 1.0).then_inc(s_ones, 1)
            dve.memset(ones_f[:, :], 1.0).then_inc(s_ones, 1)
            dve.memset(dvar[:, :], 1.0).then_inc(s_ones, 1)
            then(dve.memset(centre[:, :], 0.0), s_centre, 1)
            dve.memset(centre[0:D, 0:D], -1.0 / D).then_inc(s_centre, 1)
            then(dve.memset(centre[D:P, D:P], -1.0 / D), s_centre, 3)

            dve.wait_ge(s_win, 16)
            dve.tensor_tensor(rows[:, 0, :], rwin[:, 1:RE + 1], rwin[:, 2:RE + 2], ALU.is_gt).then_inc(s_rank, 1)
            dve.wait_ge(s_rank, 1)
            dve.tensor_reduce(usum, rows[:, 0, :], AX.X, ALU.add).then_inc(s_ucount, 1)
            dve.wait_ge(s_hsrc, 32)
            dve.tensor_scalar(rtmp, rsrc, 4, P - 1, ALU.arith_shift_right, ALU.bitwise_and).then_inc(s_rank, 1)
            dve.tensor_scalar(rtm2, rsrc, J - 1, None, ALU.bitwise_and).then_inc(s_rank, 1)
            dve.wait_ge(s_rank, 3)
            dve.tensor_scalar(rsrc, rsrc, 11, 4, ALU.arith_shift_right, ALU.logical_shift_left).then_inc(s_rank, 1)
            dve.wait_ge(s_rank, 4)
            dve.tensor_tensor(rows[:, 7, :], rsrc, rtm2, ALU.add).then_inc(s_hidx, 1)
            dve.tensor_copy(rows[:, 6, :], rtmp).then_inc(s_hidx, 1)
            dve.wait_ge(s_iT, 1)
            dve.tensor_scalar(flag[:, :], ps_u, 1.0, None, ALU.min).then_inc(s_flag, 1)
            dve.wait_ge(s_flag, 1)
            unsorted = dve.value_load(flag[0:1, 0:1], min_val=0, max_val=1)
            with dve.If(unsorted == 1):
                dve.wait_ge(s_lower, 1)
                dve.wait_ge(s_keyf, 1)
                dve.wait_ge(s_keys, 32)
                then(dve.tensor_copy(dst_ef, dst_e), s_ranked, 1)
                with dve.Fori(0, TILES) as t:
                    mine = dst_ef[:, bass.ds(t, 1)]
                    for g in range(SEG):
                        n = EP // SEG
                        dve.tensor_scalar(seg_out, keys[:, g * n:(g + 1) * n], mine, 0.0, ALU.is_lt, ALU.add,
                                          accum_out=seg_n[:, g:g + 1]).then_inc(s_rank, 1)
                        dve.wait_ge(s_rank, 4 + t * (SEG + 5) + g + 1)
                    tile_keys = keys[:, bass.ds(t * P, P)]
                    base = 4 + t * (SEG + 5) + SEG
                    then(dve.tensor_scalar(eq_t, tile_keys, mine, None, ALU.is_equal), s_rank, base + 1)
                    then(dve.tensor_tensor(eq_t, eq_t, lower, ALU.mult), s_rank, base + 2)
                    then(dve.tensor_reduce(seg_n[:, SEG:SEG + 1], eq_t, AX.X, ALU.add), s_rank, base + 3)
                    then(dve.tensor_reduce(pos_f[:, bass.ds(t, 1)], seg_n, AX.X, ALU.add), s_rank, base + 4)
                    then(dve.tensor_scalar(tile_keys, tile_keys, -0.5, None, ALU.add), s_rank, base + 5)
                then(dve.tensor_copy(pos_i, pos_f), s_ranked, 2)

            dve.wait_ge(s_iota, 2)
            dve.wait_ge(s_iT, 2)
            dve.tensor_copy(hp[:, :].rearrange("p (q h) -> p h q", h=2), ps_i[:, 4, 0, :, :]).then_inc(s_idx, 1)
            dve.tensor_copy(hcol[:, :].rearrange("p (q h) -> p h q", h=2), ps_i[:, 4, 1, :, :]).then_inc(s_idx, 1)
            dve.wait_ge(s_idx, 2)

            def onehots(turn, slot, wait):
                t = 4 * turn + slot
                if wait:
                    dve.wait_ge(s_hist, t - 3)
                if slot % 2 == 0:
                    dve.tensor_scalar(ha[slot], iota_p[:, :], hp[:, bass.ds(t, 1)], None, ALU.is_equal)
                dve.tensor_scalar(hb[slot], iota_c, hcol[:, bass.ds(t, 1)], None, ALU.is_equal
                                  ).then_inc(s_onehot, 1)

            for slot in range(4):
                onehots(0, slot, False)
            with dve.Fori(1, EARLY) as turn:
                for slot in range(4):
                    onehots(turn, slot, True)

            dve.wait_ge(s_rows, 32)
            here, prev, nxt = rwin[:, 1:RE + 1], rwin[:, 0:RE], rwin[:, 2:RE + 2]
            dve.tensor_copy(rows[:, 0, :], rsorted)
            dve.tensor_scalar(rows[:, 1, :], here, float(N - 1), None, ALU.min)
            then(dve.tensor_tensor(rows[:, 4, :], here, prev, ALU.is_equal), s_ri, 1)
            then(dve.tensor_tensor(rows[:, 5, :], here, nxt, ALU.is_equal), s_ri, 2)
            dve.scalar_tensor_tensor(rows[:, 2, :], rows[:, 5, :], float(OFF), here, ALU.mult, ALU.add
                                     ).then_inc(s_ri, 1)
            dve.scalar_tensor_tensor(rows[:, 3, :], rows[:, 4, :], float(OFF), here, ALU.mult, ALU.add
                                     ).then_inc(s_ri, 1)
            then(dve.tensor_scalar(rtmp, here, float(N - 1), None, ALU.min), s_ri, 5)
            dve.tensor_scalar(rtm2, rtmp, J - 1, None, ALU.bitwise_and).then_inc(s_ri, 1)
            then(dve.tensor_scalar(rsrc, rtmp, 11, 4, ALU.arith_shift_right, ALU.logical_shift_left), s_ri, 7)
            dve.tensor_tensor(rows[:, 7, :], rsrc, rtm2, ALU.add).then_inc(s_ri, 1)
            then(dve.tensor_scalar(rtmp, rtmp, 4, P - 1, ALU.arith_shift_right, ALU.bitwise_and), s_ri, 9)
            dve.tensor_copy(rows[:, 6, :], rtmp).then_inc(s_ri, 1)
            dve.wait_ge(s_iT, 3)
            by_tile = lambda a: ps_i[:, a // 2, a % 2, :, :]
            qh = lambda a: a.rearrange("p (q h) -> p h q", h=2)
            dve.tensor_copy(qh(sq[:, 0, 0:TILES]), by_tile(3)).then_inc(s_idx, 1)
            four = idx[:, :, :].rearrange("p k (a i) -> p k a i", i=TPC)
            for a in range(3):
                for h in range(2):
                    dve.tensor_copy(
                        four[:, :, a, h::2],
                        ps_i[:, a // 2, a % 2, h, :].rearrange("p (k i) -> p k i", i=2)).then_inc(s_idx, 1)
            dve.tensor_copy(qh(same_prev[:, :]), by_tile(4)).then_inc(s_idx, 1)
            dve.tensor_copy(qh(same_next[:, :]), by_tile(5)).then_inc(s_idx, 1)
            dve.wait_ge(s_iT, 4)
            dve.tensor_copy(qh(lp[:, :]), by_tile(6)).then_inc(s_idx, 1)
            dve.tensor_copy(qh(lcol[:, :]), by_tile(7)).then_inc(s_idx, 1)
            dve.wait_ge(s_idx, 13)
            dve.tensor_scalar(is_last[:, :], same_next[:, :], -1.0, 1.0, ALU.mult, ALU.add).then_inc(s_idx, 1)
            dve.wait_ge(s_iT, 5)
            dve.tensor_copy(four[:, :, 3, :], ps_flip.rearrange("p (k i) -> p k i", i=TPC)).then_inc(s_idx, 1)

            with dve.Fori(EARLY, TILES // 4) as turn:
                for slot in range(4):
                    onehots(turn, slot, True)
            root = zT[:, 1, 0:CH * J]
            dve.wait_ge(s_hist, TILES)
            dve.tensor_scalar(deg[:, :].rearrange("p (a b) -> p a b", a=2), hist, 1.0, None, ALU.add).then_inc(s_deg, 1)
            dve.wait_ge(s_root, 1)
            then(dve.reciprocal(dinv[:, :], root), s_deg, 2)
            newton(dinv[:, :], deg[:, :], root, s_deg, 2)
            dve.sem_inc(s_dinv, 1)
            a1, r1 = zT[:, 0, 0:CH * J], zT[:, 1, 0:CH * J]
            then(dve.tensor_tensor(a1, dinv[:, :], dinv[:, :], ALU.mult), s_scale, 1)
            then(dve.tensor_scalar(a1, a1, 1.0, None, ALU.add), s_scale, 2)
            then(dve.tensor_tensor(a1, a1, a1, ALU.mult), s_scale, 3)
            then(dve.reciprocal(r1, a1), s_scale, 4)
            then(dve.tensor_scalar(eps_a[:, :], r1, EPS, None, ALU.mult), s_scale, 5)
            dve.wait_ge(s_consts, 4)
            dve.tensor_tensor(centre[:, :], centre[:, :], ident[:, :], ALU.add).then_inc(s_centre, 1)

            def dense(c):
                a, b, g, h = c.back(1), c.back(3), c.back(4), c.back(5)
                chain = a.real() or h.real()
                rstd = drstd[:, a.two, :]

                def root_step(k):
                    if chain:
                        rsqrt_step(k, rstd, dvar[:, :], dnw[:, :], d_pow, RS * a.n)

                if a.real():
                    dve.wait_ge(d_s1, a.n + 1)
                    dve.scalar_tensor_tensor(dvar[:, 0:J], dsum[:, 1, :], 1.0 / D, eps_a[:, bass.ds(a.n * J, J)],
                                             ALU.mult, ALU.add).then_inc(d_v1, 1)
                if h.real():
                    dve.wait_ge(d_s2, h.n + 1)
                    dve.tensor_scalar(dvar[:, J:2 * J], dsum[:, 2, :], 1.0 / D, EPS, ALU.mult, ALU.add
                                      ).then_inc(d_v2, 1)
                if c.real():
                    dve.wait_ge(d_x[c.slot], 16 * (c.turn + 1))
                    x3 = col3(x_in[:, c.slot, :])
                    dve.tensor_reduce(dsum[:, 0, :], x3, AX.X, ALU.add).then_inc(d_m, 1)
                if a.real():
                    dve.wait_ge(d_v1, a.n + 1)
                if h.real():
                    dve.wait_ge(d_v2, h.n + 1)
                root_step(1)
                root_step(2)
                if b.real():
                    s = b.two
                    dve.wait_ge(d_og, b.n + 1)
                    dve.scalar_tensor_tensor(zT[:, s, :], xT[:, s, :], 2.0, zT[:, s, :], ALU.mult, ALU.add
                                             ).then_inc(d_zT, 1)
                root_step(3)
                if c.real():
                    dve.wait_ge(d_m, c.n + 1)
                    dve.scalar_tensor_tensor(x3, wide(dsum[:, 0, :], J, D), -1.0 / D, x3, ALU.mult, ALU.add
                                             ).then_inc(d_xc, 1)
                root_step(4)
                if g.real():
                    dve.wait_ge(d_sq2, g.n + 1)
                    dve.tensor_reduce(dsum[:, 2, :], col3(sq[:, 1, :]), AX.X, ALU.add).then_inc(d_s2, 1)
                root_step(5)
                root_step(6)
                if c.real():
                    dve.wait_ge(d_sq1, c.n + 1)
                    dve.tensor_reduce(dsum[:, 1, :], col3(sq[:, 0, :]), AX.X, ALU.add).then_inc(d_s1, 1)
                for k in range(7, RS + 1):
                    root_step(k)
                if a.real():
                    dve.wait_ge(d_pow, RS * (a.n + 1))
                    xa = col3(x_in[:, a.slot, :])
                    dve.tensor_tensor(xa, xa, wide(rstd[:, 0:J], J, D), ALU.mult).then_inc(d_x1, 1)
                if h.real():
                    s = h.two
                    dve.wait_ge(d_pow, RS * (a.n + 1))
                    dve.wait_ge(d_sq2, h.n + 1)
                    if h.after(2):
                        dve.wait_ge(d_st[s], 16 * h.uses)
                    dve.tensor_tensor(col3(outb[:, s, :]), col3(ps_z[s]), wide(rstd[:, J:2 * J], J, D), ALU.mult
                                      ).then_inc(d_out, 1)

            run_chunks(dve, dense, 4, 8, 5)

            tile4 = lambda a: a.rearrange("p (t f) -> p t f", t=TPC)
            ew = TPC + LOOK
            evars = [sm[:, 16 + s * ew:16 + (s + 1) * ew] for s in range(2)]
            rstds = [sm[:, 28 + s * ew:28 + (s + 1) * ew] for s in range(2)]
            enw = sm[:, 40:40 + ew]
            dve.memset(sm[:, 16:16 + 2 * ew], 1.0).then_inc(q_part, 1)
            by_k = lambda a: a.rearrange("p (k b) -> p k b", b=P)
            dT = ps[0:KB, 0:2, :].rearrange("p a b -> p (a b)")[:, 0:NB * P]
            deg_i, deg_j = (zT[0:KB, i, 0:NB * P].bitcast(I32) for i in range(2))
            dve.wait_ge(q_dT, 1)
            dve.wait_ge(d_z, CH)
            then(dve.tensor_copy(deg_i, dT), q_part, 2)
            dve.tensor_scalar(deg_j, deg_i, 8, 8, ALU.arith_shift_right, ALU.logical_shift_left).then_inc(q_part, 1)
            then(dve.tensor_scalar(deg_i, deg_i, 255, None, ALU.bitwise_and), q_part, 4)
            dve.tensor_copy(parts[:, :, 0, :], by_k(deg_j)).then_inc(q_part, 1)
            dve.tensor_copy(parts[:, :, 1, :], by_k(deg_i)).then_inc(q_part, 1)

            def spread_factors(c, k, eye, same, reverse):
                for t in range(TPC):
                    u = TPC - 1 - t if reverse else t
                    ins = dve.tensor_scalar(mask_rhs[:, c.two, t, :], eye[:, :], same[:, bass.ds(k * TPC + u, 1)],
                                            None, ALU.mult)
                return ins

            def sums_pass(c):
                b, m, d, g, h = c.back(1), c.back(2), c.back(3), c.back(4), c.back(5)
                now, other = c.two, 1 - c.two
                q = 8 * g.n
                if g.real():
                    dcol = d_all[:, bass.ds(g.n * (2 * TPC), TPC)]
                    xd = tile4(x_all[:, bass.ds(g.n * (2 * EF) + EF, EF)])

                def root_step(k):
                    if h.real() or d.real():
                        rsqrt_step(k, rstds[now], evars[now], enw, q_pow, RS * d.n)

                if h.real():
                    dve.wait_ge(q_sq, h.n + 1)
                    dve.tensor_scalar(evars[now][:, 0:TPC], esum, 1.0 / D, EPS, ALU.mult, ALU.add).then_inc(q_var, 1)
                if g.real():
                    dve.wait_ge(q_pow, RS * d.n)
                    dve.wait_ge(g_dk[g.slot], 16 * (g.turn + 1))
                    dve.tensor_copy(dcol[:, 0:LOOK], rstds[other][:, TPC:ew]).then_inc(q_put, 1)
                if h.real():
                    dve.wait_ge(q_var, h.n + 1)
                if d.real():
                    dve.wait_ge(q_sel, LOOK * (d.n + 1))
                root_step(1)
                if c.real():
                    dve.wait_ge(g_xk[c.slot], 16 * (c.turn + 1))
                    dve.wait_ge(g_dk[c.slot], 16 * (c.turn + 1))
                    if c.after(2):
                        dve.wait_ge(q_wT, c.n - 1)
                    dve.tensor_tensor(w_x[:, c.slot, :, :], tile4(x_all[:, bass.ds(c.n * (2 * EF), EF)]),
                                      wide(d_all[:, bass.ds(c.n * (2 * TPC) + TPC, TPC)], TPC, D), ALU.mult).then_inc(q_w, 1)
                if g.real():
                    dve.wait_ge(q_put, g.n + 1)
                    dve.tensor_tensor(sm[:, 4:8], dcol, dcol, ALU.mult).then_inc(q_v, 1)
                root_step(2)
                if c.real():
                    if c.after(2):
                        dve.wait_ge(q_hT, c.n - 1)
                    settled(dve)
                    for i in range(LOOK):
                        ins = dve.tensor_scalar(l_hot[:, c.slot, i, :], iota_c, lcol[:, bass.ds(c.n * TPC + i, 1)],
                                                None, ALU.is_equal)
                    ins.then_inc(q_hot, 1)
                if g.real():
                    dve.wait_ge(q_v, q + 1)
                    dve.tensor_scalar(sm[:, 4:8], sm[:, 4:8], 1.0, None, ALU.add).then_inc(q_v, 1)
                root_step(3)
                if g.real():
                    dve.wait_ge(q_fT, g.n + 1)
                    dve.tensor_tensor(ag_e[:, :, :], tile4(ps_ag[g.slot]), wide(dcol, TPC, D), ALU.mult
                                      ).then_inc(q_v, 1)
                root_step(4)
                if b.real():
                    dve.wait_ge(q_wT, b.n + 1)
                    dve.wait_ge(q_mask, b.n + 1)
                    if b.after(2):
                        dve.wait_ge(q_fT, b.n - 1)
                    if b.after(1):
                        dve.wait_ge(q_f, b.n)
                        carry = fsum[:, 1 - b.slot, EC - 1:EC]
                    else:
                        carry = 0.0
                    dve.tensor_tensor_scan(fsum[:, b.slot, :], mask[0:D, :], ps_w[b.slot], carry, ALU.mult, ALU.add
                                           ).then_inc(q_f, 1)
                root_step(5)
                if g.real():
                    dve.wait_ge(q_v, q + 3)
                    for t in range(TPC):
                        ins = dve.scalar_tensor_tensor(v_e[:, t, :], xd[:, t, :], sm[:, 4 + t:5 + t], ag_e[:, t, :],
                                                       ALU.mult, ALU.add, accum_out=sm[:, 8 + t:9 + t])
                        ins.then_inc(q_v, 1)
                root_step(6)
                root_step(7)
                root_step(8)
                if g.real():
                    dve.wait_ge(q_v, q + 7)
                    if g.after(2):
                        dve.wait_ge(q_xd, g.n - 1)
                    dve.scalar_tensor_tensor(vc_e[:, g.slot, :, :], wide(sm[:, 8:12], TPC, D), -1.0 / D, v_e[:, :, :],
                                             ALU.mult, ALU.add).then_inc(q_v, 1)
                root_step(9)
                if m.real():
                    dve.wait_ge(q_look, m.n + 1)
                    settled(dve)
                    for i in range(LOOK):
                        dve.scalar_tensor_tensor(l_sel[:, i, :, :], iota_p[:, :].unsqueeze(1).to_broadcast([P, 2, P]),
                                                 lp[:, bass.ds(m.n * TPC + i, 1)],
                                                 ps_look[:, i, :].rearrange("p (a b) -> p a b", a=2),
                                                 ALU.is_equal, ALU.mult,
                                                 accum_out=evars[other][:, TPC + i:TPC + i + 1]).then_inc(q_sel, 1)
                if h.real():
                    dve.wait_ge(q_pow, RS * (d.n + 1))
                    dve.tensor_tensor(elast[:, h.slot, :], rstds[now][:, 0:TPC], is_last[:, bass.ds(h.n * TPC, TPC)],
                                      ALU.mult).then_inc(q_last, 1)

            run_chunks(dve, sums_pass, 2, 6, 5)
            dve.wait_ge(q_look, CH)
            dve.memset(cT[HC:HC + 1, 0:EC], 1.0).then_inc(s_biasrow, 1)
            dve.wait_ge(s_biasrow, 1)
            dve.sem_inc(r_start, 1)
            dve.wait_ge(r_start, 4)

            def messages(c):
                b, g, h, l = c.back(1), c.back(3), c.back(4), c.back(5)
                k = (CH - 1) - c.n
                rstd = rstds[l.two][:, 0:TPC]
                evar = evars[0][:, 0:TPC]
                q = 3 * h.n
                z = zc_e[h.two]

                def root_step(i):
                    if l.real():
                        rsqrt_step(i, rstd, evar, enw[:, 0:TPC], r_pow, RS * l.n)

                if g.real():
                    dve.wait_ge(r_mg, g.n + 1)
                    dve.wait_ge(r_xs, 3 * (g.n + 1))
                    dve.wait_ge(r_h, g.n + 1)
                    if g.after(1):
                        dve.wait_ge(r_box, g.n)
                        carry = xin[g.back(1).slot][0:D, EC - 1:EC]
                    else:
                        carry = 0.0
                    dve.tensor_tensor_scan(xin[g.slot][0:D, :], mask_m[g.slot][0:D, :], mT[g.two], carry,
                                           ALU.mult, ALU.add).then_inc(r_box, 1)
                if l.real():
                    dve.wait_ge(r_s, l.n + 1)
                    dve.tensor_scalar(evar, esum, 1.0 / D, EPS, ALU.mult, ALU.add).then_inc(r_var, 1)
                if h.real():
                    dve.wait_ge(r_og, h.n + 1)
                    if h.after(2):
                        dve.wait_ge(r_out, h.n - 1)
                    dve.scalar_tensor_tensor(z, tile4(ps[:, 6 + h.two, EF:2 * EF]), 2.0, comb_e[h.two],
                                             ALU.mult, ALU.add).then_inc(r_z, 1)
                if l.real():
                    dve.wait_ge(r_var, l.n + 1)
                root_step(1)
                if c.real():
                    if c.after(2):
                        dve.wait_ge(r_tm, c.n - 1)
                    settled(dve)
                    spread_factors(c, k, flip_b, same_next, True).then_inc(r_m, 1)
                root_step(2)
                if h.real():
                    dve.wait_ge(r_z, q + 1)
                    dve.tensor_reduce(sm[:, 8:12], z, AX.X, ALU.add).then_inc(r_z, 1)
                root_step(3)
                root_step(4)
                root_step(5)
                root_step(6)
                if h.real():
                    dve.wait_ge(r_z, q + 2)
                    dve.scalar_tensor_tensor(z, wide(sm[:, 8:12], TPC, D), -1.0 / D, z, ALU.mult, ALU.add).then_inc(r_z, 1)
                root_step(7)
                root_step(8)
                if b.real():
                    dve.wait_ge(r_tm, b.n + 1)
                    dve.wait_ge(r_xs, 3 * b.n + 2)
                    if b.after(4):
                        dve.wait_ge(r_o, b.n - 3)
                    if b.after(1):
                        dve.wait_ge(r_xd, b.n)
                        carry = xin[b.back(1).slot][D:P, EC - 1:EC]
                    else:
                        carry = 0.0
                    dve.tensor_tensor_scan(xin[b.slot][D:P, :], mask_m[b.slot][D:P, :], ps[D:P, 0, :], carry,
                                           ALU.mult, ALU.add).then_inc(r_xd, 1)
                root_step(9)
                if l.real():
                    dve.wait_ge(r_pow, RS * (l.n + 1))
                    if l.after(4):
                        dve.wait_ge(r_sc[l.slot], 64 * l.turn)
                    dve.tensor_tensor(tile4(out_e[l.slot]), zc_e[l.two], wide(rstd, TPC, D), ALU.mult
                                      ).then_inc(r_out, 1)
                if h.real():
                    dve.wait_ge(r_sq, h.n + 1)
                    dve.tensor_reduce(esum, sq_e, AX.X, ALU.add).then_inc(r_s, 1)

            run_chunks(dve, messages, 4, 8, 5)

        @block.gpsimd
        def _(pool):
            pool.memset(ident[:, :], 1.0).then_inc(s_stage, 1)
            pool.memset(flip[:, :], 1.0).then_inc(s_stage, 1)
            pool.memset(lower, 1.0).then_inc(s_stage, 1)
            pool.iota(iota_p[:, :], [[1, P]], base=0, channel_multiplier=0,
                      allow_small_or_imprecise_dtypes=True).then_inc(s_iota, 1)
            pool.iota(iota_c, [[1, CH * J]], base=0, channel_multiplier=0,
                      allow_small_or_imprecise_dtypes=True).then_inc(s_iota, 1)
            pool.wait_ge(s_stage, 3)
            pool.affine_select(ident[:, :], ident[:, :], [[-1, P]], ALU.is_equal, 0.0, base=0,
                               channel_multiplier=1).then_inc(s_consts, 1)
            pool.affine_select(flip[:, :], flip[:, :], [[1, P]], ALU.is_equal, 0.0, base=-(P - 1),
                               channel_multiplier=1).then_inc(s_consts, 1)
            pool.affine_select(lower, lower, [[-1, P]], ALU.is_gt, 0.0, base=0,
                               channel_multiplier=1).then_inc(s_lower, 1)
            pool.wait_ge(s_consts, 2)
            pool.tensor_copy(ident_b[:, :], ident[:, :]).then_inc(s_consts, 1)
            pool.tensor_copy(flip_b[:, :], flip[:, :]).then_inc(s_consts, 1)

            pool.wait_ge(s_flag, 1)
            unsorted = pool.value_load(flag[0:1, 0:1], min_val=0, max_val=1)
            with pool.If(unsorted == 1):
                pool.wait_ge(s_copy, 32)
                pool.wait_ge(s_attr, 32)
                key_row = dsts[GUARD, :].rearrange("n a -> (n a)")
                pool.dma_start(keys.bitcast(I32), key_row.partition_broadcast(P)).then_inc(s_perm, 16)
                for half in range(2):
                    t0 = half * ROWS
                    pool.dma_start(dst_e[:, t0:t0 + ROWS],
                                   dsts[1 + t0 * P:1 + (t0 + ROWS) * P, :].rearrange("(t p) a -> p (t a)", p=P),
                                   allow_slow_non_contiguous=True).then_inc(s_keys, 16)
                pool.wait_ge(s_perm, 16)
                pool.tensor_copy(keys, keys.bitcast(I32)).then_inc(s_keyf, 1)
                pool.wait_ge(s_ranked, 2)
                with pool.Fori(0, TILES) as t:
                    pool.dma_start(sort_s, srcs[bass.ds(t * P, P), :]).then_inc(s_tile, 16)
                    pool.dma_start(sort_e, attrs[bass.ds(t * P, P), :]).then_inc(s_tile, 16)
                    pool.tensor_copy(sort_i[:, 0:1], pos_i[:, bass.ds(t, 1)]).then_inc(s_stage, 1)
                    pool.tensor_copy(sort_i[:, 1:2], dst_e[:, bass.ds(t, 1)]).then_inc(s_stage, 1)
                    pool.wait_ge(s_tile, 32 * (t + 1))
                    pool.wait_ge(s_stage, 3 + 2 * (t + 1))
                    at = bass.IndirectOffsetOnAxis(ap=sort_i[:, 0:1], axis=0)
                    settled(pool)
                    pool.indirect_dma_start(src_perm, at, sort_s, None).then_inc(s_perm, 16)
                    pool.indirect_dma_start(dst_perm, at, sort_i[:, 1:2], None).then_inc(s_perm, 16)
                    pool.indirect_dma_start(attr_perm, at, sort_e, None).then_inc(s_perm, 16)
                    pool.wait_ge(s_perm, 16 + 48 * (t + 1))
                pool.dma_start(srcs, src_perm).then_inc(s_back, 16)
                pool.dma_start(dsts[GUARD, :], dst_perm).then_inc(s_back, 16)
                pool.dma_start(attrs, attr_perm).then_inc(s_back, 16)
                pool.wait_ge(s_back, 48)
            pool.sem_inc(s_sorted, 1)

            pool.wait_ge(s_idx, 9)

            def stage(use, c, first, width, staged):
                n = 1 if isinstance(c.n, int) and c.n == CH - 1 else 2
                settled(pool)
                pool.tensor_copy(istage[:, use, c.slot // 2, 0:n, 0:width], idx[:, bass.ds(c.n, n), first:first + width]
                                 ).then_inc(staged, 1)

            def gather_both(use, c, staged, landed, kept, source, columns, place):
                nxt, old = c.back(-1), c.back(2)
                pool.wait_ge(staged, c.uses + 1)
                if c.after(2):
                    pool.wait_ge(kept[c.two], 16 * c.uses)
                settled(pool)
                for i, column in enumerate(columns):
                    if i == TPC and c.two == 1 and nxt.real():
                        if c.after(3):
                            pool.wait_ge(landed[old.two], 16 * len(columns) * (old.uses + 1))
                        stage(use, nxt, 0, 2 * TPC, staged)
                    at = bass.IndirectOffsetOnAxis(ap=istage[:, use, c.slot // 2, c.two, column:column + 1], axis=0)
                    pool.indirect_dma_start(place(i), None, source, at).then_inc(landed[c.two], 16)

            D_COLUMNS = list(range(TPC + LOOK, 2 * TPC)) + list(range(TPC))

            def gather_x(c):
                gather_both(0, c, g_ia, g_x, g_xk, x, list(range(2 * TPC)), lambda i: gx[:, c.two, i * D:(i + 1) * D])

            def gather_d(c):
                gather_both(1, c, g_ib, g_d, g_dk, dinv_t, D_COLUMNS, lambda i: gdv[:, c.two, i:i + 1])

            zero = Chunk(4, 0, 0)
            stage(0, zero, 0, 2 * TPC, g_ia)
            stage(1, zero, 0, 2 * TPC, g_ib)
            stage(2, zero, 2 * TPC, TPC, q_ic)
            run_chunks(pool, gather_x, 4, 4, 0, ahead=2)
            pool.wait_ge(s_dt, 16)
            run_chunks(pool, gather_d, 4, 4, 0, ahead=2)

            for i in range(4):
                pool.wait_ge(d_st1[i], 16 * ((CH - 1 - i) // 4 + 1))

            def scatter_x1(c):
                nxt, old = c.back(-1), c.back(2)
                pool.wait_ge(q_ic, c.uses + 1)
                pool.wait_ge(q_ks[c.two], 16 * (c.uses + 1))
                settled(pool)
                for t in range(TPC):
                    if t == TPC - 1 and c.two == 1 and nxt.real():
                        if c.after(3):
                            pool.wait_ge(q_sc[old.two], 64 * (old.uses + 1))
                        stage(2, nxt, 2 * TPC, TPC, q_ic)
                    pool.indirect_dma_start(
                        x1t, bass.IndirectOffsetOnAxis(ap=istage[:, 2, c.slot // 2, c.two, t:t + 1], axis=0),
                        gx[:, c.two, t * D:(t + 1) * D], None, bounds_check=N - 1, oob_is_err=False
                    ).then_inc(q_sc[c.two], 16)

            run_chunks(pool, scatter_x1, 4, 4, 0, ahead=2)
            for i in range(2):
                pool.wait_ge(d_st[i], 16 * ((CH - 1 - i) // 2 + 1))
            pool.sem_inc(r_start, 1)
            pool.wait_ge(r_start, 4)
            pool.wait_ge(q_sc[0], 64 * (CH // 2 + 1))
            pool.wait_ge(q_sc[1], 64 * (CH // 2))

            def stage_back(use, c, first, staged):
                n = 1 if isinstance(c.n, int) and c.n == CH - 1 else 2
                settled(pool)
                k = (CH - n) - c.n
                pool.tensor_copy(istage[:, use, c.slot // 2, 2 - n:2, 0:TPC], idx[:, bass.ds(k, n), first:first + TPC]
                                 ).then_inc(staged, 1)

            def messages(c):
                l = c.back(7)
                if c.real():
                    nxt, old = c.back(-1), c.back(2)
                    pool.wait_ge(r_is, c.uses + 1)
                    if c.after(4):
                        pool.wait_ge(r_tm, c.n - 3)
                    settled(pool)
                    for t in range(TPC):
                        if t == TPC - 1 and c.two == 1 and nxt.real():
                            if c.after(3):
                                pool.wait_ge(r_ga[old.slot], 64 * (old.turn + 1))
                            stage_back(3, nxt, 0, r_is)
                        at = bass.IndirectOffsetOnAxis(ap=istage[:, 3, c.slot // 2, 1 - c.two, t:t + 1], axis=0)
                        pool.indirect_dma_start(m_in[c.slot][:, t, 0:D], None, x1t, at).then_inc(r_ga[c.slot], 16)
                if l.real():
                    nxt, old = l.back(-1), l.back(2)
                    pool.wait_ge(r_io, l.uses + 1)
                    pool.wait_ge(r_out, l.n + 1)
                    settled(pool)
                    for t in range(TPC):
                        if t == TPC - 1 and l.two == 1 and nxt.real():
                            if l.after(3):
                                pool.wait_ge(r_sc[old.slot], 64 * (old.turn + 1))
                            stage_back(4, nxt, 3 * TPC, r_io)
                        u = TPC - 1 - t
                        at = bass.IndirectOffsetOnAxis(ap=istage[:, 4, l.slot // 2, 1 - l.two, u:u + 1], axis=0)
                        pool.indirect_dma_start(out, at, out_e[l.slot][:, t * D:(t + 1) * D], None,
                                                bounds_check=N - 1, oob_is_err=False).then_inc(r_sc[l.slot], 16)

            pool.wait_ge(s_idx, 15)
            stage_back(3, zero, 0, r_is)
            stage_back(4, zero, 3 * TPC, r_io)
            run_chunks(pool, messages, 4, 8, 7, ahead=2)
            for i in range(4):
                pool.wait_ge(r_sc[i], 64 * ((CH - 1 - i) // 4 + 1))


_INS = ['x', 'src', 'dst', 'edge_attr_32', 'L1_gnn_W_m1', 'L1_gnn_b_m1', 'L1_gnn_W_m2', 'L1_gnn_b_m2',
        'L1_gnn_W_c1', 'L1_gnn_b_c1', 'L1_gnn_W_c2', 'L1_gnn_b_c2']


def kernel(**inputs):
    import numpy as _np
    import concourse.bacc as _bacc
    from concourse import mybir as _mybir
    from concourse.bass_utils import run_bass_kernel_spmd as _run

    nc = _bacc.Bacc("TRN2", target_bir_lowering=False, num_devices=1)
    arrays, args = {}, []
    for name in _INS:
        a = _np.ascontiguousarray(inputs[name])
        arrays[f"in_{name}_dram"] = a
        args.append(nc.dram_tensor(f"in_{name}_dram", a.shape, _mybir.dt.from_np(a.dtype), kind="ExternalInput").ap())
    result = nc.dram_tensor("out_0_dram", (N, D), F32, kind="ExternalOutput").ap()
    build(nc, *args, result)
    r = _run(nc, [arrays], core_ids=[0])
    return r.results[0]["out_0_dram"]
```
